# Optimizing a Trainium2 kernel written in Bass

```python
import numpy as np
import jax
import jax.numpy as jnp

def _softmax(x, axis=-1):
    return jax.nn.softmax(x, axis=axis)

def _gelu(x):
    return jax.nn.gelu(x, approximate=True)

def _silu(x):
    return jax.nn.silu(x)

def _sigmoid(x):
    return jax.nn.sigmoid(x)

def _layernorm(x, axis=-1, eps=1e-05):
    m = jnp.mean(x, axis=axis, keepdims=True)
    v = jnp.var(x, axis=axis, keepdims=True)
    return (x - m) / jnp.sqrt(v + eps)

def _scatter_add(tgt, idx, src, axis=0):
    return tgt.at[idx].add(src)

def _segment_sum(src, seg, n):
    return jax.ops.segment_sum(src, seg, n)
kernel_name = 'mk_gnn_preln_d1_gnn_r64_4a9130'

def setup_inputs(seed: int=0):
    np.random.seed(seed)
    _w = jnp.asarray

    def _rec_inputs():
        import jax
        import jax.numpy as jnp
        _gk = jax.random.key(seed)
        x = -0.0003713 + 1 * jax.random.normal(jax.random.fold_in(_gk, 1), (50000, 256), jnp.float32)
        src = jax.random.randint(jax.random.fold_in(_gk, 2), (12500,), 0, 50000, jnp.int32)
        dst = jnp.minimum((50000 * jax.random.uniform(jax.random.fold_in(_gk, 3), (12500,)) ** 2.0).astype(jnp.int32), 49999)
        _o = jnp.argsort(dst, stable=True)
        src = src[_o]
        dst = dst[_o]
        edge_type_2 = jax.random.randint(jax.random.fold_in(_gk, 12), (12500,), 0, 2, jnp.int32)
        edge_weight = jax.random.uniform(jax.random.fold_in(_gk, 13), (12500,), jnp.float32, 0.0, 0.999999)
        return (x, src, dst, edge_type_2, edge_weight)
    x, src, dst, edge_type_2, edge_weight = _rec_inputs()

    def _L0_gnn_setup():
        import jax, jax.numpy as jnp
        import numpy as np
        N, E = (50000, 12500)
        IN_CH, H, C = (256, 8, 32)
        HID = H * C
        T = 2
        FFN = 4 * HID
        EPS = 1e-05

        def _layernorm(h, g, b):
            mu = jnp.mean(h, axis=-1, keepdims=True)
            var = jnp.mean(jnp.square(h - mu), axis=-1, keepdims=True)
            return (h - mu) * jax.lax.rsqrt(var + EPS) * g + b

        def _gat_forward(x, edge_index, edge_type, edge_weight, W_src, W_dst, att_src, att_dst, bias, ln1_g, ln1_b, ln2_g, ln2_b, ffn_W1, ffn_b1, ffn_W2, ffn_b2):
            n = x.shape[0]
            loop = jnp.arange(n, dtype=edge_index.dtype)
            src = jnp.concatenate([edge_index[0], loop])
            dst = jnp.concatenate([edge_index[1], loop])
            etype = jnp.concatenate([edge_type, jnp.zeros((n,), edge_type.dtype)])
            ew = jnp.concatenate([edge_weight, jnp.ones((n,), edge_weight.dtype)])
            x_src = (x @ W_src.T).reshape(n, H, C)
            x_dst = (x @ W_dst.T).reshape(n, H, C)
            xs_j = x_src[src]
            xd_i = x_dst[dst]
            a_s = att_src[etype]
            a_d = att_dst[etype]
            alpha = jnp.sum(xs_j * a_s, axis=-1) + jnp.sum(xd_i * a_d, axis=-1)
            alpha = jnp.where(alpha >= 0, alpha, 0.2 * alpha)
            m = jax.lax.stop_gradient(jax.ops.segment_max(alpha, dst, num_segments=n))
            a = jnp.exp(alpha - m[dst])
            denom = jax.ops.segment_sum(a, dst, num_segments=n)
            a = a / denom[dst]
            a = a * ew[:, None]
            msg = xs_j * a[:, :, None]
            out = jax.ops.segment_sum(msg, dst, num_segments=n)
            out = out.reshape(n, H * C) + bias
            h = _layernorm(out + x, ln1_g, ln1_b)
            ff = jax.nn.gelu(h @ ffn_W1.T + ffn_b1, approximate=False) @ ffn_W2.T + ffn_b2
            return _layernorm(h + ff, ln2_g, ln2_b)
        key = jax.random.key(seed)
        ks = jax.random.split(key, 16)
        s_in = 1.0 / np.sqrt(IN_CH)
        s_h = 1.0 / np.sqrt(HID)
        return {'x': jax.random.normal(ks[0], (N, IN_CH), jnp.float32), 'edge_index': jax.random.randint(ks[1], (2, E), 0, N, jnp.int32), 'edge_type': jax.random.randint(ks[2], (E,), 0, T, jnp.int32), 'edge_weight': jax.random.uniform(ks[3], (E,), jnp.float32), 'W_src': jax.random.normal(ks[4], (H * C, IN_CH), jnp.float32) * s_in, 'W_dst': jax.random.normal(ks[5], (H * C, IN_CH), jnp.float32) * s_in, 'att_src': jax.random.normal(ks[6], (T, H, C), jnp.float32) * (1.0 / np.sqrt(C)), 'att_dst': jax.random.normal(ks[7], (T, H, C), jnp.float32) * (1.0 / np.sqrt(C)), 'bias': jnp.zeros((HID,), jnp.float32), 'ln1_g': jnp.ones((HID,), jnp.float32), 'ln1_b': jnp.zeros((HID,), jnp.float32), 'ln2_g': jnp.ones((HID,), jnp.float32), 'ln2_b': jnp.zeros((HID,), jnp.float32), 'ffn_W1': jax.random.normal(ks[8], (FFN, HID), jnp.float32) * s_h, 'ffn_b1': jnp.zeros((FFN,), jnp.float32), 'ffn_W2': jax.random.normal(ks[9], (HID, FFN), jnp.float32) * (1.0 / np.sqrt(FFN)), 'ffn_b2': jnp.zeros((HID,), jnp.float32)}
    _L0_gnn_all = _L0_gnn_setup()
    _L0_gnn_in = {k: v for k, v in _L0_gnn_all.items() if k in ('W_src', 'W_dst', 'att_src', 'att_dst', 'bias', 'ln1_g', 'ln1_b', 'ln2_g', 'ln2_b', 'ffn_W1', 'ffn_b1', 'ffn_W2', 'ffn_b2')}
    del _L0_gnn_all
    return {'x': x, 'src': src, 'dst': dst, 'edge_type_2': edge_type_2, 'edge_weight': edge_weight, 'L0_gnn_W_src': _L0_gnn_in['W_src'], 'L0_gnn_W_dst': _L0_gnn_in['W_dst'], 'L0_gnn_att_src': _L0_gnn_in['att_src'], 'L0_gnn_att_dst': _L0_gnn_in['att_dst'], 'L0_gnn_bias': _L0_gnn_in['bias'], 'L0_gnn_ln1_g': _L0_gnn_in['ln1_g'], 'L0_gnn_ln1_b': _L0_gnn_in['ln1_b'], 'L0_gnn_ln2_g': _L0_gnn_in['ln2_g'], 'L0_gnn_ln2_b': _L0_gnn_in['ln2_b'], 'L0_gnn_ffn_W1': _L0_gnn_in['ffn_W1'], 'L0_gnn_ffn_b1': _L0_gnn_in['ffn_b1'], 'L0_gnn_ffn_W2': _L0_gnn_in['ffn_W2'], 'L0_gnn_ffn_b2': _L0_gnn_in['ffn_b2']}

def reference(x, src, dst, edge_type_2, edge_weight, L0_gnn_W_src, L0_gnn_W_dst, L0_gnn_att_src, L0_gnn_att_dst, L0_gnn_bias, L0_gnn_ln1_g, L0_gnn_ln1_b, L0_gnn_ln2_g, L0_gnn_ln2_b, L0_gnn_ffn_W1, L0_gnn_ffn_b1, L0_gnn_ffn_W2, L0_gnn_ffn_b2):
    import jax
    import jax.numpy as jnp

    def _L0_gnn_ref(x, edge_index, edge_type, edge_weight, W_src, W_dst, att_src, att_dst, bias, ln1_g, ln1_b, ln2_g, ln2_b, ffn_W1, ffn_b1, ffn_W2, ffn_b2):
        import jax, jax.numpy as jnp
        import numpy as np
        N, E = (50000, 12500)
        IN_CH, H, C = (256, 8, 32)
        HID = H * C
        T = 2
        FFN = 4 * HID
        EPS = 1e-05

        def _layernorm(h, g, b):
            mu = jnp.mean(h, axis=-1, keepdims=True)
            var = jnp.mean(jnp.square(h - mu), axis=-1, keepdims=True)
            return (h - mu) * jax.lax.rsqrt(var + EPS) * g + b

        def _gat_forward(x, edge_index, edge_type, edge_weight, W_src, W_dst, att_src, att_dst, bias, ln1_g, ln1_b, ln2_g, ln2_b, ffn_W1, ffn_b1, ffn_W2, ffn_b2):
            n = x.shape[0]
            loop = jnp.arange(n, dtype=edge_index.dtype)
            src = jnp.concatenate([edge_index[0], loop])
            dst = jnp.concatenate([edge_index[1], loop])
            etype = jnp.concatenate([edge_type, jnp.zeros((n,), edge_type.dtype)])
            ew = jnp.concatenate([edge_weight, jnp.ones((n,), edge_weight.dtype)])
            x_src = (x @ W_src.T).reshape(n, H, C)
            x_dst = (x @ W_dst.T).reshape(n, H, C)
            xs_j = x_src[src]
            xd_i = x_dst[dst]
            a_s = att_src[etype]
            a_d = att_dst[etype]
            alpha = jnp.sum(xs_j * a_s, axis=-1) + jnp.sum(xd_i * a_d, axis=-1)
            alpha = jnp.where(alpha >= 0, alpha, 0.2 * alpha)
            m = jax.lax.stop_gradient(jax.ops.segment_max(alpha, dst, num_segments=n))
            a = jnp.exp(alpha - m[dst])
            denom = jax.ops.segment_sum(a, dst, num_segments=n)
            a = a / denom[dst]
            a = a * ew[:, None]
            msg = xs_j * a[:, :, None]
            out = jax.ops.segment_sum(msg, dst, num_segments=n)
            out = out.reshape(n, H * C) + bias
            h = _layernorm(out + x, ln1_g, ln1_b)
            ff = jax.nn.gelu(h @ ffn_W1.T + ffn_b1, approximate=False) @ ffn_W2.T + ffn_b2
            return _layernorm(h + ff, ln2_g, ln2_b)
        return _gat_forward(x, edge_index, edge_type, edge_weight, W_src, W_dst, att_src, att_dst, bias, ln1_g, ln1_b, ln2_g, ln2_b, ffn_W1, ffn_b1, ffn_W2, ffn_b2)
    edge_index = jnp.stack([src, dst])
    h = jnp.maximum(_layernorm(x, axis=-1), 0.0)
    x = x + _L0_gnn_ref(h, edge_index, edge_type_2, edge_weight, L0_gnn_W_src, L0_gnn_W_dst, L0_gnn_att_src, L0_gnn_att_dst, L0_gnn_bias, L0_gnn_ln1_g, L0_gnn_ln1_b, L0_gnn_ln2_g, L0_gnn_ln2_b, L0_gnn_ffn_W1, L0_gnn_ffn_b1, L0_gnn_ffn_W2, L0_gnn_ffn_b2)
    return x

_drawn_inputs = setup_inputs


def setup_inputs(seed=0):
    import zlib

    import numpy as np

    out = dict(_drawn_inputs(seed))
    spreads = {'L0_gnn_bias': (0.0, 0.1),
     'L0_gnn_ln1_g': (1.0, 0.2),
     'L0_gnn_ln1_b': (0.0, 0.1),
     'L0_gnn_ln2_g': (1.0, 0.2),
     'L0_gnn_ln2_b': (0.0, 0.1),
     'L0_gnn_ffn_b1': (0.0, 0.1),
     'L0_gnn_ffn_b2': (0.0, 0.1)}
    factors = {}
    for name, (base, spread) in spreads.items():
        noise = np.random.default_rng([zlib.crc32(name.encode()), seed]).standard_normal(out[name].shape)
        drawn = base * np.exp(spread * noise) if base else spread * noise
        out[name] = jnp.asarray(drawn.astype(out[name].dtype))
    for name, factor in factors.items():
        out[name] = (out[name] * factor).astype(out[name].dtype)
    return out
```

```python
from contextlib import ExitStack

import numpy as np

import concourse.bass as bass
from concourse import mybir

F32 = mybir.dt.float32
F32R = mybir.dt.float32r
I32 = mybir.dt.int32
ALU = mybir.AluOpType
ACT = mybir.ActivationFunctionType
AX = mybir.AxisListType.X

P = 128
TG = 4
GR = TG * P
HEADS = 8
BLOCKS = P // HEADS
EPS = 1e-5
BIG = 1e30


class Step:

    def __init__(self, k, off):
        self.k, self.off = k, off

    def __add__(self, d):
        return Step(self.k, self.off + d)

    def __sub__(self, d):
        return Step(self.k, self.off - d)

    @property
    def n(self):
        return 2 * self.k + self.off

    @property
    def half(self):
        return self.k + self.off // 2

    @property
    def par(self):
        return self.off % 2

    def exists(self, count):
        return not isinstance(self.n, int) or 0 <= self.n < count


def wait_count(eng, sem, count):
    if not (isinstance(count, int) and count <= 0):
        eng.wait_ge(sem, count)


SPLITS = 7
SCORE_STEPS = 16
SCAN_STEPS = 19
AL_STEPS = 8


def steps(eng, body, first, last, lo, hi):
    for s in range(first, lo):
        body(Step(0, s))
    if hi > lo:
        with eng.Fori(lo // 2, hi // 2) as k:
            body(Step(k, 0))
            body(Step(k, 1))
    for s in range(max(lo, hi), last):
        body(Step(0, s))


def build(nc, x, src_cols, dst_cols, next_cols, type_cols, weight_cols, dst_line, w_src_t, w_dst_t,
          att_src, att_dst, bias, g1, b1, g2, b2, g1_cols, b1_cols, w1_t, ffn_b1_cols, w2_t, ffn_b2, out):
    NROWS, D = x.shape
    NT = NROWS // P
    NG = NT // TG
    NCH = src_cols.shape[1]
    EP = NCH * P
    BW = EP // BLOCKS
    NPAIR = NCH // 2
    C = D // HEADS
    KC = D // P
    F = w1_t.shape[1]
    MF = F // P
    SC = 2 * HEADS
    WV = D + 2 * SC
    REC = D + 2 * HEADS
    SUM = D + HEADS
    EMPTY = EP
    assert D == KC * P and NT % TG == 0 and NCH % 2 == 0 and NCH <= P and EP % BLOCKS == 0

    sums = nc.dram_tensor("sums", (EP + P, REC), F32, kind="Internal").ap()
    row_of = nc.dram_tensor("row_of", (NROWS + P, 1), I32, kind="Internal").ap()
    msgs = nc.dram_tensor("msgs", (EP, D), F32, kind="Internal").ap()
    cand_line = nc.dram_tensor("cand_line", (HEADS * EP,), F32, kind="Internal").ap()
    max_line = nc.dram_tensor("max_line", (HEADS * EP,), F32, kind="Internal").ap()
    line = nc.dram_tensor("line", (EP + 2, 1), I32, kind="Internal").ap()
    s_src = nc.dram_tensor("s_src", (EP, 1), I32, kind="Internal").ap()
    s_type = nc.dram_tensor("s_type", (EP, 1), I32, kind="Internal").ap()
    s_weight = nc.dram_tensor("s_weight", (EP, 1), I32, kind="Internal").ap()

    x_tiles = x.rearrange("(p t) d -> p t d", p=P)
    out_tiles = out.rearrange("(p t) d -> p t d", p=P)
    line_row = line.rearrange("e o -> o e")

    with ExitStack() as ctx:
        def sb(name, shape, dt=F32):
            return ctx.enter_context(nc.sbuf_tensor(name, shape, dt))

        def sem(name):
            return ctx.enter_context(nc.semaphore(name))

        proj = [sb(f"proj_{n}", [P, KC, WV], F32R) for n in ("hi", "lo")]
        ffn1 = [sb(f"ffn1_{n}", [P, KC, F], F32R) for n in ("hi", "lo")]
        ffn2 = [sb(f"ffn2_{n}", [P, MF, D], F32R) for n in ("hi", "lo")]
        ident = sb("ident", [P, P])
        ones = sb("ones", [P, 1])
        rows = sb("rows", [P, 6, D])
        hidden_bias = sb("hidden_bias", [P, MF])
        minus_half = sb("minus_half", [P, TG])
        node_rows = sb("node_rows", [P, NT], I32)
        idx = sb("idx", [P, 2, TG], I32)
        slot = sb("slot", [P, 2, 2], I32)
        xt = [sb(f"xt_{n}", [P, KC, GR], F32R) for n in ("hi", "lo")]
        zt = [sb(f"zt_{n}", [P, 2, KC, GR], F32R) for n in ("hi", "lo")]
        act_hi = sb("act_hi", [P, 2, GR], F32R)
        act_lo = sb("act_lo", [P, 2, GR], F32R)
        xb = sb("xb", [P, 2, TG, D])
        h = sb("h", [P, 2, TG, D])
        stat = sb("stat", [P, TG, 6])
        mv = sb("mv", [P, 2, TG, 2])
        vareps = sb("vareps", [P, 2, TG])
        minus_mean = sb("minus_mean", [P, 2, TG])
        rstd = sb("rstd", [P, 2, TG])
        shift = sb("shift", [P, 2, TG])

        ARENA = max(17500, 2 * EP + 13 * NCH + 3 * P + 3 * REC + 64)
        arena = sb("arena", [P, ARENA])
        used = [0]

        def part(dims, dt=None):
            n = int(np.prod(dims))
            a = arena[:, used[0]:used[0] + n]
            used[0] += n
            assert used[0] <= ARENA
            if dt is not None:
                a = a.bitcast(dt)
            if len(dims) == 2:
                a = a.rearrange("p (a b) -> p a b", a=dims[0])
            if len(dims) == 3:
                a = a.rearrange("p (a b c) -> p a b c", a=dims[0], b=dims[1])
            return a

        src_i, dst_i, next_i, type_i = (part([NCH], I32) for _ in range(4))
        ew, type_1, type_0, last = (part([NCH]) for _ in range(4))
        dst_f = part([NCH + 1])
        target_f = part([NCH])
        target_i, place_i = part([NCH], I32), part([NCH], I32)
        trash, on_last, carry, flag_f = part([1]), part([1]), part([1]), part([1])
        flag_i = part([1], I32)
        ends = part([2])
        ends_row = part([3, P])
        agg = part([2, REC])
        empty = part([REC])
        edges_end = used[0]
        src_sc, dst_sc = part([NCH, SC]), part([NCH, 2 * SC])
        alpha, prob, soft = (part([NCH, HEADS]) for _ in range(3))
        cand, tops = part([HEADS, NCH]), part([HEADS, NCH])
        turn = part([HEADS, P])
        scan = part([2, BW])
        resets = part([BW + 1])
        line_b = part([BW + 2], I32)
        line_c = part([2, P], I32)
        eq, eq_carry = part([2, P]), part([2, P])
        msg_out = part([2, 2, D])
        msg_in = part([4, D])
        used[0] = edges_end
        w_src, w_dst = part([KC, D]), part([KC, D])
        att = part([4, D])
        att_prod = part([D])
        w1, w2 = part([KC, F]), part([MF, D])
        g1_col, b1_col = part([KC]), part([KC])
        proj_f = part([KC, 2 * SC])
        used[0] = edges_end
        all_dst, all_num = part([EP], I32), part([EP], I32)
        cmp_a = xb[:, 0, :, :].rearrange("p t d -> p (t d)")[:, 0:BW]
        cmp_b = xb[:, 1, :, :].rearrange("p t d -> p (t d)")[:, 0:BW]
        counts = h[:, 0, 0, 0:2 * BLOCKS]
        number_f = h[:, 0, 1, 0:NCH]
        rank_f = h[:, 0, 2, 0:NCH]
        rank_i = h[:, 0, 3, 0:NCH].bitcast(I32)
        rank1_i = h[:, 1, 3, 0:NCH].bitcast(I32)
        moved = h[:, 1, 2, 0:6].bitcast(I32)
        used[0] = 0
        xs = part([TG, WV])
        rec = part([2, TG * REC]).rearrange("p b (t d) -> p b t d", t=TG)
        x_res = part([2, TG, D])
        y, hb, z = part([TG, D]), part([TG, D]), part([TG, D])
        res = part([2, TG, D])
        u = part([TG, D])
        ob = part([2, TG, D])
        act_f = part([2, GR])
        y_stat, y_mv = part([TG, 6]), part([TG, 2])
        y_var, y_mm, y_rstd, y_shift = (part([TG]) for _ in range(4))
        u_stat, u_mv = part([TG, 6]), part([TG, 2])
        u_var, u_rstd = part([TG]), part([TG])
        al, top, den = (part([TG, HEADS]) for _ in range(3))
        expo, coef = part([TG, 2 * HEADS]), part([TG, 2 * HEADS])

        def pb(name):
            return ctx.enter_context(nc.psum_tensor(name, [P, 2, 512], F32))
        ps_t, ps_x, ps_f, ps_a = pb("ps_t"), pb("ps_x"), pb("ps_f"), pb("ps_a")

        (weights_in, rows_in, cols_in, consts, setup_step, hidden_pe, proj_hi_ready, weights_split, line_in,
         flag_sum, flag_pe, flag_done, all_in, num_ready, rank_step, ranked, moved_copied, sorted_out, sorted_in, in_order,
         cols_ready, rows_cleared, empty_set, empty_stored, idx_copied, stat_step, x_stats, x_prepared, x_pow, x_scaled,
         h_ready, xt_turned, xt_hi, xt_lo, xs_done, xs_out, alpha_step, cand_ready, cand_turned, cand_copied,
         cand_out, scan_in, scan_step, scan_pe, max_out, max_in, max_turned, diff_ready, exp_ready,
         soft_ready, vals_ready, eq_ready, agg_done, agg_out, agg_max, target_ready, target_step, rows_stored,
         slot_ready, sp_gate, pool_gate, act_gate, dve_gate, node_rows_in, al_step, exps_in, exps_out, coef_ready, hb_made, hb_ready,
         y_scaled_part, y_mul, y_ready, y_stats, y_prepared, y_pow, y_scaled, z_ready, zt_turned, zt_hi, zt_lo,
         x_res_ready, res_part, res_ready, f_done, act_hi_ready, act_f_ready, act_lo_ready, act_used,
         u_ready, u_stats, u_prepared, u_scaled, out_step, out_ready) = (sem(n) for n in """
         weights_in rows_in cols_in consts setup_step hidden_pe proj_hi_ready weights_split line_in
         flag_sum flag_pe flag_done all_in num_ready rank_step ranked moved_copied sorted_out sorted_in in_order
         cols_ready rows_cleared empty_set empty_stored idx_copied stat_step x_stats x_prepared x_pow x_scaled
         h_ready xt_turned xt_hi xt_lo xs_done xs_out alpha_step cand_ready cand_turned cand_copied
         cand_out scan_in scan_step scan_pe max_out max_in max_turned diff_ready exp_ready
         soft_ready vals_ready eq_ready agg_done agg_out agg_max target_ready target_step rows_stored
         slot_ready sp_gate pool_gate act_gate dve_gate node_rows_in al_step exps_in exps_out coef_ready hb_made hb_ready
         y_scaled_part y_mul y_ready y_stats y_prepared y_pow y_scaled z_ready zt_turned zt_hi zt_lo
         x_res_ready res_part res_ready f_done act_hi_ready act_f_ready act_lo_ready act_used
         u_ready u_stats u_prepared u_scaled out_step out_ready""".split())

        def sem_pair(name):
            return [sem(f"{name}_{i}") for i in range(2)]
        gathered, msg_stored, msg_loaded, line_c_in, agg_stored, x_in, rec_in, stored = (
            sem_pair(n) for n in ("gathered", "msg_stored", "msg_loaded", "line_c_in", "agg_stored",
                                  "x_in", "rec_in", "stored"))

        def wide(a, dims):
            return a.to_broadcast(dims)

        def edges_done(eng):
            for i in range(2):
                eng.wait_ge(agg_stored[i], 16 * NPAIR)
            eng.wait_ge(rows_stored, 16 * NCH)

        def front_stats(eng, f):
            wait_count(eng, x_scaled, f.n - 1)
            for t in range(TG):
                eng.bn_stats(stat[:, t, :], xb[:, f.par, t, :]).then_inc(stat_step, 1)
            eng.wait_ge(stat_step, TG * f.n + TG)
            eng.sem_inc(dve_gate, 1)
            for t in range(TG):
                eng.bn_aggr(mv[:, f.par, t, :], stat[:, t, :]).then_inc(x_stats, 1)
            eng.wait_ge(x_stats, TG * f.n + TG)
            eng.tensor_scalar(vareps[:, f.par, :], mv[:, f.par, :, 1], EPS, None, ALU.add).then_inc(x_prepared, 1)
            eng.tensor_scalar(minus_mean[:, f.par, :], mv[:, f.par, :, 0], -1.0, None,
                              ALU.mult).then_inc(x_prepared, 1)

        def front_rstd(eng, f):
            eng.wait_ge(x_prepared, 2 * f.n + 2)
            wait_count(eng, h_ready, f.n - 1)
            eng.tensor_tensor(rstd[:, f.par, :], vareps[:, f.par, :], minus_half[:, :], ALU.pow).then_inc(x_pow, 1)
            eng.wait_ge(x_pow, f.n + 1)
            eng.tensor_tensor(shift[:, f.par, :], minus_mean[:, f.par, :], rstd[:, f.par, :],
                              ALU.mult).then_inc(x_scaled, 1)

        def front_relu(eng, f):
            eng.wait_ge(x_scaled, f.n + 1)
            wait_count(eng, xt_turned, KC * (f.n - 1))
            for t in range(TG):
                ins = eng.activation(h[:, f.par, t, :], xb[:, f.par, t, :], ACT.Relu,
                                     bias=shift[:, f.par, t:t + 1], scale=rstd[:, f.par, t:t + 1])
            ins.then_inc(h_ready, 1)

        def front_turn(eng, f):
            eng.wait_ge(h_ready, f.n + 1)
            wait_count(eng, xt_lo, KC * f.n)
            for k in range(KC):
                for t in range(TG):
                    ins = eng.transpose(ps_t[:, k, t * P:(t + 1) * P], h[:, f.par, t, k * P:(k + 1) * P],
                                        ident[:, :])
                ins.then_inc(xt_turned, 1)

        def front_hi(eng, f):
            wait_count(eng, xs_done, TG * f.n)
            for k in range(KC):
                eng.wait_ge(xt_turned, KC * f.n + k + 1)
                eng.copy(xt[0][:, k, :], ps_t[:, k, :]).then_inc(xt_hi, 1)

        def front_lo(eng, f):
            wait_count(eng, xs_done, TG * f.n)
            for k in range(KC):
                eng.wait_ge(xt_hi, KC * f.n + k + 1)
                eng.tensor_tensor(xt[1][:, k, :], ps_t[:, k, :], xt[0][:, k, :].bitcast(F32),
                                  ALU.subtract).then_inc(xt_lo, 1)

        def front_project(eng, f, t, c0, c1):
            if t == 0:
                eng.wait_ge(xt_lo, KC * f.n + KC)
            wait_count(eng, xs_out, TG * f.n + t - 1)
            n = 0
            for k in range(KC):
                for a, b in ((0, 0), (0, 1), (1, 0)):
                    ins = eng.matmul(ps_x[:, t % 2, c0:c1], xt[a][:, k, t * P:(t + 1) * P],
                                     proj[b][:, k, c0:c1], start=(n == 0), stop=(n == 3 * KC - 1))
                    n += 1
            ins.then_inc(xs_done, 1)

        PAIR_LOOP = (2, max(2, 2 * ((NPAIR - 2) // 2)))
        CHUNK_LOOP = (4, max(4, 2 * ((NCH - 4) // 2)))
        NODE_LOOP = (2, max(2, 2 * ((NG - 3) // 2)))

        block = ctx.enter_context(nc.Block())

        @block.sync
        def _(sp):
            sp.dma_start(w_src, w_src_t.rearrange("(k p) n -> p k n", p=P)).then_inc(weights_in, 16)
            sp.dma_start(w_dst, w_dst_t.rearrange("(k p) n -> p k n", p=P)).then_inc(weights_in, 16)
            for n, a in enumerate((att_src[0:1], att_src[1:2], att_dst[0:1], att_dst[1:2])):
                sp.dma_start(att[:, n, :], a.to_broadcast([P, D])).then_inc(weights_in, 16)
            sp.dma_start(src_i, src_cols).then_inc(cols_in, 16)
            sp.dma_start(dst_i, dst_cols).then_inc(cols_in, 16)
            sp.dma_start(next_i, next_cols).then_inc(cols_in, 16)
            sp.dma_start(type_i, type_cols).then_inc(cols_in, 16)
            sp.dma_start(ew, weight_cols).then_inc(cols_in, 16)
            sp.dma_start(line_row, dst_line).then_inc(line_in, 16)
            sp.dma_start(w1, w1_t.rearrange("(k p) n -> p k n", p=P)).then_inc(rows_in, 16)
            sp.dma_start(w2, w2_t.rearrange("(m p) n -> p m n", p=P)).then_inc(rows_in, 16)
            sp.dma_start(g1_col, g1_cols).then_inc(rows_in, 16)
            sp.dma_start(b1_col, b1_cols).then_inc(rows_in, 16)
            sp.dma_start(hidden_bias[:, :], ffn_b1_cols).then_inc(rows_in, 16)
            for n, a in enumerate((bias, g1, b1, g2, b2, ffn_b2)):
                sp.dma_start(rows[:, n, :], a.to_broadcast([P, D])).then_inc(rows_in, 16)

            sp.wait_ge(empty_set, 4)
            sp.dma_start(sums[EMPTY:EMPTY + P, :], empty).then_inc(empty_stored, 16)
            sp.dma_start(row_of[0:NROWS, :].rearrange("(p t) o -> p (t o)", p=P), node_rows[:, :]).then_inc(rows_cleared, 16)

            def pair(j):
                if not j.exists(NPAIR):
                    return
                sp.wait_ge(xs_out, TG * j.n + 2)
                sp.dma_start(msgs.rearrange("(j c p) d -> j p c d", p=P, c=2)[bass.ds(j.n, 1)].rearrange("o p c d -> (o p) c d"),
                             msg_out[:, j.par, :, :]).then_inc(msg_stored[j.par], 16)
            steps(sp, pair, 0, NPAIR, *PAIR_LOOP)

            sp.wait_ge(cand_copied, 2)
            sp.dma_start(cand_line.rearrange("(h c e) -> c h e", h=HEADS, e=P), turn[0:NCH, :, :]).then_inc(cand_out, 16)
            for hd in range(HEADS):
                src = bass.AP(line.tensor, 0, [[BW, BLOCKS], [1, BW + 2]])
                sp.dma_start(line_b[hd * BLOCKS:(hd + 1) * BLOCKS, :], src).then_inc(scan_in, 16)
            sp.wait_ge(cand_out, 16)
            sp.dma_start(scan[:, 0, :], cand_line.rearrange("(p n) -> p n", p=P)).then_inc(scan_in, 16)
            sp.wait_ge(scan_step, SCAN_STEPS)
            sp.dma_start(max_line.rearrange("(p n) -> p n", p=P), scan[:, 1, :]).then_inc(max_out, 16)
            sp.wait_ge(max_out, 16)
            sp.dma_start(turn[0:NCH, :, :], max_line.rearrange("(h c e) -> c h e", h=HEADS, e=P)).then_inc(max_in, 16)

            sp.wait_ge(msg_stored[0], 16 * ((NPAIR + 1) // 2))
            sp.wait_ge(msg_stored[1], 16 * (NPAIR // 2))

            def load_chunk(c):
                if not c.exists(NCH):
                    return
                wait_count(sp, eq_ready, 2 * (c.n - 1))
                sp.dma_start(line_c[:, c.par, :], line_row[0:1, bass.ds(P * c.n + 1, P)].to_broadcast([P, P])).then_inc(line_c_in[c.par], 16)
                wait_count(sp, agg_done, c.n - 1)
                sp.dma_start(msg_in[:, c.par, :], msgs.rearrange("(c p) d -> c p d", p=P)[bass.ds(c.n, 1)].rearrange("o p d -> (o p) d")).then_inc(msg_loaded[c.par], 16)

            def chunk(c):
                load_chunk(c + 1)
                if c.exists(NCH):
                    sp.wait_ge(agg_out, c.n + 1)
                    sp.wait_ge(agg_max, c.n + 1)
                    sp.dma_start(sums[0:EP].rearrange("(c p) d -> c p d", p=P)[bass.ds(c.n, 1)].rearrange("o p d -> (o p) d"),
                                 agg[:, c.par, :]).then_inc(agg_stored[c.par], 16)
            steps(sp, chunk, -1, NCH, *CHUNK_LOOP)

            def load_nodes(g):
                if not g.exists(NG):
                    return
                f = g + NPAIR
                wait_count(sp, h_ready, f.n - 1)
                sp.sem_inc(sp_gate, 1)
                wait_count(sp, x_res_ready, g.n - 1)
                sp.dma_start(xb[:, f.par, :, :], x_tiles[:, bass.ds(TG * g.n, TG), :]).then_inc(x_in[g.par], 16)

            def nodes(i):
                load_nodes(i + 3)
                o = i - 1
                if o.exists(NG):
                    sp.wait_ge(out_ready, o.n + 1)
                    sp.dma_start(out_tiles[:, bass.ds(TG * o.n, TG), :], ob[:, o.par, :, :]).then_inc(stored[o.par], 16)
            sp.wait_ge(node_rows_in, 16)
            load_nodes(Step(0, 0))
            steps(sp, nodes, -2, NG + 1, *NODE_LOOP)
            sp.wait_ge(stored[0], 16 * ((NG + 1) // 2))
            if NG > 1:
                sp.wait_ge(stored[1], 16 * (NG // 2))

        @block.gpsimd
        def _(pool):
            pool.memset(ident[:, :], 0.0).then_inc(consts, 1)
            pool.memset(ones[:, :], 1.0).then_inc(consts, 1)
            pool.memset(minus_half[:, :], -0.5).then_inc(consts, 1)
            pool.memset(node_rows[:, :], EMPTY).then_inc(empty_set, 1)
            pool.memset(empty[:, 0:SUM], 0.0).then_inc(empty_set, 1)
            pool.memset(empty[:, SUM:REC], -BIG).then_inc(empty_set, 1)
            pool.memset(agg[:, 1, :], 0.0).then_inc(empty_set, 1)
            pool.memset(on_last, 0.0).then_inc(consts, 1)
            pool.iota(place_i, pattern=[[P, NCH]], base=0, channel_multiplier=1).then_inc(consts, 1)
            pool.iota(flag_i, pattern=[[1, 1]], base=NROWS, channel_multiplier=1).then_inc(consts, 1)
            pool.memset(dst_f[:, 0:1], -5.0).then_inc(consts, 1)
            pool.wait_ge(consts, 7)
            pool.affine_select(out=ident[:, :], in_=ident[:, :], compare_op=ALU.not_equal, fill=1.0, base=0,
                               pattern=[[-1, P]], channel_multiplier=1).then_inc(consts, 1)
            pool.affine_select(out=on_last, in_=on_last, compare_op=ALU.not_equal, fill=1.0, base=-(P - 1),
                               pattern=[[0, 1]], channel_multiplier=1).then_inc(consts, 1)

            pool.wait_ge(flag_done, 1)
            pool.wait_ge(line_in, 16)
            pool.wait_ge(cols_in, 16 * 5)
            disorder = pool.value_load(flag_i[0:1, 0:1], min_val=0, max_val=EP)
            with pool.If(disorder > 0):
                pool.wait_ge(weights_split, SPLITS)
                pool.dma_start(all_dst, line_row[0:1, 1:EP + 1].to_broadcast([P, EP])).then_inc(all_in, 16)
                pool.iota(all_num, pattern=[[1, EP]], base=0, channel_multiplier=0).then_inc(num_ready, 1)
                pool.wait_ge(ranked, 2)
                pool.wait_ge(all_in, 16)
                pool.wait_ge(num_ready, 1)
                with pool.Fori(0, NCH) as c:
                    for n, a in enumerate((rank_i, rank1_i, src_i, dst_i, type_i, ew.bitcast(I32))):
                        pool.tensor_copy(moved[:, n:n + 1], a[:, bass.ds(c, 1)]).then_inc(moved_copied, 1)
                    pool.wait_ge(moved_copied, 6 * c + 6)
                    pool.sem_inc(pool_gate, 1)
                    for to, at, n in ((s_src, 0, 2), (line, 1, 3), (s_type, 0, 4), (s_weight, 0, 5)):
                        pool.indirect_dma_start(to, bass.IndirectOffsetOnAxis(ap=moved[:, at:at + 1], axis=0),
                                                moved[:, n:n + 1], None).then_inc(sorted_out, 16)
                    pool.wait_ge(sorted_out, 64 * c + 64)
                    pool.sem_inc(pool_gate, 1)
                for to, of in ((src_i, s_src), (dst_i, line[1:EP + 1]), (next_i, line[2:EP + 2]), (type_i, s_type),
                               (ew.bitcast(I32), s_weight)):
                    pool.dma_start(to, of.rearrange("(c p) o -> p (c o)", p=P), allow_slow_non_contiguous=True).then_inc(sorted_in, 16)
                pool.wait_ge(sorted_in, 16 * 5)
            pool.memset(flag_f, 0.0).then_inc(in_order, 1)

            def gather(j):
                if not j.exists(NPAIR):
                    return
                wait_count(pool, gathered[j.par], 64 * j.half)
                wait_count(pool, h_ready, j.n - 1)
                pool.sem_inc(pool_gate, 1)
                pool.tensor_copy(idx[:, j.par, 0:2], src_i[:, bass.ds(2 * j.n, 2)]).then_inc(idx_copied, 1)
                pool.tensor_copy(idx[:, j.par, 2:4], dst_i[:, bass.ds(2 * j.n, 2)]).then_inc(idx_copied, 1)
                pool.wait_ge(idx_copied, 2 * j.n + 2)
                pool.sem_inc(pool_gate, 1)
                for t in range(TG):
                    pool.indirect_dma_start(xb[:, j.par, t, :], None, x,
                                            bass.IndirectOffsetOnAxis(ap=idx[:, j.par, t:t + 1], axis=0)).then_inc(gathered[j.par], 16)

            def pair(j):
                gather(j + 2)
                if (j + 1).exists(NPAIR):
                    front_rstd(pool, j + 1)
            pool.wait_ge(in_order, 1)
            steps(pool, pair, -2, NPAIR, *PAIR_LOOP)

            pool.wait_ge(target_ready, 1)
            pool.wait_ge(rows_cleared, 16)

            def chunk(c):
                wait_count(pool, rows_stored, 16 * c.n)
                pool.sem_inc(pool_gate, 1)
                pool.tensor_copy(slot[:, c.par, 0:1], target_i[:, bass.ds(c.n, 1)]).then_inc(slot_ready, 1)
                pool.tensor_copy(slot[:, c.par, 1:2], place_i[:, bass.ds(c.n, 1)]).then_inc(slot_ready, 1)
                pool.wait_ge(slot_ready, 2 * c.n + 2)
                pool.sem_inc(pool_gate, 1)
                pool.indirect_dma_start(row_of, bass.IndirectOffsetOnAxis(ap=slot[:, c.par, 0:1], axis=0),
                                        slot[:, c.par, 1:2], None).then_inc(rows_stored, 16)
            steps(pool, chunk, 0, NCH, *CHUNK_LOOP)
            edges_done(pool)
            pool.wait_ge(empty_stored, 16)
            pool.dma_start(node_rows[:, :], row_of[0:NROWS, :].rearrange("(p t) o -> p (t o)", p=P)).then_inc(node_rows_in, 16)
            pool.wait_ge(node_rows_in, 16)

            def gather_records(g):
                if not g.exists(NG):
                    return
                wait_count(pool, rec_in[g.par], 64 * g.half)
                wait_count(pool, hb_ready, g.n - 1)
                pool.sem_inc(pool_gate, 1)
                pool.tensor_copy(idx[:, g.par, :], node_rows[:, bass.ds(TG * g.n, TG)]).then_inc(idx_copied, 1)
                pool.wait_ge(idx_copied, 2 * NPAIR + g.n + 1)
                pool.sem_inc(pool_gate, 1)
                for t in range(TG):
                    pool.indirect_dma_start(rec[:, g.par, t, :], None, sums,
                                            bass.IndirectOffsetOnAxis(ap=idx[:, g.par, t:t + 1], axis=0)).then_inc(rec_in[g.par], 16)

            def nodes(i):
                n = i + 1
                if (i - 1).exists(NG):
                    g = i - 1
                    pool.wait_ge(u_prepared, g.n + 1)
                    pool.tensor_tensor(u_rstd, u_var, minus_half[:, :], ALU.pow).then_inc(u_scaled, 1)
                gather_records(i + 2)
                if n.exists(NG):
                    f = n + NPAIR
                    wait_count(pool, y_ready, n.n)
                    pool.wait_ge(h_ready, f.n + 1)
                    pool.tensor_tensor(hb, h[:, f.par, :, :], wide(rows[:, 0:1, :], [P, TG, D]), ALU.add).then_inc(hb_made, 1)
                    wait_count(pool, out_ready, n.n - 1)
                    pool.tensor_tensor(x_res[:, n.par], xb[:, f.par, :, :], wide(rows[:, 4:5, :], [P, TG, D]), ALU.add).then_inc(x_res_ready, 1)
                    pool.wait_ge(coef_ready, n.n + 1)
                    for t in range(TG):
                        r = rec[:, n.par, t, 0:D].rearrange("p (h c) -> p h c", h=HEADS)
                        ins = pool.tensor_tensor(r, r, coef[:, t, 0:HEADS].rearrange("p (h o) -> p h o", o=1).to_broadcast([P, HEADS, C]), ALU.mult)
                    ins.then_inc(y_scaled_part, 1)
                    pool.wait_ge(y_scaled_part, n.n + 1)
                    pool.wait_ge(hb_made, n.n + 1)
                    pool.tensor_tensor(hb, hb, rec[:, n.par, :, 0:D], ALU.add).then_inc(hb_ready, 1)
                    pool.wait_ge(y_prepared, 2 * n.n + 2)
                    wait_count(pool, z_ready, n.n)
                    pool.tensor_tensor(y_rstd, y_var, minus_half[:, :], ALU.pow).then_inc(y_pow, 1)
                    pool.wait_ge(y_pow, n.n + 1)
                    pool.tensor_tensor(y_shift, y_mm, y_rstd, ALU.mult).then_inc(y_scaled, 1)
                if (i + 2).exists(NG):
                    front_rstd(pool, i + 2 + NPAIR)
                if n.exists(NG):
                    pool.wait_ge(z_ready, n.n + 1)
                    wait_count(pool, u_ready, n.n - 1)
                    pool.tensor_tensor(res[:, n.par], z, wide(rows[:, 1:2, :], [P, TG, D]), ALU.mult).then_inc(res_part, 1)
                    pool.wait_ge(res_part, n.n + 1)
                    pool.tensor_tensor(res[:, n.par], res[:, n.par], wide(rows[:, 2:3, :], [P, TG, D]), ALU.add).then_inc(res_ready, 1)
            steps(pool, nodes, -2, NG + 1, *NODE_LOOP)

        @block.scalar
        def _(act):
            act.wait_ge(weights_in, 16 * 6)
            act.wait_ge(setup_step, SCORE_STEPS)
            for k in range(KC):
                act.copy(proj[0][:, k, 0:D], w_src[:, k, :]).then_inc(proj_hi_ready, 1)
                act.copy(proj[0][:, k, D:WV], proj_f[:, k, :]).then_inc(proj_hi_ready, 1)
            act.wait_ge(setup_step, SCORE_STEPS + KC + 1)
            for k in range(KC):
                act.copy(ffn1[0][:, k, :], w1[:, k, :]).then_inc(proj_hi_ready, 1)
            act.copy(ffn2[0][:, :, :], w2).then_inc(proj_hi_ready, 1)

            def pair(j):
                if (j + 1).exists(NPAIR):
                    front_relu(act, j + 1)
                if j.exists(NPAIR):
                    front_hi(act, j)
                    for t in range(TG):
                        act.wait_ge(xs_done, TG * j.n + t + 1)
                        if t < 2:
                            wait_count(act, msg_stored[j.par], 16 * j.half)
                            act.copy(msg_out[:, j.par, t, :], ps_x[:, t, 0:D])
                            act.copy(src_sc[:, bass.ds(2 * j.n + t, 1), :], ps_x[:, t, D:D + SC].rearrange("p (o s) -> p o s", o=1)).then_inc(xs_out, 1)
                        else:
                            act.sem_inc(act_gate, 1)
                            act.copy(dst_sc[:, bass.ds(2 * j.n + t - 2, 1), :], ps_x[:, t - 2, D:WV].rearrange("p (o s) -> p o s", o=1)).then_inc(xs_out, 1)
            act.wait_ge(cols_ready, 1)
            steps(act, pair, -1, NPAIR, *PAIR_LOOP)

            for k in range(2):
                act.wait_ge(cand_turned, k + 1)
                act.copy(turn[0:NCH, 4 * k:4 * k + 4, :], ps_t[0:NCH, k, :].rearrange("p (h e) -> p h e", h=4)).then_inc(cand_copied, 1)
            act.wait_ge(diff_ready, 1)
            act.activation(prob, alpha, ACT.Exp).then_inc(exp_ready, 1)

            def chunk(c):
                act.wait_ge(agg_done, c.n + 1)
                wait_count(act, agg_stored[c.par], 16 * c.half)
                act.copy(agg[:, c.par, 0:SUM], ps_a[:, c.par, 0:SUM]).then_inc(agg_out, 1)
            act.wait_ge(empty_set, 4)
            steps(act, chunk, 0, NCH, *CHUNK_LOOP)
            edges_done(act)

            def gelu(i, m):
                n = MF * i.n + m
                act.wait_ge(f_done, n + 1)
                wait_count(act, act_used, n - 1)
                act.activation(act_hi[:, m % 2, :], ps_f[:, m % 2, :], ACT.Gelu, bias=hidden_bias[:, m:m + 1]).then_inc(act_hi_ready, 1)
                wait_count(act, act_lo_ready, n - 1)
                act.activation(act_f[:, m % 2, :], ps_f[:, m % 2, :], ACT.Gelu, bias=hidden_bias[:, m:m + 1]).then_inc(act_f_ready, 1)

            def copy_xs(n, t):
                f = n + NPAIR
                act.wait_ge(xs_done, TG * f.n + t + 1)
                if t == 0:
                    wait_count(act, y_mul, n.n)
                act.copy(xs[:, t, :], ps_x[:, t % 2, 0:WV]).then_inc(xs_out, 1)

            def nodes(i):
                n = i + 1
                on, front = i.exists(NG), n.exists(NG)
                for m in range(MF):
                    if on:
                        gelu(i, m)
                    if m == 0 and front:
                        front_hi(act, n + NPAIR)
                    if m in (1, 2) and front:
                        copy_xs(n, 2 * m - 2)
                        copy_xs(n, 2 * m - 1)
                    if m == 3 and front:
                        act.wait_ge(exps_in, n.n + 1)
                        act.activation(expo, expo, ACT.Exp).then_inc(exps_out, 1)
                    if m == 5 and front:
                        act.wait_ge(y_scaled, n.n + 1)
                        wait_count(act, zt_turned, KC * n.n)
                        wait_count(act, res_part, n.n)
                        for t in range(TG):
                            ins = act.activation(z[:, t, :], y[:, t, :], ACT.Identity, bias=y_shift[:, t:t + 1],
                                                 scale=y_rstd[:, t:t + 1])
                        ins.then_inc(z_ready, 1)
                    if m == 6 and (n + 1).exists(NG):
                        wait_count(act, hb_made, n.n)
                        front_relu(act, n + 1 + NPAIR)
                if front:
                    for k in range(KC):
                        act.wait_ge(zt_turned, KC * n.n + k + 1)
                        wait_count(act, f_done, MF * (n.n - 1))
                        act.copy(zt[0][:, n.par, k, :], ps_t[:, k, :]).then_inc(zt_hi, 1)
            steps(act, nodes, -2, NG, *NODE_LOOP)

        @block.vector
        def _(dve):
            def link(ins, s, n):
                ins.then_inc(s, 1)
                dve.wait_ge(s, n)

            dve.wait_ge(cols_in, 16 * 5)
            dve.wait_ge(consts, 9)
            link(dve.tensor_copy(trash, flag_i), flag_sum, 1)
            link(dve.tensor_tensor(target_f, dst_i, next_i, ALU.is_gt), flag_sum, 2)
            dve.tensor_reduce(flag_f, target_f, AX, ALU.add).then_inc(flag_sum, 1)
            dve.wait_ge(weights_in, 16 * 6)
            n = 0
            for k in range(KC):
                for v in range(4):
                    w = w_src if v < 2 else w_dst
                    link(dve.tensor_tensor(att_prod, w[:, k, :], att[:, v, :], ALU.mult), setup_step, n + 1)
                    link(dve.tensor_reduce(proj_f[:, k, v * HEADS:(v + 1) * HEADS], att_prod.rearrange("p (h c) -> p h c", h=HEADS),
                                           AX, ALU.add), setup_step, n + 2)
                    n += 2
            dve.wait_ge(flag_pe, 1)
            dve.tensor_copy(flag_i[0:1, :], ps_a[0:1, 0, 0:1]).then_inc(flag_done, 1)
            dve.wait_ge(rows_in, 16 * 11)
            dve.wait_ge(hidden_pe, 1)
            dve.tensor_tensor(hidden_bias[:, :], hidden_bias[:, :], ps_f[:, 0, 0:MF], ALU.add)
            for k in range(KC):
                dve.tensor_scalar(w1[:, k, :], w1[:, k, :], g1_col[:, k:k + 1], None, ALU.mult).then_inc(setup_step, 1)
            dve.tensor_tensor(rows[:, 2, :], rows[:, 2, :], rows[:, 5, :], ALU.add).then_inc(setup_step, 1)
            n = 0
            for k in range(KC):
                for of, c0, c1 in ((w_src[:, k, :], 0, D), (proj_f[:, k, :], D, WV)):
                    n += 1
                    dve.wait_ge(proj_hi_ready, n)
                    dve.tensor_tensor(proj[1][:, k, c0:c1], of, proj[0][:, k, c0:c1].bitcast(F32), ALU.subtract).then_inc(weights_split, 1)
            for k in range(KC):
                n += 1
                dve.wait_ge(proj_hi_ready, n)
                dve.tensor_tensor(ffn1[1][:, k, :], w1[:, k, :], ffn1[0][:, k, :].bitcast(F32), ALU.subtract).then_inc(weights_split, 1)
            dve.wait_ge(proj_hi_ready, n + 1)
            dve.tensor_tensor(ffn2[1][:, :, :], w2, ffn2[0][:, :, :].bitcast(F32), ALU.subtract).then_inc(weights_split, 1)

            link(dve.tensor_copy(dst_f[:, 1:NCH + 1], dst_i), flag_sum, 4)
            disorder = dve.value_load(flag_i[0:1, 0:1], min_val=0, max_val=EP)
            with dve.If(disorder > 0):
                dve.tensor_copy(number_f, place_i).then_inc(rank_step, 1)
                dve.wait_ge(all_in, 16)
                dve.wait_ge(num_ready, 1)
                with dve.Fori(0, NCH) as c:
                    ops = 3 * BLOCKS + 1
                    own, num = dst_f[:, bass.ds(c + 1, 1)], number_f[:, bass.ds(c, 1)]
                    for q in range(BLOCKS):
                        at = slice(q * BW, (q + 1) * BW)
                        dve.wait_ge(rank_step, ops * c + 3 * q + 1)
                        dve.tensor_scalar(cmp_a, all_dst[:, at], own, None, ALU.is_lt, ALU.add,
                                          accum_out=counts[:, 2 * q:2 * q + 1]).then_inc(rank_step, 1)
                        dve.tensor_scalar(cmp_b, all_num[:, at], num, None, ALU.is_lt).then_inc(rank_step, 1)
                        dve.wait_ge(rank_step, ops * c + 3 * q + 3)
                        dve.scalar_tensor_tensor(out=cmp_a, in0=all_dst[:, at], scalar=own, in1=cmp_b, op0=ALU.is_equal,
                                                 op1=ALU.mult, accum_out=counts[:, 2 * q + 1:2 * q + 2]).then_inc(rank_step, 1)
                    dve.wait_ge(rank_step, ops * c + 3 * BLOCKS + 1)
                    dve.tensor_reduce(rank_f[:, bass.ds(c, 1)], counts, AX, ALU.add).then_inc(rank_step, 1)
                dve.wait_ge(rank_step, (3 * BLOCKS + 1) * NCH + 1)
                dve.tensor_copy(rank_i, rank_f).then_inc(ranked, 1)
                dve.tensor_scalar(rank1_i, rank_f, 1.0, None, ALU.add).then_inc(ranked, 1)
            dve.wait_ge(in_order, 1)
            dve.tensor_copy(dst_f[:, 1:NCH + 1], dst_i).then_inc(target_step, 1)
            dve.tensor_copy(type_1, type_i).then_inc(target_step, 1)
            dve.tensor_tensor(last, dst_i, next_i, ALU.not_equal).then_inc(target_step, 1)
            dve.wait_ge(target_step, 3)
            dve.tensor_scalar(type_0, type_1, -1.0, 1.0, ALU.mult, ALU.add).then_inc(cols_ready, 1)
            link(dve.tensor_scalar(target_f, dst_f[:, 1:NCH + 1], trash, None, ALU.subtract), target_step, 4)
            link(dve.tensor_tensor(target_f, target_f, last, ALU.mult), target_step, 5)
            dve.tensor_scalar(target_i, target_f, trash, None, ALU.add).then_inc(target_ready, 1)

            def pair(j):
                if (j + 1).exists(NPAIR):
                    dve.wait_ge(gathered[(j + 1).par], 64 * ((j + 1).half + 1))
                    front_stats(dve, j + 1)
                if j.exists(NPAIR):
                    front_lo(dve, j)
            steps(dve, pair, -1, NPAIR, *PAIR_LOOP)

            dve.wait_ge(xs_out, TG * NPAIR)
            n = 0
            t0, t1 = (wide(a.rearrange("p (c o) -> p c o", o=1), [P, NCH, HEADS]) for a in (type_0, type_1))
            ops = [
                lambda: dve.tensor_tensor(alpha, src_sc[:, :, 0:HEADS], dst_sc[:, :, SC:SC + HEADS], ALU.add),
                lambda: dve.tensor_tensor(soft, src_sc[:, :, HEADS:SC], dst_sc[:, :, SC + HEADS:2 * SC], ALU.add),
                lambda: dve.tensor_tensor(prob, dst_sc[:, :, 0:HEADS], dst_sc[:, :, SC:SC + HEADS], ALU.add),
                lambda: dve.tensor_tensor(alpha, alpha, t0, ALU.mult),
                lambda: dve.tensor_tensor(soft, soft, t1, ALU.mult),
                lambda: dve.scalar_tensor_tensor(out=prob, in0=prob, scalar=0.2, in1=prob, op0=ALU.mult, op1=ALU.max),
                lambda: dve.tensor_tensor(alpha, alpha, soft, ALU.add),
                lambda: dve.scalar_tensor_tensor(out=alpha, in0=alpha, scalar=0.2, in1=alpha, op0=ALU.mult, op1=ALU.max),
            ]
            for op in ops:
                n += 1
                link(op(), alpha_step, n)
            dve.tensor_tensor(cand.rearrange("p h c -> p c h"), alpha, prob, ALU.max).then_inc(cand_ready, 1)

            dve.wait_ge(scan_in, 16 * (HEADS + 1))
            st = [0]

            def step(ins):
                st[0] += 1
                link(ins, scan_step, st[0])
            step(dve.tensor_tensor(resets, line_b[:, 0:BW + 1], line_b[:, 1:BW + 2], ALU.not_equal))
            step(dve.tensor_scalar(resets, resets, -BIG, None, ALU.mult))
            for way in range(2):
                r = resets[:, 0:BW] if way == 0 else resets[:, 1:BW + 1]
                of, to = (scan[:, 0, :], scan[:, 1, :]) if way == 0 else (scan[:, 0, :], scan[:, 1, :])
                flip = (lambda a: a) if way == 0 else (lambda a: a[:, ::-1])
                step(dve.tensor_tensor_scan(flip(to), flip(r), flip(of), -BIG, ALU.add, ALU.max))
                e = BW - 1 if way == 0 else 0
                step(dve.tensor_copy(ends[:, 0:1], to[:, e:e + 1]))
                step(dve.tensor_reduce(ends[:, 1:2], r, AX, ALU.min))
                dve.wait_ge(scan_pe, 2 * way + 1)
                step(dve.tensor_copy(ends_row[0:1, 0:2, :], ps_f[0:1, 0, 0:2 * P].rearrange("p (a b) -> p a b", a=2)))
                step(dve.memset(ends_row[0:1, 2, :], -BIG))
                if way == 0:
                    o, i_ = ends_row[0:1, 2, 1:P], slice(0, P - 1)
                else:
                    o, i_ = ends_row[0:1, 2, 0:P - 1], slice(1, P)
                step(dve.tensor_tensor_scan(flip(o), flip(ends_row[0:1, 1, i_]), flip(ends_row[0:1, 0, i_]), -BIG, ALU.add, ALU.max))
                dve.wait_ge(scan_pe, 2 * way + 2)
                step(dve.tensor_copy(carry, ps_f[:, 1, 0:1]))
                step(dve.tensor_tensor_scan(flip(to), flip(r), flip(of), carry, ALU.add, ALU.max))
                if way == 0:
                    step(dve.tensor_copy(scan[:, 0, :], scan[:, 1, :]))
            assert st[0] == SCAN_STEPS

            dve.wait_ge(max_turned, 2)
            for k in range(2):
                link(dve.tensor_copy(tops[:, 4 * k:4 * k + 4, :], ps_t[:, k, :].rearrange("p (h e) -> p h e", h=4)[:, :, 0:NCH]), alpha_step, n + 1)
                n += 1
            dve.tensor_tensor(alpha, alpha, tops.rearrange("p h c -> p c h"), ALU.subtract).then_inc(diff_ready, 1)
            dve.wait_ge(exp_ready, 1)
            dve.tensor_tensor(soft, prob, wide(ew.rearrange("p (c o) -> p c o", o=1), [P, NCH, HEADS]), ALU.mult).then_inc(soft_ready, 1)
            dve.wait_ge(soft_ready, 1)

            def chunk(c):
                dve.wait_ge(line_c_in[c.par], 16 * (c.half + 1))
                wait_count(dve, agg_done, c.n - 1)
                dve.tensor_scalar(eq[:, c.par, :], line_c[:, c.par, :], dst_f[:, bass.ds(c.n + 1, 1)], None,
                                  ALU.is_equal).then_inc(eq_ready, 1)
                dve.tensor_scalar(eq_carry[:, c.par, :], line_c[:, c.par, :], dst_f[:, bass.ds(c.n, 1)], on_last,
                                  ALU.is_equal, ALU.mult).then_inc(eq_ready, 1)
                dve.wait_ge(msg_loaded[c.par], 16 * (c.half + 1))
                m = msg_in[:, c.par, :].rearrange("p (h c) -> p h c", h=HEADS)
                dve.tensor_tensor(m, m, soft[:, bass.ds(c.n, 1), :].rearrange("p o h -> p (o h)").rearrange("p (h o) -> p h o", o=1).to_broadcast([P, HEADS, C]),
                                  ALU.mult).then_inc(vals_ready, 1)
                wait_count(dve, agg_stored[c.par], 16 * c.half)
                dve.tensor_copy(agg[:, c.par, SUM:REC], tops[:, :, bass.ds(c.n, 1)].rearrange("p h o -> p (h o)")).then_inc(agg_max, 1)
            dve.wait_ge(empty_set, 4)
            steps(dve, chunk, 0, NCH, *CHUNK_LOOP)
            edges_done(dve)

            def act_rest(i, m):
                n = MF * i.n + m
                dve.wait_ge(act_f_ready, n + 1)
                wait_count(dve, act_used, n - 1)
                dve.tensor_tensor(act_lo[:, m % 2, :], act_f[:, m % 2, :], act_hi[:, m % 2, :].bitcast(F32),
                                  ALU.subtract).then_inc(act_lo_ready, 1)

            def logits(n):
                s = AL_STEPS * n.n
                dve.wait_ge(xs_out, TG * (n + NPAIR).n + TG)
                dve.wait_ge(rec_in[n.par], 64 * (n.half + 1))
                dve.tensor_tensor(al, xs[:, :, D:D + HEADS], xs[:, :, D + SC:D + SC + HEADS], ALU.add).then_inc(al_step, 1)
                dve.wait_ge(al_step, s + 1)
                dve.scalar_tensor_tensor(out=al, in0=al, scalar=0.2, in1=al, op0=ALU.mult, op1=ALU.max).then_inc(al_step, 1)
                dve.wait_ge(al_step, s + 2)
                dve.tensor_tensor(top, al, rec[:, n.par, :, SUM:REC], ALU.max).then_inc(al_step, 1)
                dve.wait_ge(al_step, s + 3)
                dve.tensor_tensor(expo[:, :, 0:HEADS], rec[:, n.par, :, SUM:REC], top, ALU.subtract).then_inc(al_step, 1)
                dve.tensor_tensor(expo[:, :, HEADS:SC], al, top, ALU.subtract).then_inc(exps_in, 1)

            def coefs(n):
                s = AL_STEPS * n.n + 4
                dve.wait_ge(exps_out, n.n + 1)
                dve.tensor_tensor(den, rec[:, n.par, :, D:SUM], expo[:, :, 0:HEADS], ALU.mult).then_inc(al_step, 1)
                dve.wait_ge(al_step, s + 1)
                dve.tensor_tensor(den, den, expo[:, :, HEADS:SC], ALU.add).then_inc(al_step, 1)
                dve.wait_ge(al_step, s + 2)
                dve.reciprocal(top, den).then_inc(al_step, 1)
                dve.wait_ge(al_step, s + 3)
                wait_count(dve, y_scaled_part, n.n)
                dve.tensor_tensor(coef[:, :, 0:HEADS], expo[:, :, 0:HEADS], top, ALU.mult).then_inc(coef_ready, 1)
                dve.tensor_tensor(coef[:, :, HEADS:SC], expo[:, :, HEADS:SC], top, ALU.mult).then_inc(al_step, 1)

            def self_message(n):
                dve.wait_ge(al_step, AL_STEPS * n.n + 8)
                wait_count(dve, z_ready, n.n)
                for t in range(TG):
                    ins = dve.tensor_tensor(y[:, t, :].rearrange("p (h c) -> p h c", h=HEADS), xs[:, t, 0:D].rearrange("p (h c) -> p h c", h=HEADS),
                                            coef[:, t, HEADS:SC].rearrange("p (h o) -> p h o", o=1).to_broadcast([P, HEADS, C]), ALU.mult)
                ins.then_inc(y_mul, 1)

            def first_norm(n):
                dve.wait_ge(y_mul, n.n + 1)
                dve.wait_ge(hb_ready, n.n + 1)
                dve.tensor_tensor(y, y, hb, ALU.add).then_inc(y_ready, 1)
                dve.wait_ge(y_ready, n.n + 1)
                for t in range(TG):
                    dve.bn_stats(y_stat[:, t, :], y[:, t, :]).then_inc(y_stats, 1)
                dve.wait_ge(y_stats, 2 * TG * n.n + TG)
                dve.sem_inc(dve_gate, 1)
                for t in range(TG):
                    dve.bn_aggr(y_mv[:, t, :], y_stat[:, t, :]).then_inc(y_stats, 1)
                dve.wait_ge(y_stats, 2 * TG * n.n + 2 * TG)
                wait_count(dve, y_scaled, n.n)
                dve.tensor_scalar(y_var, y_mv[:, :, 1], EPS, None, ALU.add).then_inc(y_prepared, 1)
                dve.tensor_scalar(y_mm, y_mv[:, :, 0], -1.0, None, ALU.mult).then_inc(y_prepared, 1)

            def add_ffn(o):
                dve.wait_ge(act_used, MF * o.n + MF)
                dve.wait_ge(res_ready, o.n + 1)
                wait_count(dve, out_ready, o.n)
                for k in range(2):
                    ins = dve.tensor_tensor(u[:, 2 * k:2 * k + 2, :], ps_a[:, k, :].rearrange("p (t d) -> p t d", t=2),
                                            res[:, o.par, 2 * k:2 * k + 2, :], ALU.add)
                ins.then_inc(u_ready, 1)

            def second_norm(o):
                dve.wait_ge(u_ready, o.n + 1)
                for t in range(TG):
                    dve.bn_stats(u_stat[:, t, :], u[:, t, :]).then_inc(u_stats, 1)
                dve.wait_ge(u_stats, 2 * TG * o.n + TG)
                dve.sem_inc(dve_gate, 1)
                for t in range(TG):
                    dve.bn_aggr(u_mv[:, t, :], u_stat[:, t, :]).then_inc(u_stats, 1)
                dve.wait_ge(u_stats, 2 * TG * o.n + 2 * TG)
                dve.tensor_scalar(u_var, u_mv[:, :, 1], EPS, None, ALU.add).then_inc(u_prepared, 1)

            def finish(o):
                for t in range(TG):
                    dve.scalar_tensor_tensor(out=u[:, t, :], in0=u[:, t, :], scalar=u_mv[:, t, 0:1], in1=rows[:, 3, :],
                                             op0=ALU.subtract, op1=ALU.mult).then_inc(out_step, 1)
                dve.wait_ge(u_scaled, o.n + 1)
                wait_count(dve, stored[o.par], 16 * o.half)
                dve.wait_ge(out_step, TG * o.n + TG)
                dve.wait_ge(x_res_ready, o.n + 1)
                for t in range(TG):
                    ins = dve.scalar_tensor_tensor(out=ob[:, o.par, t, :], in0=u[:, t, :], scalar=u_rstd[:, t:t + 1],
                                                   in1=x_res[:, o.par, t, :], op0=ALU.mult, op1=ALU.add)
                ins.then_inc(out_ready, 1)

            def nodes(i):
                n, o = i + 1, i - 1
                on, front, back = i.exists(NG), n.exists(NG), o.exists(NG)
                if back:
                    add_ffn(o)
                if on:
                    act_rest(i, 0)
                if front:
                    front_lo(dve, n + NPAIR)
                if back:
                    second_norm(o)
                if on:
                    act_rest(i, 1)
                if back:
                    finish(o)
                if on:
                    act_rest(i, 2)
                if front:
                    logits(n)
                if on:
                    act_rest(i, 3)
                if front:
                    coefs(n)
                    self_message(n)
                if on:
                    act_rest(i, 4)
                if front:
                    first_norm(n)
                if on:
                    act_rest(i, 5)
                if (n + 1).exists(NG):
                    dve.wait_ge(x_in[(n + 1).par], 16 * ((n + 1).half + 1))
                    front_stats(dve, n + 1 + NPAIR)
                if on:
                    act_rest(i, 6)
                    act_rest(i, 7)
                if front:
                    for k in range(KC):
                        dve.wait_ge(zt_hi, KC * n.n + k + 1)
                        dve.tensor_tensor(zt[1][:, n.par, k, :], ps_t[:, k, :], zt[0][:, n.par, k, :].bitcast(F32),
                                          ALU.subtract).then_inc(zt_lo, 1)
            steps(dve, nodes, -2, NG + 1, *NODE_LOOP)

        @block.tensor
        def _(pe):
            pe.wait_ge(consts, 9)
            pe.wait_ge(flag_sum, 3)
            pe.matmul(ps_a[0:1, 0, 0:1], flag_f, ones[:, :], start=True, stop=True).then_inc(flag_pe, 1)
            pe.wait_ge(rows_in, 16 * 11)
            for m in range(MF):
                for k in range(KC):
                    ins = pe.matmul(ps_f[:, 0, m:m + 1], w1[:, k, m * P:(m + 1) * P], b1_col[:, k:k + 1],
                                    start=(k == 0), stop=(k == KC - 1))
            ins.then_inc(hidden_pe, 1)

            def pair(j):
                front_turn(pe, j)
                for t in range(TG):
                    front_project(pe, j, t, 0 if t < 2 else D, D + SC if t < 2 else WV)
            pe.wait_ge(weights_split, SPLITS)
            steps(pe, pair, 0, NPAIR, *PAIR_LOOP)

            pe.wait_ge(cand_ready, 1)
            pe.wait_ge(xt_lo, KC * NPAIR)
            for k in range(2):
                for q in range(4):
                    ins = pe.transpose(ps_t[0:NCH, k, q * P:(q + 1) * P], cand[:, 4 * k + q, :], ident[:, :])
                ins.then_inc(cand_turned, 1)
            for way in range(2):
                pe.wait_ge(scan_step, 5 + way * 9)
                pe.transpose(ps_f[0:1, 0, 0:P], ends[:, 0:1], ident[:, :])
                pe.transpose(ps_f[0:1, 0, P:2 * P], ends[:, 1:2], ident[:, :]).then_inc(scan_pe, 1)
                pe.wait_ge(scan_step, 8 + way * 9)
                pe.transpose(ps_f[:, 1, 0:1], ends_row[0:1, 2, :], ident[0:1, 0:1]).then_inc(scan_pe, 1)
            pe.wait_ge(max_in, 16)
            for k in range(2):
                for q in range(4):
                    ins = pe.transpose(ps_t[:, k, q * P:q * P + NCH], turn[0:NCH, 4 * k + q, :], ident[0:NCH, 0:NCH])
                ins.then_inc(max_turned, 1)

            def chunk(c):
                pe.wait_ge(eq_ready, 2 * c.n + 2)
                pe.wait_ge(vals_ready, c.n + 1)
                wait_count(pe, agg_out, c.n - 1)
                to = ps_a[:, c.par, :]
                pe.matmul(to[:, 0:D], eq[:, c.par, :], msg_in[:, c.par, :], start=True, stop=False, skip_group_check=True)
                pe.matmul(to[:, D:SUM], eq[:, c.par, :], prob[:, bass.ds(c.n, 1), :].rearrange("p o h -> p (o h)"), start=False, stop=False, skip_group_check=True)
                wait_count(pe, agg_out, c.n)
                pe.matmul(to[:, 0:SUM], eq_carry[:, c.par, :], agg[:, 1 - c.par, 0:SUM], start=False, stop=True, skip_group_check=True).then_inc(agg_done, 1)
            pe.wait_ge(exp_ready, 1)
            pe.wait_ge(empty_set, 4)
            steps(pe, chunk, 0, NCH, *CHUNK_LOOP)

            def ffn1_piece(i, m):
                n = MF * i.n + m
                if m == 0:
                    pe.wait_ge(zt_lo, KC * i.n + KC)
                wait_count(pe, act_f_ready, n - 1)
                j = 0
                for k in range(KC):
                    for a, b in ((0, 0), (0, 1), (1, 0)):
                        ins = pe.matmul(ps_f[:, m % 2, :], ffn1[a][:, k, m * P:(m + 1) * P], zt[b][:, i.par, k, :],
                                        start=(j == 0), stop=(j == 3 * KC - 1))
                        j += 1
                ins.then_inc(f_done, 1)

            def ffn2_piece(i, m):
                n = MF * i.n + m
                if m == 0:
                    wait_count(pe, u_ready, i.n)
                pe.wait_ge(act_hi_ready, n + 1)
                pe.wait_ge(act_lo_ready, n + 1)
                for t in range(TG):
                    cols = slice(t * P, (t + 1) * P)
                    to = ps_a[:, t // 2, (t % 2) * D:(t % 2 + 1) * D]
                    pe.matmul(to, act_hi[:, m % 2, cols], ffn2[0][:, m, :], start=(m == 0 and t % 2 == 0), stop=False, skip_group_check=True)
                    pe.matmul(to, act_hi[:, m % 2, cols], ffn2[1][:, m, :], start=False, stop=False, skip_group_check=True)
                    ins = pe.matmul(to, act_lo[:, m % 2, cols], ffn2[0][:, m, :], start=False, stop=(m == MF - 1), skip_group_check=True)
                ins.then_inc(act_used, 1)

            def turn_z(n):
                pe.wait_ge(z_ready, n.n + 1)
                pe.wait_ge(xt_lo, KC * (n + NPAIR).n + KC)
                for k in range(KC):
                    for t in range(TG):
                        ins = pe.transpose(ps_t[:, k, t * P:(t + 1) * P], z[:, t, k * P:(k + 1) * P], ident[:, :])
                    ins.then_inc(zt_turned, 1)

            def nodes(i):
                n = i + 1
                on, front = i.exists(NG), n.exists(NG)
                for m in range(MF):
                    if on:
                        ffn1_piece(i, m)
                    if m == 0 and front:
                        wait_count(pe, zt_lo, KC * n.n)
                        front_turn(pe, n + NPAIR)
                    if m == MF - 1 and front:
                        turn_z(n)
                    if on and m:
                        ffn2_piece(i, m - 1)
                    if m in (1, 2) and front:
                        front_project(pe, n + NPAIR, 2 * m - 2, 0, WV)
                        front_project(pe, n + NPAIR, 2 * m - 1, 0, WV)
                if on:
                    ffn2_piece(i, MF - 1)
            steps(pe, nodes, -1, NG, *NODE_LOOP)


def kernel(x, src, dst, edge_type_2, edge_weight, L0_gnn_W_src, L0_gnn_W_dst, L0_gnn_att_src, L0_gnn_att_dst,
           L0_gnn_bias, L0_gnn_ln1_g, L0_gnn_ln1_b, L0_gnn_ln2_g, L0_gnn_ln2_b, L0_gnn_ffn_W1, L0_gnn_ffn_b1,
           L0_gnn_ffn_W2, L0_gnn_ffn_b2):
    import concourse.bacc as bacc
    from concourse.bass_utils import run_bass_kernel_spmd

    a = {k: np.asarray(v) for k, v in dict(locals()).items()
         if k not in ("bacc", "run_bass_kernel_spmd")}
    n, d = a["x"].shape
    e = a["src"].shape[0]
    rows = -(-(n + 1) // GR) * GR
    ch = -(-e // (2 * P)) * 2
    ep = ch * P

    def padded(v, fill):
        return np.concatenate([v, np.full(ep - e, fill, v.dtype)])

    def columns(v, parts=P):
        return np.ascontiguousarray(v.reshape(-1, parts).T)

    dst_p = padded(a["dst"], n)
    dst_line = np.concatenate([np.full(1, -1, dst_p.dtype), dst_p, np.full(1, n + 1, dst_p.dtype)])
    put = {
        "x": np.concatenate([a["x"], np.zeros((rows - n, d), a["x"].dtype)]),
        "src_cols": columns(padded(a["src"], n)),
        "dst_cols": columns(dst_p),
        "next_cols": columns(dst_line[2:]),
        "type_cols": columns(padded(a["edge_type_2"], 0)),
        "weight_cols": columns(padded(a["edge_weight"], 0)),
        "dst_line": dst_line.reshape(1, -1),
        "w_src_t": np.ascontiguousarray(a["L0_gnn_W_src"].T),
        "w_dst_t": np.ascontiguousarray(a["L0_gnn_W_dst"].T),
        "att_src": a["L0_gnn_att_src"].reshape(2, -1),
        "att_dst": a["L0_gnn_att_dst"].reshape(2, -1),
        "bias": a["L0_gnn_bias"].reshape(1, -1),
        "g1": a["L0_gnn_ln1_g"].reshape(1, -1),
        "b1": a["L0_gnn_ln1_b"].reshape(1, -1),
        "g2": a["L0_gnn_ln2_g"].reshape(1, -1),
        "b2": a["L0_gnn_ln2_b"].reshape(1, -1),
        "g1_cols": columns(a["L0_gnn_ln1_g"]),
        "b1_cols": columns(a["L0_gnn_ln1_b"]),
        "w1_t": np.ascontiguousarray(a["L0_gnn_ffn_W1"].T),
        "ffn_b1_cols": columns(a["L0_gnn_ffn_b1"]),
        "w2_t": np.ascontiguousarray(a["L0_gnn_ffn_W2"].T),
        "ffn_b2": a["L0_gnn_ffn_b2"].reshape(1, -1),
    }
    nc = bacc.Bacc("TRN2", target_bir_lowering=False, num_devices=1)
    args = {k: nc.dram_tensor(f"in_{k}", v.shape, mybir.dt.from_np(v.dtype), kind="ExternalInput").ap()
            for k, v in put.items()}
    out = nc.dram_tensor("out_0", (rows, d), F32, kind="ExternalOutput").ap()
    build(nc, out=out, **args)
    r = run_bass_kernel_spmd(nc, [{f"in_{k}": v for k, v in put.items()}], core_ids=[0])
    return r.results[0]["out_0"][:n]
```

```python
from contextlib import ExitStack

import numpy as np

import concourse.bass as bass
from concourse import mybir

F32 = mybir.dt.float32
F32R = mybir.dt.float32r
I32 = mybir.dt.int32
ALU = mybir.AluOpType
ACT = mybir.ActivationFunctionType
AX = mybir.AxisListType.X

P = 128
TG = 4
GR = TG * P
HEADS = 8
BLOCKS = P // HEADS
EPS = 1e-5
BIG = 1e30


class Step:

    def __init__(self, k, off):
        self.k, self.off = k, off

    def __add__(self, d):
        return Step(self.k, self.off + d)

    def __sub__(self, d):
        return Step(self.k, self.off - d)

    @property
    def n(self):
        return 2 * self.k + self.off

    @property
    def half(self):
        return self.k + self.off // 2

    @property
    def par(self):
        return self.off % 2

    def exists(self, count):
        return not isinstance(self.n, int) or 0 <= self.n < count


def chunks(j):
    return [Step(2 * j.k, 2 * j.off + q) for q in range(2)]


def wait_count(eng, sem, count):
    if not (isinstance(count, int) and count <= 0):
        eng.wait_ge(sem, count)


AB = 4
LAG = 2
SPLITS = 7
SCORE_STEPS = 16
SCAN_STEPS = 19
AL_STEPS = 8


def steps(eng, body, first, last, lo, hi):
    for s in range(first, lo):
        body(Step(0, s))
    if hi > lo:
        with eng.Fori(lo // 2, hi // 2) as k:
            body(Step(k, 0))
            body(Step(k, 1))
    for s in range(max(lo, hi), last):
        body(Step(0, s))


def build(nc, x, src_cols, dst_cols, next_cols, type_cols, weight_cols, dst_line, w_src_t, w_dst_t,
          att_src, att_dst, bias, g1, b1, g2, b2, g1_cols, b1_cols, w1_t, ffn_b1_cols, w2_t, ffn_b2, out):
    NROWS, D = x.shape
    NT = NROWS // P
    NG = NT // TG
    NCH = src_cols.shape[1]
    EP = NCH * P
    BW = EP // BLOCKS
    NPAIR = NCH // 2
    C = D // HEADS
    KC = D // P
    F = w1_t.shape[1]
    MF = F // P
    SC = 2 * HEADS
    WV = D + 2 * SC
    REC = D + 2 * HEADS
    SUM = D + HEADS
    EMPTY = EP
    assert D == KC * P and NT % TG == 0 and NCH % 2 == 0 and NCH <= P and EP % BLOCKS == 0

    sums = nc.dram_tensor("sums", (EP + P, REC), F32, kind="Internal").ap()
    row_of = nc.dram_tensor("row_of", (NROWS + P, 1), I32, kind="Internal").ap()
    msgs = nc.dram_tensor("msgs", (EP, D), F32, kind="Internal").ap()
    cand_line = nc.dram_tensor("cand_line", (HEADS * EP,), F32, kind="Internal").ap()
    max_line = nc.dram_tensor("max_line", (HEADS * EP,), F32, kind="Internal").ap()
    line = nc.dram_tensor("line", (EP + 2, 1), I32, kind="Internal").ap()
    s_src = nc.dram_tensor("s_src", (EP, 1), I32, kind="Internal").ap()
    s_type = nc.dram_tensor("s_type", (EP, 1), I32, kind="Internal").ap()
    s_weight = nc.dram_tensor("s_weight", (EP, 1), I32, kind="Internal").ap()

    x_tiles = x.rearrange("(p t) d -> p t d", p=P)
    out_tiles = out.rearrange("(p t) d -> p t d", p=P)
    line_row = line.rearrange("e o -> o e")

    with ExitStack() as ctx:
        def sb(name, shape, dt=F32):
            return ctx.enter_context(nc.sbuf_tensor(name, shape, dt))

        def sem(name):
            return ctx.enter_context(nc.semaphore(name))

        proj = [sb(f"proj_{n}", [P, KC, WV], F32R) for n in ("hi", "lo")]
        ffn1 = [sb(f"ffn1_{n}", [P, KC, F], F32R) for n in ("hi", "lo")]
        ffn2 = [sb(f"ffn2_{n}", [P, MF, D], F32R) for n in ("hi", "lo")]
        ident = sb("ident", [P, P])
        ones = sb("ones", [P, 1])
        rows = sb("rows", [P, 6, D])
        hidden_bias = sb("hidden_bias", [P, MF])
        minus_half = sb("minus_half", [P, TG])
        node_rows = sb("node_rows", [P, NT], I32)
        idx = sb("idx", [P, 2, TG], I32)
        slot = sb("slot", [P, 2, 2], I32)
        xt = [sb(f"xt_{n}", [P, KC, GR], F32R) for n in ("hi", "lo")]
        zt = [sb(f"zt_{n}", [P, 2, KC, GR], F32R) for n in ("hi", "lo")]
        act_hi = sb("act_hi", [P, AB, GR], F32R)
        act_lo = sb("act_lo", [P, AB, GR], F32R)
        xb = sb("xb", [P, 2, TG, D])
        h = sb("h", [P, 2, TG, D])
        stat = sb("stat", [P, TG, 6])
        mv = sb("mv", [P, 2, TG, 2])
        vareps = sb("vareps", [P, 2, TG])
        minus_mean = sb("minus_mean", [P, 2, TG])
        rstd = sb("rstd", [P, 2, TG])
        shift = sb("shift", [P, 2, TG])

        ARENA = max(19000, EP + BW + 13 * NCH + 3 * P + 3 * REC + 64)
        arena = sb("arena", [P, ARENA])
        used = [0]

        def part(dims, dt=None):
            n = int(np.prod(dims))
            a = arena[:, used[0]:used[0] + n]
            used[0] += n
            assert used[0] <= ARENA
            if dt is not None:
                a = a.bitcast(dt)
            if len(dims) == 2:
                a = a.rearrange("p (a b) -> p a b", a=dims[0])
            if len(dims) == 3:
                a = a.rearrange("p (a b c) -> p a b c", a=dims[0], b=dims[1])
            return a

        src_i, dst_i, next_i, type_i = (part([NCH], I32) for _ in range(4))
        ew, type_1, type_0, last = (part([NCH]) for _ in range(4))
        dst_f = part([NCH + 1])
        target_f = part([NCH])
        target_i, place_i = part([NCH], I32), part([NCH], I32)
        trash, on_last, carry, flag_f = part([1]), part([1]), part([1]), part([1])
        flag_i = part([1], I32)
        ends = part([2])
        ends_row = part([3, P])
        agg = part([2, REC])
        empty = part([REC])
        edges_end = used[0]
        src_sc, dst_sc = part([NCH, SC]), part([NCH, 2 * SC])
        alpha, prob, soft = (part([NCH, HEADS]) for _ in range(3))
        cand, tops = part([HEADS, NCH]), part([HEADS, NCH])
        turn = part([HEADS, P])
        scan = part([2, BW])
        resets = part([BW + 1])
        line_b = part([BW + 2], I32)
        line_c = part([2, 2 * P], I32)
        eq, eq_carry = part([2, P]), part([2, P])
        msg_out = part([2, 2, D])
        msg_in = part([4, D])
        used[0] = edges_end
        w_src, w_dst = part([KC, D]), part([KC, D])
        att = part([4, D])
        att_prod = part([D])
        w1, w2 = part([KC, F]), part([MF, D])
        g1_col, b1_col = part([KC]), part([KC])
        proj_f = part([KC, 2 * SC])
        used[0] = edges_end
        all_dst, all_num = part([EP], I32), part([BW], I32)
        cmp_a = xb[:, 0, :, :].rearrange("p t d -> p (t d)")[:, 0:BW]
        cmp_b = xb[:, 1, :, :].rearrange("p t d -> p (t d)")[:, 0:BW]
        counts = h[:, 0, 0, 0:2 * BLOCKS]
        number_f = h[:, 0, 1, 0:NCH]
        rank_f = h[:, 0, 2, 0:NCH]
        rank_i = h[:, 0, 3, 0:NCH].bitcast(I32)
        rank1_i = h[:, 1, 3, 0:NCH].bitcast(I32)
        moved = h[:, 1, 2, 0:6].bitcast(I32)
        used[0] = 0
        xs = part([2, TG * WV]).rearrange("p b (t d) -> p b t d", t=TG)
        rec = part([2, TG * REC]).rearrange("p b (t d) -> p b t d", t=TG)
        x_res = part([2, TG, D])
        y, hb, z = part([TG, D]), part([TG, D]), part([TG, D])
        res = part([2, TG, D])
        u = part([TG, D])
        ob = part([2, TG, D])
        act_f = part([AB, GR])
        y_stat, y_mv = part([TG, 6]), part([TG, 2])
        y_var, y_mm, y_rstd, y_shift = (part([TG]) for _ in range(4))
        u_stat, u_mv = part([TG, 6]), part([TG, 2])
        u_var, u_rstd = part([TG]), part([TG])
        al, top, den = (part([TG, HEADS]) for _ in range(3))
        expo, coef = part([TG, 2 * HEADS]), part([TG, 2 * HEADS])

        def pb(name):
            return ctx.enter_context(nc.psum_tensor(name, [P, 2, 512], F32))
        ps_t, ps_x, ps_f, ps_a = pb("ps_t"), pb("ps_x"), pb("ps_f"), pb("ps_a")

        (weights_in, rows_in, cols_in, consts, setup_step, hidden_pe, proj_hi_ready, weights_split, line_in,
         flag_sum, flag_pe, flag_done, all_in, num_ready, rank_step, ranked, moved_copied, sorted_out, sorted_in, in_order,
         cols_ready, rows_cleared, empty_set, empty_stored, idx_copied, stat_step, x_stats, x_prepared, x_pow, x_scaled,
         h_ready, xt_turned, xt_hi, xt_lo, xs_done, xs_out, alpha_step, cand_ready, cand_turned, cand_copied,
         cand_out, scan_in, scan_step, scan_pe, max_out, max_in, max_turned, diff_ready, exp_ready,
         soft_ready, vals_ready, eq_ready, agg_done, agg_out, agg_max, target_ready, target_step, rows_stored,
         slot_ready, sp_gate, pool_gate, act_gate, dve_gate, node_rows_in, al_step, exps_in, exps_out, coef_ready, hb_made, hb_ready,
         y_scaled_part, y_mul, y_ready, y_stats, y_prepared, y_pow, y_scaled, z_ready, zt_turned, zt_hi, zt_lo,
         x_res_ready, res_part, res_ready, f_done, act_hi_ready, act_f_ready, act_lo_ready, act_used,
         u_ready, u_stats, u_prepared, u_scaled, out_step, out_ready) = (sem(n) for n in """
         weights_in rows_in cols_in consts setup_step hidden_pe proj_hi_ready weights_split line_in
         flag_sum flag_pe flag_done all_in num_ready rank_step ranked moved_copied sorted_out sorted_in in_order
         cols_ready rows_cleared empty_set empty_stored idx_copied stat_step x_stats x_prepared x_pow x_scaled
         h_ready xt_turned xt_hi xt_lo xs_done xs_out alpha_step cand_ready cand_turned cand_copied
         cand_out scan_in scan_step scan_pe max_out max_in max_turned diff_ready exp_ready
         soft_ready vals_ready eq_ready agg_done agg_out agg_max target_ready target_step rows_stored
         slot_ready sp_gate pool_gate act_gate dve_gate node_rows_in al_step exps_in exps_out coef_ready hb_made hb_ready
         y_scaled_part y_mul y_ready y_stats y_prepared y_pow y_scaled z_ready zt_turned zt_hi zt_lo
         x_res_ready res_part res_ready f_done act_hi_ready act_f_ready act_lo_ready act_used
         u_ready u_stats u_prepared u_scaled out_step out_ready""".split())

        def sem_pair(name):
            return [sem(f"{name}_{i}") for i in range(2)]
        gathered, msg_stored, msg_loaded, line_c_in, agg_stored, x_in, rec_in, stored = (
            sem_pair(n) for n in ("gathered", "msg_stored", "msg_loaded", "line_c_in", "agg_stored",
                                  "x_in", "rec_in", "stored"))

        def wide(a, dims):
            return a.to_broadcast(dims)

        def edges_done(eng):
            for i in range(2):
                eng.wait_ge(agg_stored[i], 16 * NPAIR)
            eng.wait_ge(rows_stored, 16 * NCH)

        def front_stats(eng, f):
            wait_count(eng, x_scaled, f.n - 1)
            for t in range(TG):
                eng.bn_stats(stat[:, t, :], xb[:, f.par, t, :]).then_inc(stat_step, 1)
            eng.wait_ge(stat_step, TG * f.n + TG)
            eng.sem_inc(dve_gate, 1)
            for t in range(TG):
                eng.bn_aggr(mv[:, f.par, t, :], stat[:, t, :]).then_inc(x_stats, 1)
            eng.wait_ge(x_stats, TG * f.n + TG)
            eng.tensor_scalar(vareps[:, f.par, :], mv[:, f.par, :, 1], EPS, None, ALU.add).then_inc(x_prepared, 1)
            eng.tensor_scalar(minus_mean[:, f.par, :], mv[:, f.par, :, 0], -1.0, None,
                              ALU.mult).then_inc(x_prepared, 1)

        def front_rstd(eng, f):
            eng.wait_ge(x_prepared, 2 * f.n + 2)
            wait_count(eng, h_ready, TG * (f.n - 1))
            eng.tensor_tensor(rstd[:, f.par, :], vareps[:, f.par, :], minus_half[:, :], ALU.pow).then_inc(x_pow, 1)
            eng.wait_ge(x_pow, f.n + 1)
            eng.tensor_tensor(shift[:, f.par, :], minus_mean[:, f.par, :], rstd[:, f.par, :],
                              ALU.mult).then_inc(x_scaled, 1)

        def front_relu(eng, f):
            eng.wait_ge(x_scaled, f.n + 1)
            wait_count(eng, xt_turned, KC * (f.n - 1))
            for t in range(TG):
                eng.activation(h[:, f.par, t, :], xb[:, f.par, t, :], ACT.Relu,
                               bias=shift[:, f.par, t:t + 1], scale=rstd[:, f.par, t:t + 1]).then_inc(h_ready, 1)

        def front_turn(eng, f):
            eng.wait_ge(h_ready, TG * f.n + TG)
            wait_count(eng, xt_lo, KC * f.n)
            for k in range(KC):
                for t in range(TG):
                    ins = eng.transpose(ps_t[:, k, t * P:(t + 1) * P], h[:, f.par, t, k * P:(k + 1) * P],
                                        ident[:, :])
                ins.then_inc(xt_turned, 1)

        def front_hi(eng, f):
            wait_count(eng, xs_done, TG * f.n)
            for k in range(KC):
                eng.wait_ge(xt_turned, KC * f.n + k + 1)
                eng.copy(xt[0][:, k, :], ps_t[:, k, :]).then_inc(xt_hi, 1)

        def front_lo(eng, f):
            wait_count(eng, xs_done, TG * f.n)
            for k in range(KC):
                eng.wait_ge(xt_hi, KC * f.n + k + 1)
                eng.tensor_tensor(xt[1][:, k, :], ps_t[:, k, :], xt[0][:, k, :].bitcast(F32),
                                  ALU.subtract).then_inc(xt_lo, 1)

        def front_project(eng, f, t, c0, c1):
            if t == 0:
                eng.wait_ge(xt_lo, KC * f.n + KC)
            wait_count(eng, xs_out, TG * f.n + t - 1)
            n = 0
            for k in range(KC):
                for a, b in ((0, 0), (0, 1), (1, 0)):
                    ins = eng.matmul(ps_x[:, t % 2, c0:c1], xt[a][:, k, t * P:(t + 1) * P],
                                     proj[b][:, k, c0:c1], start=(n == 0), stop=(n == 3 * KC - 1))
                    n += 1
            ins.then_inc(xs_done, 1)

        PAIR_LOOP = (2, max(2, 2 * ((NPAIR - 2) // 2)))
        NODE_LOOP = (2, max(2, 2 * ((NG - 3) // 2)))

        block = ctx.enter_context(nc.Block())

        @block.sync
        def _(sp):
            sp.dma_start(w_src, w_src_t.rearrange("(k p) n -> p k n", p=P)).then_inc(weights_in, 16)
            sp.dma_start(w_dst, w_dst_t.rearrange("(k p) n -> p k n", p=P)).then_inc(weights_in, 16)
            for n, a in enumerate((att_src[0:1], att_src[1:2], att_dst[0:1], att_dst[1:2])):
                sp.dma_start(att[:, n, :], a.to_broadcast([P, D])).then_inc(weights_in, 16)
            sp.dma_start(src_i, src_cols).then_inc(cols_in, 16)
            sp.dma_start(dst_i, dst_cols).then_inc(cols_in, 16)
            sp.dma_start(next_i, next_cols).then_inc(cols_in, 16)
            sp.dma_start(type_i, type_cols).then_inc(cols_in, 16)
            sp.dma_start(ew, weight_cols).then_inc(cols_in, 16)
            sp.dma_start(line_row, dst_line).then_inc(line_in, 16)
            sp.dma_start(w1, w1_t.rearrange("(k p) n -> p k n", p=P)).then_inc(rows_in, 16)
            sp.dma_start(w2, w2_t.rearrange("(m p) n -> p m n", p=P)).then_inc(rows_in, 16)
            sp.dma_start(g1_col, g1_cols).then_inc(rows_in, 16)
            sp.dma_start(b1_col, b1_cols).then_inc(rows_in, 16)
            sp.dma_start(hidden_bias[:, :], ffn_b1_cols).then_inc(rows_in, 16)
            for n, a in enumerate((bias, g1, b1, g2, b2, ffn_b2)):
                sp.dma_start(rows[:, n, :], a.to_broadcast([P, D])).then_inc(rows_in, 16)

            sp.wait_ge(empty_set, 4)
            sp.dma_start(sums[EMPTY:EMPTY + P, :], empty).then_inc(empty_stored, 16)
            sp.dma_start(row_of[0:NROWS, :].rearrange("(p t) o -> p (t o)", p=P), node_rows[:, :]).then_inc(rows_cleared, 16)

            def pair(j):
                if not j.exists(NPAIR):
                    return
                sp.wait_ge(xs_out, TG * j.n + 2)
                sp.dma_start(msgs.rearrange("(j c p) d -> j p c d", p=P, c=2)[bass.ds(j.n, 1)].rearrange("o p c d -> (o p) c d"),
                             msg_out[:, j.par, :, :]).then_inc(msg_stored[j.par], 16)
            steps(sp, pair, 0, NPAIR, *PAIR_LOOP)

            sp.wait_ge(cand_copied, 2)
            sp.dma_start(cand_line.rearrange("(h c e) -> c h e", h=HEADS, e=P), turn[0:NCH, :, :]).then_inc(cand_out, 16)
            for hd in range(HEADS):
                src = bass.AP(line.tensor, 0, [[BW, BLOCKS], [1, BW + 2]])
                sp.dma_start(line_b[hd * BLOCKS:(hd + 1) * BLOCKS, :], src).then_inc(scan_in, 16)
            sp.wait_ge(cand_out, 16)
            sp.dma_start(scan[:, 0, :], cand_line.rearrange("(p n) -> p n", p=P)).then_inc(scan_in, 16)
            sp.wait_ge(scan_step, SCAN_STEPS)
            sp.dma_start(max_line.rearrange("(p n) -> p n", p=P), scan[:, 1, :]).then_inc(max_out, 16)
            sp.wait_ge(max_out, 16)
            sp.dma_start(turn[0:NCH, :, :], max_line.rearrange("(h c e) -> c h e", h=HEADS, e=P)).then_inc(max_in, 16)

            sp.wait_ge(msg_stored[0], 16 * ((NPAIR + 1) // 2))
            sp.wait_ge(msg_stored[1], 16 * (NPAIR // 2))

            def load_pair(j):
                if not j.exists(NPAIR):
                    return
                wait_count(sp, eq_ready, 4 * (j.n - 1))
                sp.dma_start(line_c[:, j.par, :], line_row[0:1, bass.ds(2 * P * j.n + 1, 2 * P)].to_broadcast([P, 2 * P])).then_inc(line_c_in[j.par], 16)
                wait_count(sp, agg_done, 2 * (j.n - 1))
                sp.dma_start(msg_in[:, 2 * j.par:2 * j.par + 2, :], msgs.rearrange("(j c p) d -> j p c d", p=P, c=2)[bass.ds(j.n, 1)].rearrange("o p c d -> (o p) c d")).then_inc(msg_loaded[j.par], 16)

            def sum_pair(j):
                load_pair(j + 1)
                if j.exists(NPAIR):
                    for c in chunks(j):
                        sp.wait_ge(agg_out, c.n + 1)
                        sp.wait_ge(agg_max, c.n + 1)
                        sp.dma_start(sums[0:EP].rearrange("(c p) d -> c p d", p=P)[bass.ds(c.n, 1)].rearrange("o p d -> (o p) d"),
                                     agg[:, c.par, :]).then_inc(agg_stored[c.par], 16)
            steps(sp, sum_pair, -1, NPAIR, *PAIR_LOOP)

            def load_nodes(g):
                if not g.exists(NG):
                    return
                f = g + NPAIR
                wait_count(sp, h_ready, TG * (f.n - 1))
                sp.sem_inc(sp_gate, 1)
                wait_count(sp, x_res_ready, g.n - 1)
                sp.dma_start(xb[:, f.par, :, :], x_tiles[:, bass.ds(TG * g.n, TG), :]).then_inc(x_in[g.par], 16)

            def nodes(i):
                load_nodes(i + 3)
                o = i - 1
                if o.exists(NG):
                    sp.wait_ge(out_ready, o.n + 1)
                    sp.dma_start(out_tiles[:, bass.ds(TG * o.n, TG), :], ob[:, o.par, :, :]).then_inc(stored[o.par], 16)
            sp.wait_ge(node_rows_in, 16)
            steps(sp, nodes, -3, NG + 1, *NODE_LOOP)
            sp.wait_ge(stored[0], 16 * ((NG + 1) // 2))
            if NG > 1:
                sp.wait_ge(stored[1], 16 * (NG // 2))

        @block.gpsimd
        def _(pool):
            pool.memset(ident[:, :], 0.0).then_inc(consts, 1)
            pool.memset(ones[:, :], 1.0).then_inc(consts, 1)
            pool.memset(minus_half[:, :], -0.5).then_inc(consts, 1)
            pool.memset(node_rows[:, :], EMPTY).then_inc(empty_set, 1)
            pool.memset(empty[:, 0:SUM], 0.0).then_inc(empty_set, 1)
            pool.memset(empty[:, SUM:REC], -BIG).then_inc(empty_set, 1)
            pool.memset(agg[:, 1, :], 0.0).then_inc(empty_set, 1)
            pool.memset(on_last, 0.0).then_inc(consts, 1)
            pool.iota(place_i, pattern=[[P, NCH]], base=0, channel_multiplier=1).then_inc(consts, 1)
            pool.iota(flag_i, pattern=[[1, 1]], base=NROWS, channel_multiplier=1).then_inc(consts, 1)
            pool.memset(dst_f[:, 0:1], -5.0).then_inc(consts, 1)
            pool.wait_ge(consts, 7)
            pool.affine_select(out=ident[:, :], in_=ident[:, :], compare_op=ALU.not_equal, fill=1.0, base=0,
                               pattern=[[-1, P]], channel_multiplier=1).then_inc(consts, 1)
            pool.affine_select(out=on_last, in_=on_last, compare_op=ALU.not_equal, fill=1.0, base=-(P - 1),
                               pattern=[[0, 1]], channel_multiplier=1).then_inc(consts, 1)

            pool.wait_ge(flag_done, 1)
            pool.wait_ge(line_in, 16)
            pool.wait_ge(cols_in, 16 * 5)
            disorder = pool.value_load(flag_i[0:1, 0:1], min_val=0, max_val=EP)
            with pool.If(disorder > 0):
                pool.wait_ge(weights_split, SPLITS)
                pool.dma_start(all_dst, line_row[0:1, 1:EP + 1].to_broadcast([P, EP])).then_inc(all_in, 16)
                pool.iota(all_num, pattern=[[1, BW]], base=0, channel_multiplier=0).then_inc(num_ready, 1)
                pool.wait_ge(ranked, 2)
                pool.wait_ge(all_in, 16)
                pool.wait_ge(num_ready, 1)
                with pool.Fori(0, NCH) as c:
                    for n, a in enumerate((rank_i, rank1_i, src_i, dst_i, type_i, ew.bitcast(I32))):
                        pool.tensor_copy(moved[:, n:n + 1], a[:, bass.ds(c, 1)]).then_inc(moved_copied, 1)
                    pool.wait_ge(moved_copied, 6 * c + 6)
                    pool.sem_inc(pool_gate, 1)
                    for to, at, n in ((s_src, 0, 2), (line, 1, 3), (s_type, 0, 4), (s_weight, 0, 5)):
                        pool.indirect_dma_start(to, bass.IndirectOffsetOnAxis(ap=moved[:, at:at + 1], axis=0),
                                                moved[:, n:n + 1], None).then_inc(sorted_out, 16)
                    pool.wait_ge(sorted_out, 64 * c + 64)
                    pool.sem_inc(pool_gate, 1)
                for to, of in ((src_i, s_src), (dst_i, line[1:EP + 1]), (next_i, line[2:EP + 2]), (type_i, s_type),
                               (ew.bitcast(I32), s_weight)):
                    pool.dma_start(to, of.rearrange("(c p) o -> p (c o)", p=P), allow_slow_non_contiguous=True).then_inc(sorted_in, 16)
                pool.wait_ge(sorted_in, 16 * 5)
            pool.memset(flag_f, 0.0).then_inc(in_order, 1)

            def gather(j):
                if not j.exists(NPAIR):
                    return
                wait_count(pool, gathered[j.par], 64 * j.half)
                pool.sem_inc(pool_gate, 1)
                pool.tensor_copy(idx[:, j.par, 0:2], src_i[:, bass.ds(2 * j.n, 2)]).then_inc(idx_copied, 1)
                pool.tensor_copy(idx[:, j.par, 2:4], dst_i[:, bass.ds(2 * j.n, 2)]).then_inc(idx_copied, 1)
                pool.wait_ge(idx_copied, 2 * j.n + 2)
                for t in range(TG):
                    wait_count(pool, h_ready, TG * (j.n - 2) + t + 1)
                    pool.sem_inc(pool_gate, 1)
                    pool.indirect_dma_start(xb[:, j.par, t, :], None, x,
                                            bass.IndirectOffsetOnAxis(ap=idx[:, j.par, t:t + 1], axis=0)).then_inc(gathered[j.par], 16)

            def place(c, n):
                wait_count(pool, rows_stored, 16 * n)
                pool.sem_inc(pool_gate, 1)
                pool.tensor_copy(slot[:, 0, 0:1], target_i[:, bass.ds(c, 1)]).then_inc(slot_ready, 1)
                pool.tensor_copy(slot[:, 0, 1:2], place_i[:, bass.ds(c, 1)]).then_inc(slot_ready, 1)
                pool.wait_ge(slot_ready, 2 * n + 2)
                pool.sem_inc(pool_gate, 1)
                pool.indirect_dma_start(row_of, bass.IndirectOffsetOnAxis(ap=slot[:, 0, 0:1], axis=0),
                                        slot[:, 0, 1:2], None).then_inc(rows_stored, 16)

            def pair(j):
                if (j + 1).exists(NPAIR):
                    front_rstd(pool, j + 1)
                gather(j + 2)
                if j.exists(NPAIR):
                    place(j.n, j.n)
            pool.wait_ge(in_order, 1)
            pool.wait_ge(target_ready, 1)
            pool.wait_ge(rows_cleared, 16)
            steps(pool, pair, -2, NPAIR, *PAIR_LOOP)
            steps(pool, lambda j: place(j.n + NPAIR, j.n + NPAIR), 0, NPAIR, *PAIR_LOOP)
            edges_done(pool)
            pool.wait_ge(empty_stored, 16)
            pool.dma_start(node_rows[:, :], row_of[0:NROWS, :].rearrange("(p t) o -> p (t o)", p=P)).then_inc(node_rows_in, 16)
            pool.wait_ge(node_rows_in, 16)

            def gather_records(g):
                if not g.exists(NG):
                    return
                wait_count(pool, rec_in[g.par], 64 * g.half)
                wait_count(pool, hb_ready, g.n - 1)
                pool.sem_inc(pool_gate, 1)
                pool.tensor_copy(idx[:, g.par, :], node_rows[:, bass.ds(TG * g.n, TG)]).then_inc(idx_copied, 1)
                pool.wait_ge(idx_copied, 2 * NPAIR + g.n + 1)
                pool.sem_inc(pool_gate, 1)
                for t in range(TG):
                    pool.indirect_dma_start(rec[:, g.par, t, :], None, sums,
                                            bass.IndirectOffsetOnAxis(ap=idx[:, g.par, t:t + 1], axis=0)).then_inc(rec_in[g.par], 16)

            def nodes(i):
                o, n, a = i - 1, i + 1, i + 2
                if n.exists(NG):
                    wait_count(pool, y_ready, n.n)
                    pool.wait_ge(h_ready, TG * (n + NPAIR).n + TG)
                    pool.tensor_tensor(hb, h[:, (n + NPAIR).par, :, :], wide(rows[:, 0:1, :], [P, TG, D]), ALU.add).then_inc(hb_made, 1)
                if a.exists(NG):
                    front_rstd(pool, a + NPAIR)
                if n.exists(NG):
                    pool.wait_ge(coef_ready, n.n + 1)
                    for t in range(TG):
                        r = rec[:, n.par, t, 0:D].rearrange("p (h c) -> p h c", h=HEADS)
                        ins = pool.tensor_tensor(r, r, coef[:, t, 0:HEADS].rearrange("p (h o) -> p h o", o=1).to_broadcast([P, HEADS, C]), ALU.mult)
                    ins.then_inc(y_scaled_part, 1)
                    pool.wait_ge(y_scaled_part, n.n + 1)
                    pool.wait_ge(hb_made, n.n + 1)
                    pool.tensor_tensor(hb, hb, rec[:, n.par, :, 0:D], ALU.add).then_inc(hb_ready, 1)
                gather_records(i + 3)
                if n.exists(NG):
                    pool.wait_ge(y_prepared, 2 * n.n + 2)
                    wait_count(pool, z_ready, n.n)
                    pool.tensor_tensor(y_rstd, y_var, minus_half[:, :], ALU.pow).then_inc(y_pow, 1)
                    pool.wait_ge(y_pow, n.n + 1)
                    pool.tensor_tensor(y_shift, y_mm, y_rstd, ALU.mult).then_inc(y_scaled, 1)
                if o.exists(NG):
                    pool.wait_ge(u_prepared, o.n + 1)
                    pool.tensor_tensor(u_rstd, u_var, minus_half[:, :], ALU.pow).then_inc(u_scaled, 1)
                if n.exists(NG):
                    pool.wait_ge(z_ready, n.n + 1)
                    wait_count(pool, u_ready, n.n - 1)
                    pool.tensor_tensor(res[:, n.par], z, wide(rows[:, 1:2, :], [P, TG, D]), ALU.mult).then_inc(res_part, 1)
                    wait_count(pool, out_ready, n.n - 1)
                    pool.tensor_tensor(x_res[:, n.par], xb[:, (n + NPAIR).par, :, :], wide(rows[:, 4:5, :], [P, TG, D]), ALU.add).then_inc(x_res_ready, 1)
                    pool.wait_ge(res_part, n.n + 1)
                    pool.tensor_tensor(res[:, n.par], res[:, n.par], wide(rows[:, 2:3, :], [P, TG, D]), ALU.add).then_inc(res_ready, 1)
            steps(pool, nodes, -3, NG + 1, *NODE_LOOP)

        @block.scalar
        def _(act):
            act.wait_ge(weights_in, 16 * 6)
            act.wait_ge(setup_step, SCORE_STEPS)
            for k in range(KC):
                act.copy(proj[0][:, k, 0:D], w_src[:, k, :]).then_inc(proj_hi_ready, 1)
                act.copy(proj[0][:, k, D:WV], proj_f[:, k, :]).then_inc(proj_hi_ready, 1)
            act.wait_ge(setup_step, SCORE_STEPS + KC + 1)
            for k in range(KC):
                act.copy(ffn1[0][:, k, :], w1[:, k, :]).then_inc(proj_hi_ready, 1)
            act.copy(ffn2[0][:, :, :], w2).then_inc(proj_hi_ready, 1)

            def pair(j):
                if j.exists(NPAIR):
                    front_hi(act, j)
                if (j + 1).exists(NPAIR):
                    front_relu(act, j + 1)
                if j.exists(NPAIR):
                    for t in range(TG):
                        act.wait_ge(xs_done, TG * j.n + t + 1)
                        if t < 2:
                            wait_count(act, msg_stored[j.par], 16 * j.half)
                            act.copy(msg_out[:, j.par, t, :], ps_x[:, t, 0:D])
                            act.copy(src_sc[:, bass.ds(2 * j.n + t, 1), :], ps_x[:, t, D:D + SC].rearrange("p (o s) -> p o s", o=1)).then_inc(xs_out, 1)
                        else:
                            act.sem_inc(act_gate, 1)
                            act.copy(dst_sc[:, bass.ds(2 * j.n + t - 2, 1), :], ps_x[:, t - 2, D:WV].rearrange("p (o s) -> p o s", o=1)).then_inc(xs_out, 1)
            act.wait_ge(cols_ready, 1)
            steps(act, pair, -1, NPAIR, *PAIR_LOOP)

            for k in range(2):
                act.wait_ge(cand_turned, k + 1)
                act.copy(turn[0:NCH, 4 * k:4 * k + 4, :], ps_t[0:NCH, k, :].rearrange("p (h e) -> p h e", h=4)).then_inc(cand_copied, 1)
            act.wait_ge(diff_ready, 1)
            act.activation(prob, alpha, ACT.Exp).then_inc(exp_ready, 1)

            def chunk(c):
                act.wait_ge(agg_done, c.n + 1)
                wait_count(act, agg_stored[c.par], 16 * c.half)
                act.copy(agg[:, c.par, 0:SUM], ps_a[:, c.par, 0:SUM]).then_inc(agg_out, 1)
            act.wait_ge(empty_set, 4)
            steps(act, lambda j: [chunk(c) for c in chunks(j)], 0, NPAIR, *PAIR_LOOP)
            edges_done(act)

            def gelu(i, m):
                n = MF * i.n + m
                act.wait_ge(f_done, n + 1)
                wait_count(act, act_used, n + 1 - AB)
                act.activation(act_hi[:, m % AB, :], ps_f[:, m % 2, :], ACT.Gelu, bias=hidden_bias[:, m:m + 1]).then_inc(act_hi_ready, 1)
                wait_count(act, act_lo_ready, n + 1 - AB)
                act.activation(act_f[:, m % AB, :], ps_f[:, m % 2, :], ACT.Gelu, bias=hidden_bias[:, m:m + 1]).then_inc(act_f_ready, 1)

            def copy_xs(a, t):
                act.wait_ge(xs_done, TG * (a + NPAIR).n + t + 1)
                if t == 0:
                    wait_count(act, y_mul, a.n - 1)
                act.copy(xs[:, a.par, t, :], ps_x[:, t % 2, 0:WV]).then_inc(xs_out, 1)

            def first_norm(n):
                act.wait_ge(y_scaled, n.n + 1)
                wait_count(act, zt_turned, KC * n.n)
                wait_count(act, res_part, n.n)
                for t in range(TG):
                    ins = act.activation(z[:, t, :], y[:, t, :], ACT.Identity, bias=y_shift[:, t:t + 1],
                                         scale=y_rstd[:, t:t + 1])
                ins.then_inc(z_ready, 1)

            def z_hi(n):
                wait_count(act, f_done, MF * (n.n - 1))
                for k in range(KC):
                    act.wait_ge(zt_turned, KC * n.n + k + 1)
                    act.copy(zt[0][:, n.par, k, :], ps_t[:, k, :]).then_inc(zt_hi, 1)

            def nodes(i):
                n, a = i + 1, i + 2
                on, norm, front = i.exists(NG), n.exists(NG), a.exists(NG)
                for m in range(MF):
                    if on:
                        gelu(i, m)
                    if m == 1 and front:
                        wait_count(act, hb_made, a.n - 1)
                        front_relu(act, a + NPAIR)
                    if m == 2 and front:
                        front_hi(act, a + NPAIR)
                    if m == 4 and norm:
                        first_norm(n)
                    if m == 6 and norm:
                        z_hi(n)
                    if m in (5, 6) and front:
                        copy_xs(a, 2 * m - 10)
                        copy_xs(a, 2 * m - 9)
                if front:
                    act.wait_ge(exps_in, a.n + 1)
                    act.activation(expo, expo, ACT.Exp).then_inc(exps_out, 1)
            steps(act, nodes, -2, NG, *NODE_LOOP)

        @block.vector
        def _(dve):
            def link(ins, s, n):
                ins.then_inc(s, 1)
                dve.wait_ge(s, n)

            dve.wait_ge(cols_in, 16 * 5)
            dve.wait_ge(consts, 9)
            link(dve.tensor_copy(trash, flag_i), flag_sum, 1)
            link(dve.tensor_tensor(target_f, dst_i, next_i, ALU.is_gt), flag_sum, 2)
            dve.tensor_reduce(flag_f, target_f, AX, ALU.add).then_inc(flag_sum, 1)
            dve.wait_ge(weights_in, 16 * 6)
            n = 0
            for k in range(KC):
                for v in range(4):
                    w = w_src if v < 2 else w_dst
                    link(dve.tensor_tensor(att_prod, w[:, k, :], att[:, v, :], ALU.mult), setup_step, n + 1)
                    link(dve.tensor_reduce(proj_f[:, k, v * HEADS:(v + 1) * HEADS], att_prod.rearrange("p (h c) -> p h c", h=HEADS),
                                           AX, ALU.add), setup_step, n + 2)
                    n += 2
            dve.wait_ge(flag_pe, 1)
            dve.tensor_copy(flag_i[0:1, :], ps_a[0:1, 0, 0:1]).then_inc(flag_done, 1)
            dve.wait_ge(rows_in, 16 * 11)
            dve.wait_ge(hidden_pe, 1)
            dve.tensor_tensor(hidden_bias[:, :], hidden_bias[:, :], ps_f[:, 0, 0:MF], ALU.add)
            for k in range(KC):
                dve.tensor_scalar(w1[:, k, :], w1[:, k, :], g1_col[:, k:k + 1], None, ALU.mult).then_inc(setup_step, 1)
            dve.tensor_tensor(rows[:, 2, :], rows[:, 2, :], rows[:, 5, :], ALU.add).then_inc(setup_step, 1)
            n = 0
            for k in range(KC):
                for of, c0, c1 in ((w_src[:, k, :], 0, D), (proj_f[:, k, :], D, WV)):
                    n += 1
                    dve.wait_ge(proj_hi_ready, n)
                    dve.tensor_tensor(proj[1][:, k, c0:c1], of, proj[0][:, k, c0:c1].bitcast(F32), ALU.subtract).then_inc(weights_split, 1)
            for k in range(KC):
                n += 1
                dve.wait_ge(proj_hi_ready, n)
                dve.tensor_tensor(ffn1[1][:, k, :], w1[:, k, :], ffn1[0][:, k, :].bitcast(F32), ALU.subtract).then_inc(weights_split, 1)
            dve.wait_ge(proj_hi_ready, n + 1)
            dve.tensor_tensor(ffn2[1][:, :, :], w2, ffn2[0][:, :, :].bitcast(F32), ALU.subtract).then_inc(weights_split, 1)

            link(dve.tensor_copy(dst_f[:, 1:NCH + 1], dst_i), flag_sum, 4)
            disorder = dve.value_load(flag_i[0:1, 0:1], min_val=0, max_val=EP)
            with dve.If(disorder > 0):
                dve.tensor_copy(number_f, place_i).then_inc(rank_step, 1)
                dve.wait_ge(all_in, 16)
                dve.wait_ge(num_ready, 1)
                with dve.Fori(0, NCH) as c:
                    ops = 3 * BLOCKS + 1
                    own, num = dst_f[:, bass.ds(c + 1, 1)], number_f[:, bass.ds(c, 1)]
                    for q in range(BLOCKS):
                        at = slice(q * BW, (q + 1) * BW)
                        dve.wait_ge(rank_step, ops * c + 3 * q + 1)
                        dve.tensor_scalar(cmp_a, all_dst[:, at], own, None, ALU.is_lt, ALU.add,
                                          accum_out=counts[:, 2 * q:2 * q + 1]).then_inc(rank_step, 1)
                        dve.tensor_scalar(cmp_b, all_num, float(q * BW), num, ALU.add, ALU.is_lt).then_inc(rank_step, 1)
                        dve.wait_ge(rank_step, ops * c + 3 * q + 3)
                        dve.scalar_tensor_tensor(out=cmp_a, in0=all_dst[:, at], scalar=own, in1=cmp_b, op0=ALU.is_equal,
                                                 op1=ALU.mult, accum_out=counts[:, 2 * q + 1:2 * q + 2]).then_inc(rank_step, 1)
                    dve.wait_ge(rank_step, ops * c + 3 * BLOCKS + 1)
                    dve.tensor_reduce(rank_f[:, bass.ds(c, 1)], counts, AX, ALU.add).then_inc(rank_step, 1)
                dve.wait_ge(rank_step, (3 * BLOCKS + 1) * NCH + 1)
                dve.tensor_copy(rank_i, rank_f).then_inc(ranked, 1)
                dve.tensor_scalar(rank1_i, rank_f, 1.0, None, ALU.add).then_inc(ranked, 1)
            dve.wait_ge(in_order, 1)
            dve.tensor_copy(dst_f[:, 1:NCH + 1], dst_i).then_inc(target_step, 1)
            dve.tensor_copy(type_1, type_i).then_inc(target_step, 1)
            dve.tensor_tensor(last, dst_i, next_i, ALU.not_equal).then_inc(target_step, 1)
            dve.wait_ge(target_step, 3)
            dve.tensor_scalar(type_0, type_1, -1.0, 1.0, ALU.mult, ALU.add).then_inc(cols_ready, 1)
            link(dve.tensor_scalar(target_f, dst_f[:, 1:NCH + 1], trash, None, ALU.subtract), target_step, 4)
            link(dve.tensor_tensor(target_f, target_f, last, ALU.mult), target_step, 5)
            dve.tensor_scalar(target_i, target_f, trash, None, ALU.add).then_inc(target_ready, 1)

            def pair(j):
                if j.exists(NPAIR):
                    front_lo(dve, j)
                if (j + 2).exists(NPAIR):
                    dve.wait_ge(gathered[j.par], 64 * ((j + 2).half + 1))
                    front_stats(dve, j + 2)
            steps(dve, pair, -2, NPAIR, *PAIR_LOOP)

            dve.wait_ge(xs_out, TG * NPAIR)
            n = 0
            t0, t1 = (wide(a.rearrange("p (c o) -> p c o", o=1), [P, NCH, HEADS]) for a in (type_0, type_1))
            ops = [
                lambda: dve.tensor_tensor(alpha, src_sc[:, :, 0:HEADS], dst_sc[:, :, SC:SC + HEADS], ALU.add),
                lambda: dve.tensor_tensor(soft, src_sc[:, :, HEADS:SC], dst_sc[:, :, SC + HEADS:2 * SC], ALU.add),
                lambda: dve.tensor_tensor(prob, dst_sc[:, :, 0:HEADS], dst_sc[:, :, SC:SC + HEADS], ALU.add),
                lambda: dve.tensor_tensor(alpha, alpha, t0, ALU.mult),
                lambda: dve.tensor_tensor(soft, soft, t1, ALU.mult),
                lambda: dve.scalar_tensor_tensor(out=prob, in0=prob, scalar=0.2, in1=prob, op0=ALU.mult, op1=ALU.max),
                lambda: dve.tensor_tensor(alpha, alpha, soft, ALU.add),
                lambda: dve.scalar_tensor_tensor(out=alpha, in0=alpha, scalar=0.2, in1=alpha, op0=ALU.mult, op1=ALU.max),
            ]
            for op in ops:
                n += 1
                link(op(), alpha_step, n)
            dve.tensor_tensor(cand.rearrange("p h c -> p c h"), alpha, prob, ALU.max).then_inc(cand_ready, 1)

            dve.wait_ge(scan_in, 16 * (HEADS + 1))
            st = [0]

            def step(ins):
                st[0] += 1
                link(ins, scan_step, st[0])
            step(dve.tensor_tensor(resets, line_b[:, 0:BW + 1], line_b[:, 1:BW + 2], ALU.not_equal))
            step(dve.tensor_scalar(resets, resets, -BIG, None, ALU.mult))
            for way in range(2):
                r = resets[:, 0:BW] if way == 0 else resets[:, 1:BW + 1]
                of, to = (scan[:, 0, :], scan[:, 1, :]) if way == 0 else (scan[:, 0, :], scan[:, 1, :])
                flip = (lambda a: a) if way == 0 else (lambda a: a[:, ::-1])
                step(dve.tensor_tensor_scan(flip(to), flip(r), flip(of), -BIG, ALU.add, ALU.max))
                e = BW - 1 if way == 0 else 0
                step(dve.tensor_copy(ends[:, 0:1], to[:, e:e + 1]))
                step(dve.tensor_reduce(ends[:, 1:2], r, AX, ALU.min))
                dve.wait_ge(scan_pe, 2 * way + 1)
                step(dve.tensor_copy(ends_row[0:1, 0:2, :], ps_f[0:1, 0, 0:2 * P].rearrange("p (a b) -> p a b", a=2)))
                step(dve.memset(ends_row[0:1, 2, :], -BIG))
                if way == 0:
                    o, i_ = ends_row[0:1, 2, 1:P], slice(0, P - 1)
                else:
                    o, i_ = ends_row[0:1, 2, 0:P - 1], slice(1, P)
                step(dve.tensor_tensor_scan(flip(o), flip(ends_row[0:1, 1, i_]), flip(ends_row[0:1, 0, i_]), -BIG, ALU.add, ALU.max))
                dve.wait_ge(scan_pe, 2 * way + 2)
                step(dve.tensor_copy(carry, ps_f[:, 1, 0:1]))
                step(dve.tensor_tensor_scan(flip(to), flip(r), flip(of), carry, ALU.add, ALU.max))
                if way == 0:
                    step(dve.tensor_copy(scan[:, 0, :], scan[:, 1, :]))
            assert st[0] == SCAN_STEPS

            dve.wait_ge(max_turned, 2)
            for k in range(2):
                link(dve.tensor_copy(tops[:, 4 * k:4 * k + 4, :], ps_t[:, k, :].rearrange("p (h e) -> p h e", h=4)[:, :, 0:NCH]), alpha_step, n + 1)
                n += 1
            dve.tensor_tensor(alpha, alpha, tops.rearrange("p h c -> p c h"), ALU.subtract).then_inc(diff_ready, 1)
            dve.wait_ge(exp_ready, 1)
            dve.tensor_tensor(soft, prob, wide(ew.rearrange("p (c o) -> p c o", o=1), [P, NCH, HEADS]), ALU.mult).then_inc(soft_ready, 1)
            dve.wait_ge(soft_ready, 1)

            def chunk(j, c):
                q = c.par
                if q == 0:
                    dve.wait_ge(line_c_in[j.par], 16 * (j.half + 1))
                line = line_c[:, j.par, q * P:(q + 1) * P]
                wait_count(dve, agg_done, c.n - 1)
                dve.tensor_scalar(eq[:, q, :], line, dst_f[:, bass.ds(c.n + 1, 1)], None,
                                  ALU.is_equal).then_inc(eq_ready, 1)
                dve.tensor_scalar(eq_carry[:, q, :], line, dst_f[:, bass.ds(c.n, 1)], on_last,
                                  ALU.is_equal, ALU.mult).then_inc(eq_ready, 1)
                if q == 0:
                    dve.wait_ge(msg_loaded[j.par], 16 * (j.half + 1))
                m = msg_in[:, 2 * j.par + q, :].rearrange("p (h c) -> p h c", h=HEADS)
                dve.tensor_tensor(m, m, soft[:, bass.ds(c.n, 1), :].rearrange("p o h -> p (o h)").rearrange("p (h o) -> p h o", o=1).to_broadcast([P, HEADS, C]),
                                  ALU.mult).then_inc(vals_ready, 1)
                wait_count(dve, agg_stored[q], 16 * c.half)
                dve.tensor_copy(agg[:, q, SUM:REC], tops[:, :, bass.ds(c.n, 1)].rearrange("p h o -> p (h o)")).then_inc(agg_max, 1)
            dve.wait_ge(empty_set, 4)
            steps(dve, lambda j: [chunk(j, c) for c in chunks(j)], 0, NPAIR, *PAIR_LOOP)
            edges_done(dve)

            def act_rest(i, m):
                n = MF * i.n + m
                dve.wait_ge(act_f_ready, n + 1)
                wait_count(dve, act_used, n + 1 - AB)
                dve.tensor_tensor(act_lo[:, m % AB, :], act_f[:, m % AB, :], act_hi[:, m % AB, :].bitcast(F32),
                                  ALU.subtract).then_inc(act_lo_ready, 1)

            def logits(n):
                s = AL_STEPS * n.n
                dve.wait_ge(xs_out, TG * (n + NPAIR).n + TG)
                dve.wait_ge(rec_in[n.par], 64 * (n.half + 1))
                dve.tensor_tensor(al, xs[:, n.par, :, D:D + HEADS], xs[:, n.par, :, D + SC:D + SC + HEADS], ALU.add).then_inc(al_step, 1)
                dve.wait_ge(al_step, s + 1)
                dve.scalar_tensor_tensor(out=al, in0=al, scalar=0.2, in1=al, op0=ALU.mult, op1=ALU.max).then_inc(al_step, 1)
                dve.wait_ge(al_step, s + 2)
                dve.tensor_tensor(top, al, rec[:, n.par, :, SUM:REC], ALU.max).then_inc(al_step, 1)
                dve.wait_ge(al_step, s + 3)
                dve.tensor_tensor(expo[:, :, 0:HEADS], rec[:, n.par, :, SUM:REC], top, ALU.subtract).then_inc(al_step, 1)
                dve.tensor_tensor(expo[:, :, HEADS:SC], al, top, ALU.subtract).then_inc(exps_in, 1)

            def coefs(n):
                s = AL_STEPS * n.n + 4
                dve.wait_ge(exps_out, n.n + 1)
                dve.tensor_tensor(den, rec[:, n.par, :, D:SUM], expo[:, :, 0:HEADS], ALU.mult).then_inc(al_step, 1)
                dve.wait_ge(al_step, s + 1)
                dve.tensor_tensor(den, den, expo[:, :, HEADS:SC], ALU.add).then_inc(al_step, 1)
                dve.wait_ge(al_step, s + 2)
                dve.reciprocal(top, den).then_inc(al_step, 1)
                dve.wait_ge(al_step, s + 3)
                wait_count(dve, y_scaled_part, n.n)
                dve.tensor_tensor(coef[:, :, 0:HEADS], expo[:, :, 0:HEADS], top, ALU.mult).then_inc(coef_ready, 1)
                dve.tensor_tensor(coef[:, :, HEADS:SC], expo[:, :, HEADS:SC], top, ALU.mult).then_inc(al_step, 1)

            def self_message(n):
                dve.wait_ge(al_step, AL_STEPS * n.n + 8)
                wait_count(dve, z_ready, n.n)
                for t in range(TG):
                    ins = dve.tensor_tensor(y[:, t, :].rearrange("p (h c) -> p h c", h=HEADS), xs[:, n.par, t, 0:D].rearrange("p (h c) -> p h c", h=HEADS),
                                            coef[:, t, HEADS:SC].rearrange("p (h o) -> p h o", o=1).to_broadcast([P, HEADS, C]), ALU.mult)
                ins.then_inc(y_mul, 1)

            def first_norm(n):
                dve.wait_ge(y_mul, n.n + 1)
                dve.wait_ge(hb_ready, n.n + 1)
                dve.tensor_tensor(y, y, hb, ALU.add).then_inc(y_ready, 1)
                dve.wait_ge(y_ready, n.n + 1)
                for t in range(TG):
                    dve.bn_stats(y_stat[:, t, :], y[:, t, :]).then_inc(y_stats, 1)
                dve.wait_ge(y_stats, 2 * TG * n.n + TG)
                dve.sem_inc(dve_gate, 1)
                for t in range(TG):
                    dve.bn_aggr(y_mv[:, t, :], y_stat[:, t, :]).then_inc(y_stats, 1)
                dve.wait_ge(y_stats, 2 * TG * n.n + 2 * TG)
                wait_count(dve, y_scaled, n.n)
                dve.tensor_scalar(y_var, y_mv[:, :, 1], EPS, None, ALU.add).then_inc(y_prepared, 1)
                dve.tensor_scalar(y_mm, y_mv[:, :, 0], -1.0, None, ALU.mult).then_inc(y_prepared, 1)

            def add_ffn(o):
                dve.wait_ge(act_used, MF * o.n + MF)
                dve.wait_ge(res_ready, o.n + 1)
                wait_count(dve, out_ready, o.n)
                for k in range(2):
                    ins = dve.tensor_tensor(u[:, 2 * k:2 * k + 2, :], ps_a[:, k, :].rearrange("p (t d) -> p t d", t=2),
                                            res[:, o.par, 2 * k:2 * k + 2, :], ALU.add)
                ins.then_inc(u_ready, 1)

            def second_norm(o):
                dve.wait_ge(u_ready, o.n + 1)
                for t in range(TG):
                    dve.bn_stats(u_stat[:, t, :], u[:, t, :]).then_inc(u_stats, 1)
                dve.wait_ge(u_stats, 2 * TG * o.n + TG)
                dve.sem_inc(dve_gate, 1)
                for t in range(TG):
                    dve.bn_aggr(u_mv[:, t, :], u_stat[:, t, :]).then_inc(u_stats, 1)
                dve.wait_ge(u_stats, 2 * TG * o.n + 2 * TG)
                dve.tensor_scalar(u_var, u_mv[:, :, 1], EPS, None, ALU.add).then_inc(u_prepared, 1)

            def finish(o):
                for t in range(TG):
                    dve.scalar_tensor_tensor(out=u[:, t, :], in0=u[:, t, :], scalar=u_mv[:, t, 0:1], in1=rows[:, 3, :],
                                             op0=ALU.subtract, op1=ALU.mult).then_inc(out_step, 1)
                dve.wait_ge(u_scaled, o.n + 1)
                wait_count(dve, stored[o.par], 16 * o.half)
                dve.wait_ge(out_step, TG * o.n + TG)
                dve.wait_ge(x_res_ready, o.n + 1)
                for t in range(TG):
                    ins = dve.scalar_tensor_tensor(out=ob[:, o.par, t, :], in0=u[:, t, :], scalar=u_rstd[:, t:t + 1],
                                                   in1=x_res[:, o.par, t, :], op0=ALU.mult, op1=ALU.add)
                ins.then_inc(out_ready, 1)

            def z_rest(n):
                for k in range(KC):
                    dve.wait_ge(zt_hi, KC * n.n + k + 1)
                    dve.tensor_tensor(zt[1][:, n.par, k, :], ps_t[:, k, :], zt[0][:, n.par, k, :].bitcast(F32),
                                      ALU.subtract).then_inc(zt_lo, 1)

            def nodes(i):
                o, n, a = i - 1, i + 1, i + 2
                back, on, norm, front = o.exists(NG), i.exists(NG), n.exists(NG), a.exists(NG)
                if on:
                    act_rest(i, 0)
                if back:
                    add_ffn(o)
                if norm:
                    self_message(n)
                if on:
                    act_rest(i, 1)
                    act_rest(i, 2)
                if front:
                    front_lo(dve, a + NPAIR)
                if norm:
                    first_norm(n)
                if on:
                    act_rest(i, 3)
                if back:
                    second_norm(o)
                if on:
                    act_rest(i, 4)
                if back:
                    finish(o)
                if on:
                    act_rest(i, 5)
                    act_rest(i, 6)
                if norm:
                    z_rest(n)
                if front:
                    logits(a)
                if on:
                    act_rest(i, 7)
                if front:
                    coefs(a)
                if (i + 3).exists(NG):
                    dve.wait_ge(x_in[(i + 3).par], 16 * ((i + 3).half + 1))
                    front_stats(dve, i + 3 + NPAIR)
            steps(dve, nodes, -3, NG + 1, *NODE_LOOP)

        @block.tensor
        def _(pe):
            pe.wait_ge(consts, 9)
            pe.wait_ge(flag_sum, 3)
            pe.matmul(ps_a[0:1, 0, 0:1], flag_f, ones[:, :], start=True, stop=True).then_inc(flag_pe, 1)
            pe.wait_ge(rows_in, 16 * 11)
            for m in range(MF):
                for k in range(KC):
                    ins = pe.matmul(ps_f[:, 0, m:m + 1], w1[:, k, m * P:(m + 1) * P], b1_col[:, k:k + 1],
                                    start=(k == 0), stop=(k == KC - 1))
            ins.then_inc(hidden_pe, 1)

            def pair(j):
                front_turn(pe, j)
                for t in range(TG):
                    front_project(pe, j, t, 0 if t < 2 else D, D + SC if t < 2 else WV)
            pe.wait_ge(weights_split, SPLITS)
            steps(pe, pair, 0, NPAIR, *PAIR_LOOP)

            pe.wait_ge(cand_ready, 1)
            pe.wait_ge(xt_lo, KC * NPAIR)
            for k in range(2):
                for q in range(4):
                    ins = pe.transpose(ps_t[0:NCH, k, q * P:(q + 1) * P], cand[:, 4 * k + q, :], ident[:, :])
                ins.then_inc(cand_turned, 1)
            for way in range(2):
                pe.wait_ge(scan_step, 5 + way * 9)
                pe.transpose(ps_f[0:1, 0, 0:P], ends[:, 0:1], ident[:, :])
                pe.transpose(ps_f[0:1, 0, P:2 * P], ends[:, 1:2], ident[:, :]).then_inc(scan_pe, 1)
                pe.wait_ge(scan_step, 8 + way * 9)
                pe.transpose(ps_f[:, 1, 0:1], ends_row[0:1, 2, :], ident[0:1, 0:1]).then_inc(scan_pe, 1)
            pe.wait_ge(max_in, 16)
            for k in range(2):
                for q in range(4):
                    ins = pe.transpose(ps_t[:, k, q * P:q * P + NCH], turn[0:NCH, 4 * k + q, :], ident[0:NCH, 0:NCH])
                ins.then_inc(max_turned, 1)

            def chunk(j, c):
                pe.wait_ge(eq_ready, 2 * c.n + 2)
                pe.wait_ge(vals_ready, c.n + 1)
                wait_count(pe, agg_out, c.n - 1)
                to = ps_a[:, c.par, :]
                pe.matmul(to[:, 0:D], eq[:, c.par, :], msg_in[:, 2 * j.par + c.par, :], start=True, stop=False, skip_group_check=True)
                pe.matmul(to[:, D:SUM], eq[:, c.par, :], prob[:, bass.ds(c.n, 1), :].rearrange("p o h -> p (o h)"), start=False, stop=False, skip_group_check=True)
                wait_count(pe, agg_out, c.n)
                pe.matmul(to[:, 0:SUM], eq_carry[:, c.par, :], agg[:, 1 - c.par, 0:SUM], start=False, stop=True, skip_group_check=True).then_inc(agg_done, 1)
            pe.wait_ge(exp_ready, 1)
            pe.wait_ge(empty_set, 4)
            steps(pe, lambda j: [chunk(j, c) for c in chunks(j)], 0, NPAIR, *PAIR_LOOP)

            def ffn1_piece(i, m):
                n = MF * i.n + m
                if m == 0:
                    pe.wait_ge(zt_lo, KC * i.n + KC)
                wait_count(pe, act_f_ready, n - 1)
                j = 0
                for k in range(KC):
                    for a, b in ((0, 0), (0, 1), (1, 0)):
                        ins = pe.matmul(ps_f[:, m % 2, :], ffn1[a][:, k, m * P:(m + 1) * P], zt[b][:, i.par, k, :],
                                        start=(j == 0), stop=(j == 3 * KC - 1))
                        j += 1
                ins.then_inc(f_done, 1)

            def ffn2_piece(i, m):
                n = MF * i.n + m
                if m == 0:
                    wait_count(pe, u_ready, i.n)
                pe.wait_ge(act_hi_ready, n + 1)
                pe.wait_ge(act_lo_ready, n + 1)
                for t in range(TG):
                    cols = slice(t * P, (t + 1) * P)
                    to = ps_a[:, t // 2, (t % 2) * D:(t % 2 + 1) * D]
                    pe.matmul(to, act_hi[:, m % AB, cols], ffn2[0][:, m, :], start=(m == 0 and t % 2 == 0), stop=False, skip_group_check=True)
                    pe.matmul(to, act_hi[:, m % AB, cols], ffn2[1][:, m, :], start=False, stop=False, skip_group_check=True)
                    ins = pe.matmul(to, act_lo[:, m % AB, cols], ffn2[0][:, m, :], start=False, stop=(m == MF - 1), skip_group_check=True)
                ins.then_inc(act_used, 1)

            def turn_z(n, front):
                pe.wait_ge(z_ready, n.n + 1)
                pe.wait_ge(xt_lo, KC * (n + NPAIR + front).n + KC)
                for k in range(KC):
                    for t in range(TG):
                        ins = pe.transpose(ps_t[:, k, t * P:(t + 1) * P], z[:, t, k * P:(k + 1) * P], ident[:, :])
                    ins.then_inc(zt_turned, 1)

            def nodes(i):
                o, n, a = i - 1, i + 1, i + 2
                back, on, norm, front = o.exists(NG), i.exists(NG), n.exists(NG), a.exists(NG)
                for m in range(MF):
                    if on:
                        ffn1_piece(i, m)
                    if m == 6 and norm:
                        turn_z(n, front)
                    if m < LAG and back:
                        ffn2_piece(o, MF - LAG + m)
                    if m >= LAG and on:
                        ffn2_piece(i, m - LAG)
                    if m == 2 and front:
                        wait_count(pe, zt_lo, KC * (a.n - 1))
                        front_turn(pe, a + NPAIR)
                    if m in (5, 6) and front:
                        front_project(pe, a + NPAIR, 2 * m - 10, 0, WV)
                        front_project(pe, a + NPAIR, 2 * m - 9, 0, WV)
            steps(pe, nodes, -2, NG + 1, *NODE_LOOP)


def kernel(x, src, dst, edge_type_2, edge_weight, L0_gnn_W_src, L0_gnn_W_dst, L0_gnn_att_src, L0_gnn_att_dst,
           L0_gnn_bias, L0_gnn_ln1_g, L0_gnn_ln1_b, L0_gnn_ln2_g, L0_gnn_ln2_b, L0_gnn_ffn_W1, L0_gnn_ffn_b1,
           L0_gnn_ffn_W2, L0_gnn_ffn_b2):
    import concourse.bacc as bacc
    from concourse.bass_utils import run_bass_kernel_spmd

    a = {k: np.asarray(v) for k, v in dict(locals()).items()
         if k not in ("bacc", "run_bass_kernel_spmd")}
    n, d = a["x"].shape
    e = a["src"].shape[0]
    rows = -(-(n + 1) // GR) * GR
    ch = -(-e // (2 * P)) * 2
    ep = ch * P

    def padded(v, fill):
        return np.concatenate([v, np.full(ep - e, fill, v.dtype)])

    def columns(v, parts=P):
        return np.ascontiguousarray(v.reshape(-1, parts).T)

    dst_p = padded(a["dst"], n)
    dst_line = np.concatenate([np.full(1, -1, dst_p.dtype), dst_p, np.full(1, n + 1, dst_p.dtype)])
    put = {
        "x": np.concatenate([a["x"], np.zeros((rows - n, d), a["x"].dtype)]),
        "src_cols": columns(padded(a["src"], n)),
        "dst_cols": columns(dst_p),
        "next_cols": columns(dst_line[2:]),
        "type_cols": columns(padded(a["edge_type_2"], 0)),
        "weight_cols": columns(padded(a["edge_weight"], 0)),
        "dst_line": dst_line.reshape(1, -1),
        "w_src_t": np.ascontiguousarray(a["L0_gnn_W_src"].T),
        "w_dst_t": np.ascontiguousarray(a["L0_gnn_W_dst"].T),
        "att_src": a["L0_gnn_att_src"].reshape(2, -1),
        "att_dst": a["L0_gnn_att_dst"].reshape(2, -1),
        "bias": a["L0_gnn_bias"].reshape(1, -1),
        "g1": a["L0_gnn_ln1_g"].reshape(1, -1),
        "b1": a["L0_gnn_ln1_b"].reshape(1, -1),
        "g2": a["L0_gnn_ln2_g"].reshape(1, -1),
        "b2": a["L0_gnn_ln2_b"].reshape(1, -1),
        "g1_cols": columns(a["L0_gnn_ln1_g"]),
        "b1_cols": columns(a["L0_gnn_ln1_b"]),
        "w1_t": np.ascontiguousarray(a["L0_gnn_ffn_W1"].T),
        "ffn_b1_cols": columns(a["L0_gnn_ffn_b1"]),
        "w2_t": np.ascontiguousarray(a["L0_gnn_ffn_W2"].T),
        "ffn_b2": a["L0_gnn_ffn_b2"].reshape(1, -1),
    }
    nc = bacc.Bacc("TRN2", target_bir_lowering=False, num_devices=1)
    args = {k: nc.dram_tensor(f"in_{k}", v.shape, mybir.dt.from_np(v.dtype), kind="ExternalInput").ap()
            for k, v in put.items()}
    out = nc.dram_tensor("out_0", (rows, d), F32, kind="ExternalOutput").ap()
    build(nc, out=out, **args)
    r = run_bass_kernel_spmd(nc, [{f"in_{k}": v for k, v in put.items()}], core_ids=[0])
    return r.results[0]["out_0"][:n]
```

```python
from contextlib import ExitStack

import numpy as np

import concourse.bass as bass
from concourse import mybir

F32 = mybir.dt.float32
F32R = mybir.dt.float32r
I32 = mybir.dt.int32
ALU = mybir.AluOpType
ACT = mybir.ActivationFunctionType
AX = mybir.AxisListType.X

P = 128
TG = 4
GR = TG * P
HEADS = 8
BLOCKS = P // HEADS
EPS = 1e-5
BIG = 1e30


class Step:

    def __init__(self, k, off, turn=2):
        self.k, self.off, self.turn = k, off, turn

    def __add__(self, d):
        return Step(self.k, self.off + d, self.turn)

    def __sub__(self, d):
        return Step(self.k, self.off - d, self.turn)

    @property
    def n(self):
        return self.turn * self.k + self.off

    def before(self, bufs):
        return (self.turn // bufs) * self.k + self.off // bufs

    @property
    def half(self):
        return self.before(2)

    @property
    def par(self):
        return self.off % 2

    def exists(self, count):
        return not isinstance(self.n, int) or 0 <= self.n < count


def chunks(j):
    return [Step(j.k, 2 * j.off + q, 2 * j.turn) for q in range(2)]


def wait_count(eng, sem, count):
    if not (isinstance(count, int) and count <= 0):
        eng.wait_ge(sem, count)


AB = 4
LAG = 2
XB = 4
RB = 4
SB = 4
SPLITS = 7
SCORE_STEPS = 16
SCAN_STEPS = 19
AL_STEPS = 8


def steps(eng, body, first, last, lo, hi, turn=2):
    for s in range(first, lo):
        body(Step(0, s, turn))
    if hi > lo:
        with eng.Fori(lo // turn, hi // turn) as k:
            for s in range(turn):
                body(Step(k, s, turn))
    for s in range(max(lo, hi), last):
        body(Step(0, s, turn))


def build(nc, x, ends_cols, next_cols, type_cols, weight_cols, dst_line, w_src_t, w_dst_t,
          att_src, att_dst, bias, g1, b1, g2, b2, g1_cols, b1_cols, w1_t, ffn_b1_cols, w2_t, ffn_b2, out):
    NROWS, D = x.shape
    NT = NROWS // P
    NG = NT // TG
    NCH = next_cols.shape[1]
    EP = NCH * P
    BW = EP // BLOCKS
    NPAIR = NCH // 2
    C = D // HEADS
    KC = D // P
    F = w1_t.shape[1]
    MF = F // P
    SC = 2 * HEADS
    WV = D + 2 * SC
    REC = D + 2 * HEADS
    SUM = D + HEADS
    EMPTY = EP
    assert D == KC * P and NT % TG == 0 and NCH % 2 == 0 and NCH <= P and EP % BLOCKS == 0

    sums = nc.dram_tensor("sums", (EP + P, REC), F32, kind="Internal").ap()
    row_of = [nc.dram_tensor(f"row_of_{i}", (NROWS + P, 1), I32, kind="Internal").ap() for i in range(RB)]
    msgs = nc.dram_tensor("msgs", (EP, D), F32, kind="Internal").ap()
    cand_line = nc.dram_tensor("cand_line", (HEADS * EP,), F32, kind="Internal").ap()
    max_line = nc.dram_tensor("max_line", (HEADS * EP,), F32, kind="Internal").ap()
    line = nc.dram_tensor("line", (EP + 2, 1), I32, kind="Internal").ap()
    s_src = nc.dram_tensor("s_src", (EP, 1), I32, kind="Internal").ap()
    s_type = nc.dram_tensor("s_type", (EP, 1), I32, kind="Internal").ap()
    s_weight = nc.dram_tensor("s_weight", (EP, 1), I32, kind="Internal").ap()

    x_tiles = x.rearrange("(p t) d -> p t d", p=P)
    out_tiles = out.rearrange("(p t) d -> p t d", p=P)
    line_row = line.rearrange("e o -> o e")

    with ExitStack() as ctx:
        def sb(name, shape, dt=F32):
            return ctx.enter_context(nc.sbuf_tensor(name, shape, dt))

        def sem(name):
            return ctx.enter_context(nc.semaphore(name))

        proj = [sb(f"proj_{n}", [P, KC, WV], F32R) for n in ("hi", "lo")]
        ffn1 = [sb(f"ffn1_{n}", [P, KC, F], F32R) for n in ("hi", "lo")]
        ffn2 = [sb(f"ffn2_{n}", [P, MF, D], F32R) for n in ("hi", "lo")]
        ident = sb("ident", [P, P])
        ones = sb("ones", [P, 1])
        rows = sb("rows", [P, 6, D])
        hidden_bias = sb("hidden_bias", [P, MF])
        minus_half = sb("minus_half", [P, TG])
        node_rows = sb("node_rows", [P, NT], I32)
        idx = sb("idx", [P, XB, TG], I32)
        slot = sb("slot", [P, RB, 2], I32)
        xt = [sb(f"xt_{n}", [P, KC, GR], F32R) for n in ("hi", "lo")]
        zt = [sb(f"zt_{n}", [P, 2, KC, GR], F32R) for n in ("hi", "lo")]
        act_hi = sb("act_hi", [P, AB, GR], F32R)
        act_lo = sb("act_lo", [P, AB, GR], F32R)
        xb = sb("xb", [P, XB, TG, D])
        h = sb("h", [P, 2, TG, D])
        stat = sb("stat", [P, TG, 6])
        mv = sb("mv", [P, 2, TG, 2])
        vareps = sb("vareps", [P, 2, TG])
        minus_mean = sb("minus_mean", [P, 2, TG])
        rstd = sb("rstd", [P, 2, TG])
        shift = sb("shift", [P, 2, TG])

        ARENA = max(21000, EP + BW + 13 * NCH + 3 * P + 5 * REC + 64)
        arena = sb("arena", [P, ARENA])
        used = [0]

        def part(dims, dt=None):
            n = int(np.prod(dims))
            a = arena[:, used[0]:used[0] + n]
            used[0] += n
            assert used[0] <= ARENA
            if dt is not None:
                a = a.bitcast(dt)
            if len(dims) == 2:
                a = a.rearrange("p (a b) -> p a b", a=dims[0])
            if len(dims) == 3:
                a = a.rearrange("p (a b c) -> p a b c", a=dims[0], b=dims[1])
            return a

        edge_ends = part([NCH, 2], I32)
        src_i, dst_i = edge_ends[:, :, 0], edge_ends[:, :, 1]
        next_i, type_i = part([NCH], I32), part([NCH], I32)
        ew, type_1, type_0, last = (part([NCH]) for _ in range(4))
        dst_f = part([NCH + 1])
        target_f = part([NCH])
        records = part([NCH, 2], I32)
        target_i, place_i = records[:, :, 0], records[:, :, 1]
        trash, on_last, carry, flag_f = part([1]), part([1]), part([1]), part([1])
        flag_i = part([1], I32)
        ends = part([2])
        ends_row = part([3, P])
        agg = part([4, REC])
        empty = part([REC])
        edges_end = used[0]
        src_sc, dst_sc = part([NCH, SC]), part([NCH, 2 * SC])
        alpha, prob, soft = (part([NCH, HEADS]) for _ in range(3))
        cand, tops = part([HEADS, NCH]), part([HEADS, NCH])
        turn = part([HEADS, P])
        scan = part([2, BW])
        resets = part([BW + 1])
        line_b = part([BW + 2], I32)
        line_c = part([SB, 2 * P], I32)
        eq, eq_carry = part([4, P]), part([4, P])
        msg_out = part([2, 2, D])
        msg_in = part([2 * SB, D])
        used[0] = edges_end
        w_src, w_dst = part([KC, D]), part([KC, D])
        att = part([4, D])
        att_prod = part([D])
        w1, w2 = part([KC, F]), part([MF, D])
        g1_col, b1_col = part([KC]), part([KC])
        proj_f = part([KC, 2 * SC])
        used[0] = edges_end
        all_dst, all_num = part([EP], I32), part([BW], I32)
        cmp_a = xb[:, 0, :, :].rearrange("p t d -> p (t d)")[:, 0:BW]
        cmp_b = xb[:, 1, :, :].rearrange("p t d -> p (t d)")[:, 0:BW]
        counts = h[:, 0, 0, 0:2 * BLOCKS]
        number_f = h[:, 0, 1, 0:NCH]
        rank_f = h[:, 0, 2, 0:NCH]
        rank_i = h[:, 0, 3, 0:NCH].bitcast(I32)
        rank1_i = h[:, 1, 3, 0:NCH].bitcast(I32)
        moved = h[:, 1, 2, 0:6].bitcast(I32)
        used[0] = 0
        xs = part([2, TG * WV]).rearrange("p b (t d) -> p b t d", t=TG)
        rec = part([2, TG * REC]).rearrange("p b (t d) -> p b t d", t=TG)
        x_res = part([2, TG, D])
        y, hb, z = part([TG, D]), part([TG, D]), part([TG, D])
        res = part([2, TG, D])
        u = part([TG, D])
        ob = part([2, TG, D])
        act_f = part([AB, GR])
        y_stat, y_mv = part([TG, 6]), part([TG, 2])
        y_var, y_mm, y_rstd, y_shift = (part([TG]) for _ in range(4))
        u_stat, u_mv = part([TG, 6]), part([TG, 2])
        u_var, u_rstd = part([TG]), part([TG])
        al, top, den = (part([TG, HEADS]) for _ in range(3))
        expo, coef = part([TG, 2 * HEADS]), part([TG, 2 * HEADS])
        other_rows = part([RB - 1, NT], I32)

        def pb(name):
            return ctx.enter_context(nc.psum_tensor(name, [P, 2, 512], F32))
        ps_t, ps_x, ps_f, ps_a = pb("ps_t"), pb("ps_x"), pb("ps_f"), pb("ps_a")

        (weights_in, rows_in, cols_in, consts, setup_step, hidden_pe, proj_hi_ready, weights_split, line_in,
         flag_sum, flag_pe, flag_done, all_in, num_ready, rank_step, ranked, moved_copied, sorted_out, sorted_in, in_order,
         cols_ready, rows_cleared, empty_set, empty_stored, idx_copied, stat_step, x_stats, x_prepared, x_pow, x_scaled,
         h_ready, xt_turned, xt_hi, xt_lo, xs_done, xs_out, alpha_step, cand_ready, cand_turned, cand_copied,
         cand_out, scan_in, scan_step, scan_pe, max_out, max_in, max_turned, diff_ready, exp_ready,
         soft_ready, vals_ready, eq_ready, agg_done, agg_out, agg_max, target_ready, target_step, node_rows_set,
         slot_ready, sp_gate, pool_gate, act_gate, dve_gate, node_rows_in, al_step, exps_in, exps_out, coef_ready, hb_made, hb_ready,
         y_scaled_part, y_mul, y_ready, y_stats, y_prepared, y_pow, y_scaled, z_ready, zt_turned, zt_hi, zt_lo,
         x_res_ready, res_part, res_ready, f_done, act_hi_ready, act_f_ready, act_lo_ready, act_used,
         u_ready, u_stats, u_prepared, u_scaled, out_step, out_ready) = (sem(n) for n in """
         weights_in rows_in cols_in consts setup_step hidden_pe proj_hi_ready weights_split line_in
         flag_sum flag_pe flag_done all_in num_ready rank_step ranked moved_copied sorted_out sorted_in in_order
         cols_ready rows_cleared empty_set empty_stored idx_copied stat_step x_stats x_prepared x_pow x_scaled
         h_ready xt_turned xt_hi xt_lo xs_done xs_out alpha_step cand_ready cand_turned cand_copied
         cand_out scan_in scan_step scan_pe max_out max_in max_turned diff_ready exp_ready
         soft_ready vals_ready eq_ready agg_done agg_out agg_max target_ready target_step node_rows_set
         slot_ready sp_gate pool_gate act_gate dve_gate node_rows_in al_step exps_in exps_out coef_ready hb_made hb_ready
         y_scaled_part y_mul y_ready y_stats y_prepared y_pow y_scaled z_ready zt_turned zt_hi zt_lo
         x_res_ready res_part res_ready f_done act_hi_ready act_f_ready act_lo_ready act_used
         u_ready u_stats u_prepared u_scaled out_step out_ready""".split())

        def sem_pair(name):
            return [sem(f"{name}_{i}") for i in range(2)]
        msg_stored, agg_stored, x_in, rec_in, stored = (
            sem_pair(n) for n in ("msg_stored", "agg_stored",
                                  "x_in", "rec_in", "stored"))
        rows_stored = [sem(f"rows_stored_{i}") for i in range(RB)]
        gathered = [sem(f"gathered_{i}") for i in range(XB)]
        msg_loaded, line_c_in = ([sem(f"{n}_{i}") for i in range(SB)] for n in ("msg_loaded", "line_c_in"))

        def wide(a, dims):
            return a.to_broadcast(dims)

        def edges_done(eng):
            for i in range(2):
                eng.wait_ge(agg_stored[i], 16 * ((NPAIR + 1 - i) // 2))
            for i in range(RB):
                eng.wait_ge(rows_stored[i], 16 * ((NCH + RB - 1 - i) // RB))

        def front_stats(eng, f):
            wait_count(eng, x_scaled, f.n - 1)
            for t in range(TG):
                eng.bn_stats(stat[:, t, :], xb[:, f.off % f.turn, t, :]).then_inc(stat_step, 1)
            eng.wait_ge(stat_step, TG * f.n + TG)
            eng.sem_inc(dve_gate, 1)
            for t in range(TG):
                eng.bn_aggr(mv[:, f.par, t, :], stat[:, t, :]).then_inc(x_stats, 1)
            eng.wait_ge(x_stats, TG * f.n + TG)
            eng.tensor_scalar(vareps[:, f.par, :], mv[:, f.par, :, 1], EPS, None, ALU.add).then_inc(x_prepared, 1)
            eng.tensor_scalar(minus_mean[:, f.par, :], mv[:, f.par, :, 0], -1.0, None,
                              ALU.mult).then_inc(x_prepared, 1)

        def front_rstd(eng, f):
            eng.wait_ge(x_prepared, 2 * f.n + 2)
            wait_count(eng, h_ready, TG * (f.n - 1))
            eng.tensor_tensor(rstd[:, f.par, :], vareps[:, f.par, :], minus_half[:, :], ALU.pow).then_inc(x_pow, 1)
            eng.wait_ge(x_pow, f.n + 1)
            eng.tensor_tensor(shift[:, f.par, :], minus_mean[:, f.par, :], rstd[:, f.par, :],
                              ALU.mult).then_inc(x_scaled, 1)

        def front_relu(eng, f):
            eng.wait_ge(x_scaled, f.n + 1)
            wait_count(eng, xt_turned, KC * (f.n - 1))
            for t in range(TG):
                eng.activation(h[:, f.par, t, :], xb[:, f.off % f.turn, t, :], ACT.Relu,
                               bias=shift[:, f.par, t:t + 1], scale=rstd[:, f.par, t:t + 1]).then_inc(h_ready, 1)

        def front_turn(eng, f):
            eng.wait_ge(h_ready, TG * f.n + TG)
            wait_count(eng, xt_lo, KC * f.n)
            for k in range(KC):
                for t in range(TG):
                    ins = eng.transpose(ps_t[:, k, t * P:(t + 1) * P], h[:, f.par, t, k * P:(k + 1) * P],
                                        ident[:, :])
                ins.then_inc(xt_turned, 1)

        def turned(f, part):
            return zt[part][:, f.par] if f.turn == XB else xt[part]

        def wait_turned_free(eng, f):
            wait_count(eng, xs_done, TG * (f.n - 1 if f.turn == XB else f.n))

        def front_hi(eng, f):
            wait_turned_free(eng, f)
            for k in range(KC):
                eng.wait_ge(xt_turned, KC * f.n + k + 1)
                eng.copy(turned(f, 0)[:, k, :], ps_t[:, k, :]).then_inc(xt_hi, 1)

        def front_lo(eng, f):
            wait_turned_free(eng, f)
            for k in range(KC):
                eng.wait_ge(xt_hi, KC * f.n + k + 1)
                eng.tensor_tensor(turned(f, 1)[:, k, :], ps_t[:, k, :], turned(f, 0)[:, k, :].bitcast(F32),
                                  ALU.subtract).then_inc(xt_lo, 1)

        def front_project(eng, f, t, c0, c1):
            if t == 0:
                eng.wait_ge(xt_lo, KC * f.n + KC)
            wait_count(eng, xs_out, TG * f.n + t - 1)
            n = 0
            for k in range(KC):
                for a, b in ((0, 0), (0, 1), (1, 0)):
                    ins = eng.matmul(ps_x[:, t % 2, c0:c1], turned(f, a)[:, k, t * P:(t + 1) * P],
                                     proj[b][:, k, c0:c1], start=(n == 0), stop=(n == 3 * KC - 1))
                    n += 1
            ins.then_inc(xs_done, 1)

        PAIR_LOOP = (XB, max(XB, XB * ((NPAIR - 4) // XB)), XB)
        SUM_LOOP = (SB, max(SB, SB * ((NPAIR - 3) // SB)), SB)
        NODE_LOOP = (4, max(4, 2 * ((NG - 3) // 2)))

        block = ctx.enter_context(nc.Block())

        @block.sync
        def _(sp):
            sp.dma_start(edge_ends.rearrange("p c o -> p (c o)"), ends_cols).then_inc(cols_in, 16)
            sp.dma_start(next_i, next_cols).then_inc(cols_in, 16)
            sp.dma_start(type_i, type_cols).then_inc(cols_in, 16)
            sp.dma_start(ew, weight_cols).then_inc(cols_in, 16)
            sp.dma_start(line_row, dst_line).then_inc(line_in, 16)
            sp.dma_start(w_src, w_src_t.rearrange("(k p) n -> p k n", p=P)).then_inc(weights_in, 16)
            sp.dma_start(w_dst, w_dst_t.rearrange("(k p) n -> p k n", p=P)).then_inc(weights_in, 16)
            for n, a in enumerate((att_src[0:1], att_src[1:2], att_dst[0:1], att_dst[1:2])):
                sp.dma_start(att[:, n, :], a.to_broadcast([P, D])).then_inc(weights_in, 16)
            sp.dma_start(w1, w1_t.rearrange("(k p) n -> p k n", p=P)).then_inc(rows_in, 16)
            sp.dma_start(w2, w2_t.rearrange("(m p) n -> p m n", p=P)).then_inc(rows_in, 16)
            sp.dma_start(g1_col, g1_cols).then_inc(rows_in, 16)
            sp.dma_start(b1_col, b1_cols).then_inc(rows_in, 16)
            sp.dma_start(hidden_bias[:, :], ffn_b1_cols).then_inc(rows_in, 16)
            for n, a in enumerate((bias, g1, b1, g2, b2, ffn_b2)):
                sp.dma_start(rows[:, n, :], a.to_broadcast([P, D])).then_inc(rows_in, 16)

            sp.wait_ge(empty_set, 4)
            sp.dma_start(sums[EMPTY:EMPTY + P, :], empty).then_inc(empty_stored, 16)
            for i in range(RB):
                sp.dma_start(row_of[i][0:NROWS, :].rearrange("(p t) o -> p (t o)", p=P), node_rows[:, :]).then_inc(rows_cleared, 16)

            def pair(j):
                if not j.exists(NPAIR):
                    return
                sp.wait_ge(xs_out, TG * j.n + 2)
                sp.dma_start(msgs.rearrange("(j c p) d -> j p c d", p=P, c=2)[bass.ds(j.n, 1)].rearrange("o p c d -> (o p) c d"),
                             msg_out[:, j.par, :, :]).then_inc(msg_stored[j.par], 16)
            steps(sp, pair, 0, NPAIR, *PAIR_LOOP)

            sp.wait_ge(cand_copied, 2)
            sp.dma_start(cand_line.rearrange("(h c e) -> c h e", h=HEADS, e=P), turn[0:NCH, :, :]).then_inc(cand_out, 16)
            for hd in range(HEADS):
                src = bass.AP(line.tensor, 0, [[BW, BLOCKS], [1, BW + 2]])
                sp.dma_start(line_b[hd * BLOCKS:(hd + 1) * BLOCKS, :], src).then_inc(scan_in, 16)
            sp.wait_ge(cand_out, 16)
            sp.dma_start(scan[:, 0, :], cand_line.rearrange("(p n) -> p n", p=P)).then_inc(scan_in, 16)
            sp.wait_ge(scan_step, SCAN_STEPS)
            sp.dma_start(max_line.rearrange("(p n) -> p n", p=P), scan[:, 1, :]).then_inc(max_out, 16)
            sp.wait_ge(max_out, 16)
            sp.dma_start(turn[0:NCH, :, :], max_line.rearrange("(h c e) -> c h e", h=HEADS, e=P)).then_inc(max_in, 16)

            sp.wait_ge(msg_stored[0], 16 * ((NPAIR + 1) // 2))
            sp.wait_ge(msg_stored[1], 16 * (NPAIR // 2))

            def load_pair(j):
                if not j.exists(NPAIR):
                    return
                b = j.off % SB
                wait_count(sp, eq_ready, 4 * (j.n + 1 - SB))
                sp.sem_inc(sp_gate, 1)
                sp.dma_start(line_c[:, b, :], line_row[0:1, bass.ds(2 * P * j.n + 1, 2 * P)].to_broadcast([P, 2 * P])).then_inc(line_c_in[b], 16)
                wait_count(sp, agg_done, 2 * (j.n + 1 - SB))
                sp.sem_inc(sp_gate, 1)
                sp.dma_start(msg_in[:, 2 * b:2 * b + 2, :], msgs.rearrange("(j c p) d -> j p c d", p=P, c=2)[bass.ds(j.n, 1)].rearrange("o p c d -> (o p) c d")).then_inc(msg_loaded[b], 16)

            def sum_pair(j):
                load_pair(j + 3)
                if j.exists(NPAIR):
                    sp.wait_ge(agg_out, 2 * j.n + 2)
                    sp.sem_inc(sp_gate, 1)
                    sp.wait_ge(agg_max, j.n + 1)
                    sp.dma_start(sums[0:EP].rearrange("(j c p) d -> j p c d", p=P, c=2)[bass.ds(j.n, 1)].rearrange("o p c d -> (o p) c d"),
                                 agg[:, 2 * j.par:2 * j.par + 2, :]).then_inc(agg_stored[j.par], 16)
            steps(sp, sum_pair, -3, NPAIR, *SUM_LOOP)

            def load_nodes(g):
                if not g.exists(NG):
                    return
                f = g + NPAIR
                wait_count(sp, h_ready, TG * (f.n - 1))
                sp.sem_inc(sp_gate, 1)
                wait_count(sp, x_res_ready, g.n - 1)
                sp.dma_start(xb[:, f.par, :, :], x_tiles[:, bass.ds(TG * g.n, TG), :]).then_inc(x_in[g.par], 16)

            def nodes(i):
                load_nodes(i + 3)
                o = i - 1
                if o.exists(NG):
                    sp.wait_ge(out_ready, o.n + 1)
                    sp.dma_start(out_tiles[:, bass.ds(TG * o.n, TG), :], ob[:, o.par, :, :]).then_inc(stored[o.par], 16)
            sp.wait_ge(node_rows_in, 16 * RB)
            steps(sp, nodes, -3, NG + 1, *NODE_LOOP)
            sp.wait_ge(stored[0], 16 * ((NG + 1) // 2))
            if NG > 1:
                sp.wait_ge(stored[1], 16 * (NG // 2))

        @block.gpsimd
        def _(pool):
            pool.memset(ident[:, :], 0.0).then_inc(consts, 1)
            pool.memset(ones[:, :], 1.0).then_inc(consts, 1)
            pool.memset(minus_half[:, :], -0.5).then_inc(consts, 1)
            pool.memset(node_rows[:, :], EMPTY).then_inc(empty_set, 1)
            pool.memset(empty[:, 0:SUM], 0.0).then_inc(empty_set, 1)
            pool.memset(empty[:, SUM:REC], -BIG).then_inc(empty_set, 1)
            pool.memset(agg[:, 3, :], 0.0).then_inc(empty_set, 1)
            pool.memset(on_last, 0.0).then_inc(consts, 1)
            pool.iota(place_i, pattern=[[P, NCH]], base=0, channel_multiplier=1).then_inc(consts, 1)
            pool.iota(flag_i, pattern=[[1, 1]], base=NROWS, channel_multiplier=1).then_inc(consts, 1)
            pool.memset(dst_f[:, 0:1], -5.0).then_inc(consts, 1)
            pool.wait_ge(consts, 7)
            pool.affine_select(out=ident[:, :], in_=ident[:, :], compare_op=ALU.not_equal, fill=1.0, base=0,
                               pattern=[[-1, P]], channel_multiplier=1).then_inc(consts, 1)
            pool.affine_select(out=on_last, in_=on_last, compare_op=ALU.not_equal, fill=1.0, base=-(P - 1),
                               pattern=[[0, 1]], channel_multiplier=1).then_inc(consts, 1)

            pool.wait_ge(flag_done, 1)
            pool.wait_ge(line_in, 16)
            pool.wait_ge(cols_in, 16 * 4)
            disorder = pool.value_load(flag_i[0:1, 0:1], min_val=0, max_val=EP)
            with pool.If(disorder > 0):
                pool.wait_ge(weights_split, SPLITS)
                pool.dma_start(all_dst, line_row[0:1, 1:EP + 1].to_broadcast([P, EP])).then_inc(all_in, 16)
                pool.iota(all_num, pattern=[[1, BW]], base=0, channel_multiplier=0).then_inc(num_ready, 1)
                pool.wait_ge(ranked, 2)
                pool.wait_ge(all_in, 16)
                pool.wait_ge(num_ready, 1)
                with pool.Fori(0, NCH) as c:
                    for n, a in enumerate((rank_i, rank1_i, src_i, dst_i, type_i, ew.bitcast(I32))):
                        pool.tensor_copy(moved[:, n:n + 1], a[:, bass.ds(c, 1)]).then_inc(moved_copied, 1)
                    pool.wait_ge(moved_copied, 6 * c + 6)
                    pool.sem_inc(pool_gate, 1)
                    for to, at, n in ((s_src, 0, 2), (line, 1, 3), (s_type, 0, 4), (s_weight, 0, 5)):
                        pool.indirect_dma_start(to, bass.IndirectOffsetOnAxis(ap=moved[:, at:at + 1], axis=0),
                                                moved[:, n:n + 1], None).then_inc(sorted_out, 16)
                    pool.wait_ge(sorted_out, 64 * c + 64)
                    pool.sem_inc(pool_gate, 1)
                for to, of in ((src_i, s_src), (dst_i, line[1:EP + 1]), (next_i, line[2:EP + 2]), (type_i, s_type),
                               (ew.bitcast(I32), s_weight)):
                    pool.dma_start(to, of.rearrange("(c p) o -> p (c o)", p=P), allow_slow_non_contiguous=True).then_inc(sorted_in, 16)
                pool.wait_ge(sorted_in, 16 * 5)
            pool.memset(flag_f, 0.0).then_inc(in_order, 1)

            def gather(j):
                if not j.exists(NPAIR):
                    return
                b = j.off % XB
                wait_count(pool, gathered[b], 64 * j.before(XB))
                pool.sem_inc(pool_gate, 1)
                pool.tensor_copy(idx[:, b, :], edge_ends[:, bass.ds(2 * j.n, 2), :].rearrange("p c o -> p (c o)")).then_inc(idx_copied, 1)
                pool.wait_ge(idx_copied, j.n + 1)
                for t in range(TG):
                    wait_count(pool, h_ready, TG * (j.n - XB) + t + 1)
                    pool.sem_inc(pool_gate, 1)
                    at = 2 * (t % 2) + t // 2
                    pool.indirect_dma_start(xb[:, b, t, :], None, x,
                                            bass.IndirectOffsetOnAxis(ap=idx[:, b, at:at + 1], axis=0)).then_inc(gathered[b], 16)

            def place(c):
                b = c.off % RB
                wait_count(pool, rows_stored[b], 16 * c.before(RB))
                pool.sem_inc(pool_gate, 1)
                pool.tensor_copy(slot[:, b, :], records[:, bass.ds(c.n, 1), :].rearrange("p c o -> p (c o)")).then_inc(slot_ready, 1)
                pool.wait_ge(slot_ready, c.n + 1)
                pool.sem_inc(pool_gate, 1)
                pool.indirect_dma_start(row_of[b], bass.IndirectOffsetOnAxis(ap=slot[:, b, 0:1], axis=0),
                                        slot[:, b, 1:2], None).then_inc(rows_stored[b], 16)

            def pair(j):
                gather(j + 4)
                if (j + 2).exists(NPAIR):
                    front_rstd(pool, j + 2)
            pool.wait_ge(in_order, 1)
            steps(pool, pair, -4, NPAIR, *PAIR_LOOP)
            pool.wait_ge(target_ready, 1)
            pool.wait_ge(rows_cleared, 16 * RB)
            steps(pool, place, 0, NCH, RB, max(RB, RB * (NCH // RB)), RB)
            edges_done(pool)
            pool.wait_ge(empty_stored, 16)
            for to, of in zip([node_rows[:, :]] + [other_rows[:, i, :] for i in range(RB - 1)], row_of):
                pool.dma_start(to, of[0:NROWS, :].rearrange("(p t) o -> p (t o)", p=P)).then_inc(node_rows_in, 16)
            pool.wait_ge(node_rows_set, RB - 1)

            def gather_records(g):
                if not g.exists(NG):
                    return
                wait_count(pool, rec_in[g.par], 64 * g.half)
                wait_count(pool, hb_ready, g.n - 1)
                pool.sem_inc(pool_gate, 1)
                pool.tensor_copy(idx[:, g.par, :], node_rows[:, bass.ds(TG * g.n, TG)]).then_inc(idx_copied, 1)
                pool.wait_ge(idx_copied, NPAIR + g.n + 1)
                pool.sem_inc(pool_gate, 1)
                for t in range(TG):
                    pool.indirect_dma_start(rec[:, g.par, t, :], None, sums,
                                            bass.IndirectOffsetOnAxis(ap=idx[:, g.par, t:t + 1], axis=0)).then_inc(rec_in[g.par], 16)

            def nodes(i):
                o, n, a = i - 1, i + 1, i + 2
                if n.exists(NG):
                    wait_count(pool, y_ready, n.n)
                    pool.wait_ge(h_ready, TG * (n + NPAIR).n + TG)
                    pool.tensor_tensor(hb, h[:, (n + NPAIR).par, :, :], wide(rows[:, 0:1, :], [P, TG, D]), ALU.add).then_inc(hb_made, 1)
                if a.exists(NG):
                    front_rstd(pool, a + NPAIR)
                if n.exists(NG):
                    pool.wait_ge(coef_ready, n.n + 1)
                    for t in range(TG):
                        r = rec[:, n.par, t, 0:D].rearrange("p (h c) -> p h c", h=HEADS)
                        ins = pool.tensor_tensor(r, r, coef[:, t, 0:HEADS].rearrange("p (h o) -> p h o", o=1).to_broadcast([P, HEADS, C]), ALU.mult)
                    ins.then_inc(y_scaled_part, 1)
                    pool.wait_ge(y_scaled_part, n.n + 1)
                    pool.wait_ge(hb_made, n.n + 1)
                    pool.tensor_tensor(hb, hb, rec[:, n.par, :, 0:D], ALU.add).then_inc(hb_ready, 1)
                gather_records(i + 3)
                if n.exists(NG):
                    pool.wait_ge(y_prepared, 2 * n.n + 2)
                    wait_count(pool, z_ready, n.n)
                    pool.tensor_tensor(y_rstd, y_var, minus_half[:, :], ALU.pow).then_inc(y_pow, 1)
                    pool.wait_ge(y_pow, n.n + 1)
                    pool.tensor_tensor(y_shift, y_mm, y_rstd, ALU.mult).then_inc(y_scaled, 1)
                if o.exists(NG):
                    pool.wait_ge(u_prepared, o.n + 1)
                    pool.tensor_tensor(u_rstd, u_var, minus_half[:, :], ALU.pow).then_inc(u_scaled, 1)
                if n.exists(NG):
                    pool.wait_ge(z_ready, n.n + 1)
                    wait_count(pool, u_ready, 2 * (n.n - 1))
                    pool.tensor_tensor(res[:, n.par], z, wide(rows[:, 1:2, :], [P, TG, D]), ALU.mult).then_inc(res_part, 1)
                    wait_count(pool, out_ready, n.n - 1)
                    pool.tensor_tensor(x_res[:, n.par], xb[:, (n + NPAIR).par, :, :], wide(rows[:, 4:5, :], [P, TG, D]), ALU.add).then_inc(x_res_ready, 1)
                    pool.wait_ge(res_part, n.n + 1)
                    pool.tensor_tensor(res[:, n.par], res[:, n.par], wide(rows[:, 2:3, :], [P, TG, D]), ALU.add).then_inc(res_ready, 1)
            steps(pool, nodes, -3, NG + 1, *NODE_LOOP)

        @block.scalar
        def _(act):
            act.wait_ge(weights_in, 16 * 6)
            act.wait_ge(setup_step, SCORE_STEPS)
            for k in range(KC):
                act.copy(proj[0][:, k, 0:D], w_src[:, k, :]).then_inc(proj_hi_ready, 1)
                act.copy(proj[0][:, k, D:WV], proj_f[:, k, :]).then_inc(proj_hi_ready, 1)
            act.wait_ge(setup_step, SCORE_STEPS + KC + 1)
            for k in range(KC):
                act.copy(ffn1[0][:, k, :], w1[:, k, :]).then_inc(proj_hi_ready, 1)
            act.copy(ffn2[0][:, :, :], w2).then_inc(proj_hi_ready, 1)

            def pair(j):
                for t in range(TG):
                    if j.exists(NPAIR):
                        act.wait_ge(xs_done, TG * j.n + t + 1)
                        if t < 2:
                            wait_count(act, msg_stored[j.par], 16 * j.half)
                            act.copy(msg_out[:, j.par, t, :], ps_x[:, t, 0:D])
                            act.copy(src_sc[:, bass.ds(2 * j.n + t, 1), :], ps_x[:, t, D:D + SC].rearrange("p (o s) -> p o s", o=1)).then_inc(xs_out, 1)
                        else:
                            act.sem_inc(act_gate, 1)
                            act.copy(dst_sc[:, bass.ds(2 * j.n + t - 2, 1), :], ps_x[:, t - 2, D:WV].rearrange("p (o s) -> p o s", o=1)).then_inc(xs_out, 1)
                    if t == 1 and (j + 1).exists(NPAIR):
                        front_hi(act, j + 1)
                if (j + 2).exists(NPAIR):
                    front_relu(act, j + 2)
            act.wait_ge(cols_ready, 1)
            steps(act, pair, -2, NPAIR, *PAIR_LOOP)

            for k in range(2):
                act.wait_ge(cand_turned, k + 1)
                act.copy(turn[0:NCH, 4 * k:4 * k + 4, :], ps_t[0:NCH, k, :].rearrange("p (h e) -> p h e", h=4)).then_inc(cand_copied, 1)
            act.wait_ge(diff_ready, 1)
            act.activation(prob, alpha, ACT.Exp).then_inc(exp_ready, 1)

            def sum_pair(j):
                wait_count(act, agg_stored[j.par], 16 * j.half)
                for c in chunks(j):
                    act.wait_ge(agg_done, c.n + 1)
                    act.copy(agg[:, 2 * j.par + c.par, 0:SUM], ps_a[:, c.par, 0:SUM]).then_inc(agg_out, 1)
            act.wait_ge(empty_set, 4)
            steps(act, sum_pair, 0, NPAIR, *SUM_LOOP)
            edges_done(act)

            def gelu(i, m):
                n = MF * i.n + m
                act.wait_ge(f_done, n + 1)
                wait_count(act, act_used, n + 1 - AB)
                act.activation(act_hi[:, m % AB, :], ps_f[:, m % 2, :], ACT.Gelu, bias=hidden_bias[:, m:m + 1]).then_inc(act_hi_ready, 1)
                wait_count(act, act_lo_ready, n + 1 - AB)
                act.activation(act_f[:, m % AB, :], ps_f[:, m % 2, :], ACT.Gelu, bias=hidden_bias[:, m:m + 1]).then_inc(act_f_ready, 1)

            def copy_xs(a, t):
                act.wait_ge(xs_done, TG * (a + NPAIR).n + t + 1)
                if t == 0:
                    wait_count(act, y_mul, a.n - 1)
                act.copy(xs[:, a.par, t, :], ps_x[:, t % 2, 0:WV]).then_inc(xs_out, 1)

            def first_norm(n):
                act.wait_ge(y_scaled, n.n + 1)
                wait_count(act, zt_turned, KC * n.n)
                wait_count(act, res_part, n.n)
                for t in range(TG):
                    ins = act.activation(z[:, t, :], y[:, t, :], ACT.Identity, bias=y_shift[:, t:t + 1],
                                         scale=y_rstd[:, t:t + 1])
                ins.then_inc(z_ready, 1)

            def z_hi(n):
                wait_count(act, f_done, MF * (n.n - 1))
                for k in range(KC):
                    act.wait_ge(zt_turned, KC * n.n + k + 1)
                    act.copy(zt[0][:, n.par, k, :], ps_t[:, k, :]).then_inc(zt_hi, 1)

            def nodes(i):
                n, a = i + 1, i + 2
                on, norm, front = i.exists(NG), n.exists(NG), a.exists(NG)
                for m in range(MF):
                    if on:
                        gelu(i, m)
                    if m == 1 and front:
                        wait_count(act, hb_made, a.n - 1)
                        front_relu(act, a + NPAIR)
                    if m == 3 and front:
                        front_hi(act, a + NPAIR)
                    if m == 4 and norm:
                        first_norm(n)
                    if m == 6 and norm:
                        z_hi(n)
                    if m in (5, 6) and front:
                        copy_xs(a, 2 * m - 10)
                        copy_xs(a, 2 * m - 9)
                if front:
                    act.wait_ge(exps_in, a.n + 1)
                    act.activation(expo, expo, ACT.Exp).then_inc(exps_out, 1)
            steps(act, nodes, -2, NG, *NODE_LOOP)

        @block.vector
        def _(dve):
            def link(ins, s, n):
                ins.then_inc(s, 1)
                dve.wait_ge(s, n)

            dve.wait_ge(cols_in, 16 * 4)
            dve.wait_ge(consts, 9)
            link(dve.tensor_copy(trash, flag_i), flag_sum, 1)
            link(dve.tensor_tensor(target_f, dst_i, next_i, ALU.is_gt), flag_sum, 2)
            dve.tensor_reduce(flag_f, target_f, AX, ALU.add).then_inc(flag_sum, 1)
            dve.wait_ge(flag_pe, 1)
            dve.tensor_copy(flag_i[0:1, :], ps_a[0:1, 0, 0:1]).then_inc(flag_done, 1)
            dve.wait_ge(weights_in, 16 * 6)
            n = 0
            for k in range(KC):
                for v in range(4):
                    w = w_src if v < 2 else w_dst
                    link(dve.tensor_tensor(att_prod, w[:, k, :], att[:, v, :], ALU.mult), setup_step, n + 1)
                    link(dve.tensor_reduce(proj_f[:, k, v * HEADS:(v + 1) * HEADS], att_prod.rearrange("p (h c) -> p h c", h=HEADS),
                                           AX, ALU.add), setup_step, n + 2)
                    n += 2
            dve.wait_ge(rows_in, 16 * 11)
            dve.wait_ge(hidden_pe, 1)
            dve.tensor_tensor(hidden_bias[:, :], hidden_bias[:, :], ps_f[:, 0, 0:MF], ALU.add)
            for k in range(KC):
                dve.tensor_scalar(w1[:, k, :], w1[:, k, :], g1_col[:, k:k + 1], None, ALU.mult).then_inc(setup_step, 1)
            dve.tensor_tensor(rows[:, 2, :], rows[:, 2, :], rows[:, 5, :], ALU.add).then_inc(setup_step, 1)
            n = 0
            for k in range(KC):
                for of, c0, c1 in ((w_src[:, k, :], 0, D), (proj_f[:, k, :], D, WV)):
                    n += 1
                    dve.wait_ge(proj_hi_ready, n)
                    dve.tensor_tensor(proj[1][:, k, c0:c1], of, proj[0][:, k, c0:c1].bitcast(F32), ALU.subtract).then_inc(weights_split, 1)
            for k in range(KC):
                n += 1
                dve.wait_ge(proj_hi_ready, n)
                dve.tensor_tensor(ffn1[1][:, k, :], w1[:, k, :], ffn1[0][:, k, :].bitcast(F32), ALU.subtract).then_inc(weights_split, 1)
            dve.wait_ge(proj_hi_ready, n + 1)
            dve.tensor_tensor(ffn2[1][:, :, :], w2, ffn2[0][:, :, :].bitcast(F32), ALU.subtract).then_inc(weights_split, 1)

            link(dve.tensor_copy(dst_f[:, 1:NCH + 1], dst_i), flag_sum, 4)
            disorder = dve.value_load(flag_i[0:1, 0:1], min_val=0, max_val=EP)
            with dve.If(disorder > 0):
                dve.tensor_copy(number_f, place_i).then_inc(rank_step, 1)
                dve.wait_ge(all_in, 16)
                dve.wait_ge(num_ready, 1)
                with dve.Fori(0, NCH) as c:
                    ops = 3 * BLOCKS + 1
                    own, num = dst_f[:, bass.ds(c + 1, 1)], number_f[:, bass.ds(c, 1)]
                    for q in range(BLOCKS):
                        at = slice(q * BW, (q + 1) * BW)
                        dve.wait_ge(rank_step, ops * c + 3 * q + 1)
                        dve.tensor_scalar(cmp_a, all_dst[:, at], own, None, ALU.is_lt, ALU.add,
                                          accum_out=counts[:, 2 * q:2 * q + 1]).then_inc(rank_step, 1)
                        dve.tensor_scalar(cmp_b, all_num, float(q * BW), num, ALU.add, ALU.is_lt).then_inc(rank_step, 1)
                        dve.wait_ge(rank_step, ops * c + 3 * q + 3)
                        dve.scalar_tensor_tensor(out=cmp_a, in0=all_dst[:, at], scalar=own, in1=cmp_b, op0=ALU.is_equal,
                                                 op1=ALU.mult, accum_out=counts[:, 2 * q + 1:2 * q + 2]).then_inc(rank_step, 1)
                    dve.wait_ge(rank_step, ops * c + 3 * BLOCKS + 1)
                    dve.tensor_reduce(rank_f[:, bass.ds(c, 1)], counts, AX, ALU.add).then_inc(rank_step, 1)
                dve.wait_ge(rank_step, (3 * BLOCKS + 1) * NCH + 1)
                dve.tensor_copy(rank_i, rank_f).then_inc(ranked, 1)
                dve.tensor_scalar(rank1_i, rank_f, 1.0, None, ALU.add).then_inc(ranked, 1)
            dve.wait_ge(in_order, 1)
            dve.tensor_copy(dst_f[:, 1:NCH + 1], dst_i).then_inc(target_step, 1)
            dve.tensor_copy(type_1, type_i).then_inc(target_step, 1)
            dve.tensor_tensor(last, dst_i, next_i, ALU.not_equal).then_inc(target_step, 1)
            dve.wait_ge(target_step, 3)
            dve.tensor_scalar(type_0, type_1, -1.0, 1.0, ALU.mult, ALU.add).then_inc(cols_ready, 1)
            link(dve.tensor_scalar(target_f, dst_f[:, 1:NCH + 1], trash, None, ALU.subtract), target_step, 4)
            link(dve.tensor_tensor(target_f, target_f, last, ALU.mult), target_step, 5)
            dve.tensor_scalar(target_i, target_f, trash, None, ALU.add).then_inc(target_ready, 1)

            def pair(j):
                if (j + 1).exists(NPAIR):
                    front_lo(dve, j + 1)
                if (j + 3).exists(NPAIR):
                    dve.wait_ge(gathered[(j + 3).off % XB], 64 * ((j + 3).before(XB) + 1))
                    front_stats(dve, j + 3)
            steps(dve, pair, -3, NPAIR, *PAIR_LOOP)

            dve.wait_ge(xs_out, TG * NPAIR)
            n = 0
            t0, t1 = (wide(a.rearrange("p (c o) -> p c o", o=1), [P, NCH, HEADS]) for a in (type_0, type_1))
            ops = [
                lambda: dve.tensor_tensor(alpha, src_sc[:, :, 0:HEADS], dst_sc[:, :, SC:SC + HEADS], ALU.add),
                lambda: dve.tensor_tensor(soft, src_sc[:, :, HEADS:SC], dst_sc[:, :, SC + HEADS:2 * SC], ALU.add),
                lambda: dve.tensor_tensor(prob, dst_sc[:, :, 0:HEADS], dst_sc[:, :, SC:SC + HEADS], ALU.add),
                lambda: dve.tensor_tensor(alpha, alpha, t0, ALU.mult),
                lambda: dve.tensor_tensor(soft, soft, t1, ALU.mult),
                lambda: dve.scalar_tensor_tensor(out=prob, in0=prob, scalar=0.2, in1=prob, op0=ALU.mult, op1=ALU.max),
                lambda: dve.tensor_tensor(alpha, alpha, soft, ALU.add),
                lambda: dve.scalar_tensor_tensor(out=alpha, in0=alpha, scalar=0.2, in1=alpha, op0=ALU.mult, op1=ALU.max),
            ]
            for op in ops:
                n += 1
                link(op(), alpha_step, n)
            dve.tensor_tensor(cand.rearrange("p h c -> p c h"), alpha, prob, ALU.max).then_inc(cand_ready, 1)

            dve.wait_ge(scan_in, 16 * (HEADS + 1))
            st = [0]

            def step(ins):
                st[0] += 1
                link(ins, scan_step, st[0])
            step(dve.tensor_tensor(resets, line_b[:, 0:BW + 1], line_b[:, 1:BW + 2], ALU.not_equal))
            step(dve.tensor_scalar(resets, resets, -BIG, None, ALU.mult))
            for way in range(2):
                r = resets[:, 0:BW] if way == 0 else resets[:, 1:BW + 1]
                of, to = scan[:, 0, :], scan[:, 1, :]
                flip = (lambda a: a) if way == 0 else (lambda a: a[:, ::-1])
                step(dve.tensor_tensor_scan(flip(to), flip(r), flip(of), -BIG, ALU.add, ALU.max))
                e = BW - 1 if way == 0 else 0
                step(dve.tensor_copy(ends[:, 0:1], to[:, e:e + 1]))
                step(dve.tensor_reduce(ends[:, 1:2], r, AX, ALU.min))
                dve.wait_ge(scan_pe, 2 * way + 1)
                step(dve.tensor_copy(ends_row[0:1, 0:2, :], ps_f[0:1, 0, 0:2 * P].rearrange("p (a b) -> p a b", a=2)))
                step(dve.memset(ends_row[0:1, 2, :], -BIG))
                if way == 0:
                    o, i_ = ends_row[0:1, 2, 1:P], slice(0, P - 1)
                else:
                    o, i_ = ends_row[0:1, 2, 0:P - 1], slice(1, P)
                step(dve.tensor_tensor_scan(flip(o), flip(ends_row[0:1, 1, i_]), flip(ends_row[0:1, 0, i_]), -BIG, ALU.add, ALU.max))
                dve.wait_ge(scan_pe, 2 * way + 2)
                step(dve.tensor_copy(carry, ps_f[:, 1, 0:1]))
                step(dve.tensor_tensor_scan(flip(to), flip(r), flip(of), carry, ALU.add, ALU.max))
                if way == 0:
                    step(dve.tensor_copy(scan[:, 0, :], scan[:, 1, :]))
            assert st[0] == SCAN_STEPS

            dve.wait_ge(max_turned, 2)
            for k in range(2):
                link(dve.tensor_copy(tops[:, 4 * k:4 * k + 4, :], ps_t[:, k, :].rearrange("p (h e) -> p h e", h=4)[:, :, 0:NCH]), alpha_step, n + 1)
                n += 1
            dve.tensor_tensor(alpha, alpha, tops.rearrange("p h c -> p c h"), ALU.subtract).then_inc(diff_ready, 1)
            dve.wait_ge(exp_ready, 1)
            dve.tensor_tensor(soft, prob, wide(ew.rearrange("p (c o) -> p c o", o=1), [P, NCH, HEADS]), ALU.mult).then_inc(soft_ready, 1)
            dve.wait_ge(soft_ready, 1)

            def chunk(j, c):
                q, b, e = c.par, j.off % SB, c.off % 4
                if q == 0:
                    dve.wait_ge(line_c_in[b], 16 * (j.before(SB) + 1))
                line = line_c[:, b, q * P:(q + 1) * P]
                wait_count(dve, agg_done, c.n - 3)
                dve.tensor_scalar(eq[:, e, :], line, dst_f[:, bass.ds(c.n + 1, 1)], None,
                                  ALU.is_equal).then_inc(eq_ready, 1)
                dve.tensor_scalar(eq_carry[:, e, :], line, dst_f[:, bass.ds(c.n, 1)], on_last,
                                  ALU.is_equal, ALU.mult).then_inc(eq_ready, 1)
                if q == 0:
                    dve.wait_ge(msg_loaded[b], 16 * (j.before(SB) + 1))
                m = msg_in[:, 2 * b + q, :].rearrange("p (h c) -> p h c", h=HEADS)
                dve.tensor_tensor(m, m, soft[:, bass.ds(c.n, 1), :].rearrange("p o h -> p (o h)").rearrange("p (h o) -> p h o", o=1).to_broadcast([P, HEADS, C]),
                                  ALU.mult).then_inc(vals_ready, 1)
                if q == 1:
                    wait_count(dve, agg_stored[j.par], 16 * j.half)
                    dve.tensor_copy(agg[:, 2 * j.par:2 * j.par + 2, SUM:REC],
                                    tops[:, :, bass.ds(2 * j.n, 2)].rearrange("p h c -> p c h")).then_inc(agg_max, 1)
            dve.wait_ge(empty_set, 4)
            steps(dve, lambda j: [chunk(j, c) for c in chunks(j)], 0, NPAIR, *SUM_LOOP)
            edges_done(dve)
            dve.wait_ge(node_rows_in, 16 * RB)
            for i in range(RB - 1):
                link(dve.tensor_tensor(node_rows[:, :], node_rows[:, :], other_rows[:, i, :], ALU.min), node_rows_set, i + 1)

            def act_rest(i, m):
                n = MF * i.n + m
                dve.wait_ge(act_f_ready, n + 1)
                wait_count(dve, act_used, n + 1 - AB)
                dve.tensor_tensor(act_lo[:, m % AB, :], act_f[:, m % AB, :], act_hi[:, m % AB, :].bitcast(F32),
                                  ALU.subtract).then_inc(act_lo_ready, 1)

            def logits(n):
                s = AL_STEPS * n.n
                dve.wait_ge(xs_out, TG * (n + NPAIR).n + TG)
                dve.wait_ge(rec_in[n.par], 64 * (n.half + 1))
                dve.tensor_tensor(al, xs[:, n.par, :, D:D + HEADS], xs[:, n.par, :, D + SC:D + SC + HEADS], ALU.add).then_inc(al_step, 1)
                dve.wait_ge(al_step, s + 1)
                dve.scalar_tensor_tensor(out=al, in0=al, scalar=0.2, in1=al, op0=ALU.mult, op1=ALU.max).then_inc(al_step, 1)
                dve.wait_ge(al_step, s + 2)
                dve.tensor_tensor(top, al, rec[:, n.par, :, SUM:REC], ALU.max).then_inc(al_step, 1)
                dve.wait_ge(al_step, s + 3)
                dve.tensor_tensor(expo[:, :, 0:HEADS], rec[:, n.par, :, SUM:REC], top, ALU.subtract).then_inc(al_step, 1)
                dve.tensor_tensor(expo[:, :, HEADS:SC], al, top, ALU.subtract).then_inc(exps_in, 1)

            def coefs(n):
                s = AL_STEPS * n.n + 4
                dve.wait_ge(exps_out, n.n + 1)
                dve.tensor_tensor(den, rec[:, n.par, :, D:SUM], expo[:, :, 0:HEADS], ALU.mult).then_inc(al_step, 1)
                dve.wait_ge(al_step, s + 1)
                dve.tensor_tensor(den, den, expo[:, :, HEADS:SC], ALU.add).then_inc(al_step, 1)
                dve.wait_ge(al_step, s + 2)
                dve.reciprocal(top, den).then_inc(al_step, 1)
                dve.wait_ge(al_step, s + 3)
                wait_count(dve, y_scaled_part, n.n)
                dve.tensor_tensor(coef[:, :, 0:HEADS], expo[:, :, 0:HEADS], top, ALU.mult).then_inc(coef_ready, 1)
                dve.tensor_tensor(coef[:, :, HEADS:SC], expo[:, :, HEADS:SC], top, ALU.mult).then_inc(al_step, 1)

            def self_message(n):
                dve.wait_ge(al_step, AL_STEPS * n.n + 8)
                wait_count(dve, z_ready, n.n)
                for t in range(TG):
                    ins = dve.tensor_tensor(y[:, t, :].rearrange("p (h c) -> p h c", h=HEADS), xs[:, n.par, t, 0:D].rearrange("p (h c) -> p h c", h=HEADS),
                                            coef[:, t, HEADS:SC].rearrange("p (h o) -> p h o", o=1).to_broadcast([P, HEADS, C]), ALU.mult)
                ins.then_inc(y_mul, 1)

            def first_norm(n):
                dve.wait_ge(y_mul, n.n + 1)
                dve.wait_ge(hb_ready, n.n + 1)
                dve.tensor_tensor(y, y, hb, ALU.add).then_inc(y_ready, 1)
                dve.wait_ge(y_ready, n.n + 1)
                for t in range(TG):
                    dve.bn_stats(y_stat[:, t, :], y[:, t, :]).then_inc(y_stats, 1)
                dve.wait_ge(y_stats, 2 * TG * n.n + TG)
                dve.sem_inc(dve_gate, 1)
                for t in range(TG):
                    dve.bn_aggr(y_mv[:, t, :], y_stat[:, t, :]).then_inc(y_stats, 1)
                dve.wait_ge(y_stats, 2 * TG * n.n + 2 * TG)
                wait_count(dve, y_scaled, n.n)
                dve.tensor_scalar(y_var, y_mv[:, :, 1], EPS, None, ALU.add).then_inc(y_prepared, 1)
                dve.tensor_scalar(y_mm, y_mv[:, :, 0], -1.0, None, ALU.mult).then_inc(y_prepared, 1)

            def add_ffn(o):
                dve.wait_ge(act_used, MF * o.n + MF)
                dve.wait_ge(res_ready, o.n + 1)
                wait_count(dve, out_ready, o.n)
                for k in range(2):
                    dve.tensor_tensor(u[:, 2 * k:2 * k + 2, :], ps_a[:, k, :].rearrange("p (t d) -> p t d", t=2),
                                      res[:, o.par, 2 * k:2 * k + 2, :], ALU.add).then_inc(u_ready, 1)

            def second_norm(o):
                dve.wait_ge(u_ready, 2 * o.n + 2)
                for t in range(TG):
                    dve.bn_stats(u_stat[:, t, :], u[:, t, :]).then_inc(u_stats, 1)
                dve.wait_ge(u_stats, 2 * TG * o.n + TG)
                dve.sem_inc(dve_gate, 1)
                for t in range(TG):
                    dve.bn_aggr(u_mv[:, t, :], u_stat[:, t, :]).then_inc(u_stats, 1)
                dve.wait_ge(u_stats, 2 * TG * o.n + 2 * TG)
                dve.tensor_scalar(u_var, u_mv[:, :, 1], EPS, None, ALU.add).then_inc(u_prepared, 1)

            def finish(o):
                for t in range(TG):
                    dve.scalar_tensor_tensor(out=u[:, t, :], in0=u[:, t, :], scalar=u_mv[:, t, 0:1], in1=rows[:, 3, :],
                                             op0=ALU.subtract, op1=ALU.mult).then_inc(out_step, 1)
                dve.wait_ge(u_scaled, o.n + 1)
                wait_count(dve, stored[o.par], 16 * o.half)
                dve.wait_ge(out_step, TG * o.n + TG)
                dve.wait_ge(x_res_ready, o.n + 1)
                for t in range(TG):
                    ins = dve.scalar_tensor_tensor(out=ob[:, o.par, t, :], in0=u[:, t, :], scalar=u_rstd[:, t:t + 1],
                                                   in1=x_res[:, o.par, t, :], op0=ALU.mult, op1=ALU.add)
                ins.then_inc(out_ready, 1)

            def z_rest(n):
                for k in range(KC):
                    dve.wait_ge(zt_hi, KC * n.n + k + 1)
                    dve.tensor_tensor(zt[1][:, n.par, k, :], ps_t[:, k, :], zt[0][:, n.par, k, :].bitcast(F32),
                                      ALU.subtract).then_inc(zt_lo, 1)

            def nodes(i):
                o, n, a = i - 1, i + 1, i + 2
                back, on, norm, front = o.exists(NG), i.exists(NG), n.exists(NG), a.exists(NG)
                if on:
                    act_rest(i, 0)
                if back:
                    add_ffn(o)
                if norm:
                    self_message(n)
                if on:
                    act_rest(i, 1)
                    act_rest(i, 2)
                if norm:
                    first_norm(n)
                if on:
                    act_rest(i, 3)
                if front:
                    front_lo(dve, a + NPAIR)
                if back:
                    second_norm(o)
                if on:
                    act_rest(i, 4)
                if back:
                    finish(o)
                if on:
                    act_rest(i, 5)
                    act_rest(i, 6)
                if norm:
                    z_rest(n)
                if front:
                    logits(a)
                if on:
                    act_rest(i, 7)
                if front:
                    coefs(a)
                if (i + 3).exists(NG):
                    dve.wait_ge(x_in[(i + 3).par], 16 * ((i + 3).half + 1))
                    front_stats(dve, i + 3 + NPAIR)
            steps(dve, nodes, -3, NG + 1, *NODE_LOOP)

        @block.tensor
        def _(pe):
            pe.wait_ge(consts, 9)
            pe.wait_ge(flag_sum, 3)
            pe.matmul(ps_a[0:1, 0, 0:1], flag_f, ones[:, :], start=True, stop=True).then_inc(flag_pe, 1)
            pe.wait_ge(rows_in, 16 * 11)
            for m in range(MF):
                for k in range(KC):
                    ins = pe.matmul(ps_f[:, 0, m:m + 1], w1[:, k, m * P:(m + 1) * P], b1_col[:, k:k + 1],
                                    start=(k == 0), stop=(k == KC - 1))
            ins.then_inc(hidden_pe, 1)

            def pair(j):
                for t in range(TG):
                    if j.exists(NPAIR):
                        front_project(pe, j, t, 0 if t < 2 else D, D + SC if t < 2 else WV)
                    if t == 1 and (j + 1).exists(NPAIR):
                        front_turn(pe, j + 1)
            pe.wait_ge(weights_split, SPLITS)
            steps(pe, pair, -1, NPAIR, *PAIR_LOOP)

            pe.wait_ge(cand_ready, 1)
            pe.wait_ge(xt_lo, KC * NPAIR)
            for k in range(2):
                for q in range(4):
                    ins = pe.transpose(ps_t[0:NCH, k, q * P:(q + 1) * P], cand[:, 4 * k + q, :], ident[:, :])
                ins.then_inc(cand_turned, 1)
            for way in range(2):
                pe.wait_ge(scan_step, 5 + way * 9)
                pe.transpose(ps_f[0:1, 0, 0:P], ends[:, 0:1], ident[:, :])
                pe.transpose(ps_f[0:1, 0, P:2 * P], ends[:, 1:2], ident[:, :]).then_inc(scan_pe, 1)
                pe.wait_ge(scan_step, 8 + way * 9)
                pe.transpose(ps_f[:, 1, 0:1], ends_row[0:1, 2, :], ident[0:1, 0:1]).then_inc(scan_pe, 1)
            pe.wait_ge(max_in, 16)
            for k in range(2):
                for q in range(4):
                    ins = pe.transpose(ps_t[:, k, q * P:q * P + NCH], turn[0:NCH, 4 * k + q, :], ident[0:NCH, 0:NCH])
                ins.then_inc(max_turned, 1)

            def chunk(j, c):
                pe.wait_ge(eq_ready, 2 * c.n + 2)
                pe.wait_ge(vals_ready, c.n + 1)
                wait_count(pe, agg_out, c.n - 1)
                to = ps_a[:, c.par, :]
                pe.matmul(to[:, 0:D], eq[:, c.off % 4, :], msg_in[:, c.off % (2 * SB), :], start=True, stop=False, skip_group_check=True)
                pe.matmul(to[:, D:SUM], eq[:, c.off % 4, :], prob[:, bass.ds(c.n, 1), :].rearrange("p o h -> p (o h)"), start=False, stop=False, skip_group_check=True)
                wait_count(pe, agg_out, c.n)
                pe.matmul(to[:, 0:SUM], eq_carry[:, c.off % 4, :], agg[:, (2 * j.par + c.par - 1) % 4, 0:SUM], start=False, stop=True, skip_group_check=True).then_inc(agg_done, 1)
            pe.wait_ge(exp_ready, 1)
            pe.wait_ge(empty_set, 4)
            steps(pe, lambda j: [chunk(j, c) for c in chunks(j)], 0, NPAIR, *SUM_LOOP)

            def ffn1_piece(i, m):
                n = MF * i.n + m
                if m == 0:
                    pe.wait_ge(zt_lo, KC * i.n + KC)
                wait_count(pe, act_f_ready, n - 1)
                j = 0
                for k in range(KC):
                    for a, b in ((0, 0), (0, 1), (1, 0)):
                        ins = pe.matmul(ps_f[:, m % 2, :], ffn1[a][:, k, m * P:(m + 1) * P], zt[b][:, i.par, k, :],
                                        start=(j == 0), stop=(j == 3 * KC - 1))
                        j += 1
                ins.then_inc(f_done, 1)

            def ffn2_piece(i, m):
                n = MF * i.n + m
                pe.wait_ge(act_hi_ready, n + 1)
                pe.wait_ge(act_lo_ready, n + 1)
                for t in range(TG):
                    if m == 0 and t % 2 == 0:
                        wait_count(pe, u_ready, 2 * i.n - 1 + t // 2)
                    cols = slice(t * P, (t + 1) * P)
                    to = ps_a[:, t // 2, (t % 2) * D:(t % 2 + 1) * D]
                    pe.matmul(to, act_hi[:, m % AB, cols], ffn2[0][:, m, :], start=(m == 0 and t % 2 == 0), stop=False, skip_group_check=True)
                    pe.matmul(to, act_hi[:, m % AB, cols], ffn2[1][:, m, :], start=False, stop=False, skip_group_check=True)
                    ins = pe.matmul(to, act_lo[:, m % AB, cols], ffn2[0][:, m, :], start=False, stop=(m == MF - 1), skip_group_check=True)
                ins.then_inc(act_used, 1)

            def turn_z(n, front):
                pe.wait_ge(z_ready, n.n + 1)
                pe.wait_ge(xt_lo, KC * (n + NPAIR + front).n + KC)
                for k in range(KC):
                    for t in range(TG):
                        ins = pe.transpose(ps_t[:, k, t * P:(t + 1) * P], z[:, t, k * P:(k + 1) * P], ident[:, :])
                    ins.then_inc(zt_turned, 1)

            def nodes(i):
                o, n, a = i - 1, i + 1, i + 2
                back, on, norm, front = o.exists(NG), i.exists(NG), n.exists(NG), a.exists(NG)
                for m in range(MF):
                    if on:
                        ffn1_piece(i, m)
                    if m == 6 and norm:
                        turn_z(n, front)
                    if m < LAG and back:
                        ffn2_piece(o, MF - LAG + m)
                    if m >= LAG and on:
                        ffn2_piece(i, m - LAG)
                    if m == 3 and front:
                        wait_count(pe, zt_lo, KC * (a.n - 1))
                        front_turn(pe, a + NPAIR)
                    if m in (5, 6) and front:
                        front_project(pe, a + NPAIR, 2 * m - 10, 0, WV)
                        front_project(pe, a + NPAIR, 2 * m - 9, 0, WV)
            steps(pe, nodes, -2, NG + 1, *NODE_LOOP)


def kernel(x, src, dst, edge_type_2, edge_weight, L0_gnn_W_src, L0_gnn_W_dst, L0_gnn_att_src, L0_gnn_att_dst,
           L0_gnn_bias, L0_gnn_ln1_g, L0_gnn_ln1_b, L0_gnn_ln2_g, L0_gnn_ln2_b, L0_gnn_ffn_W1, L0_gnn_ffn_b1,
           L0_gnn_ffn_W2, L0_gnn_ffn_b2):
    import concourse.bacc as bacc
    from concourse.bass_utils import run_bass_kernel_spmd

    a = {k: np.asarray(v) for k, v in dict(locals()).items()
         if k not in ("bacc", "run_bass_kernel_spmd")}
    n, d = a["x"].shape
    e = a["src"].shape[0]
    rows = -(-(n + 1) // GR) * GR
    ch = -(-e // (2 * P)) * 2
    ep = ch * P

    def padded(v, fill):
        return np.concatenate([v, np.full(ep - e, fill, v.dtype)])

    def columns(v, parts=P):
        return np.ascontiguousarray(v.reshape(-1, parts).T)

    dst_p = padded(a["dst"], n)
    dst_line = np.concatenate([np.full(1, -1, dst_p.dtype), dst_p, np.full(1, n + 1, dst_p.dtype)])
    put = {
        "x": np.concatenate([a["x"], np.zeros((rows - n, d), a["x"].dtype)]),
        "ends_cols": np.stack([columns(padded(a["src"], n)), columns(dst_p)], axis=-1).reshape(P, -1),
        "next_cols": columns(dst_line[2:]),
        "type_cols": columns(padded(a["edge_type_2"], 0)),
        "weight_cols": columns(padded(a["edge_weight"], 0)),
        "dst_line": dst_line.reshape(1, -1),
        "w_src_t": np.ascontiguousarray(a["L0_gnn_W_src"].T),
        "w_dst_t": np.ascontiguousarray(a["L0_gnn_W_dst"].T),
        "att_src": a["L0_gnn_att_src"].reshape(2, -1),
        "att_dst": a["L0_gnn_att_dst"].reshape(2, -1),
        "bias": a["L0_gnn_bias"].reshape(1, -1),
        "g1": a["L0_gnn_ln1_g"].reshape(1, -1),
        "b1": a["L0_gnn_ln1_b"].reshape(1, -1),
        "g2": a["L0_gnn_ln2_g"].reshape(1, -1),
        "b2": a["L0_gnn_ln2_b"].reshape(1, -1),
        "g1_cols": columns(a["L0_gnn_ln1_g"]),
        "b1_cols": columns(a["L0_gnn_ln1_b"]),
        "w1_t": np.ascontiguousarray(a["L0_gnn_ffn_W1"].T),
        "ffn_b1_cols": columns(a["L0_gnn_ffn_b1"]),
        "w2_t": np.ascontiguousarray(a["L0_gnn_ffn_W2"].T),
        "ffn_b2": a["L0_gnn_ffn_b2"].reshape(1, -1),
    }
    nc = bacc.Bacc("TRN2", target_bir_lowering=False, num_devices=1)
    args = {k: nc.dram_tensor(f"in_{k}", v.shape, mybir.dt.from_np(v.dtype), kind="ExternalInput").ap()
            for k, v in put.items()}
    out = nc.dram_tensor("out_0", (rows, d), F32, kind="ExternalOutput").ap()
    build(nc, out=out, **args)
    r = run_bass_kernel_spmd(nc, [{f"in_{k}": v for k, v in put.items()}], core_ids=[0])
    return r.results[0]["out_0"][:n]
```
